# Optimizing a Trainium2 kernel written in Bass

```python
import numpy as np
import jax
import jax.numpy as jnp

def _softmax(x, axis=-1):
    return jax.nn.softmax(x, axis=axis)

def _gelu(x):
    return jax.nn.gelu(x, approximate=True)

def _silu(x):
    return jax.nn.silu(x)

def _sigmoid(x):
    return jax.nn.sigmoid(x)

def _layernorm(x, axis=-1, eps=1e-05):
    m = jnp.mean(x, axis=axis, keepdims=True)
    v = jnp.var(x, axis=axis, keepdims=True)
    return (x - m) / jnp.sqrt(v + eps)

def _scatter_add(tgt, idx, src, axis=0):
    return tgt.at[idx].add(src)

def _segment_sum(src, seg, n):
    return jax.ops.segment_sum(src, seg, n)
kernel_name = 'mk_perceiver_d2_seqx_r2_d03762'

def setup_inputs(seed: int=0):
    np.random.seed(seed)
    _w = jnp.asarray

    def _rec_inputs():
        import jax
        import jax.numpy as jnp
        _rk = jax.random.key(seed)
        x = -0.0002928 + 1 * jax.random.normal(jax.random.fold_in(_rk, 1), (32, 32, 512), jnp.float32)
        _lenS = 32 - jax.random.randint(jax.random.fold_in(_rk, 7), (32,), 0, max(1, 32 // 4) + 1, jnp.int32)
        _lenS2 = 257 - jax.random.randint(jax.random.fold_in(_rk, 8), (32,), 0, max(1, 257 // 4) + 1, jnp.int32)
        _ctx_1024P = jax.random.normal(jax.random.fold_in(_rk, 11), (32, 16, 512), jnp.float32)
        _ctx_1024c = jax.random.dirichlet(jax.random.fold_in(_rk, 511), 0.3 * jnp.ones((16,), jnp.float32), (32, 257))
        _ctx_1024t = jnp.einsum('bsk,bkd->bsd', _ctx_1024c, _ctx_1024P)
        _ctx_1024t = _ctx_1024t * jax.lax.rsqrt(jnp.mean(jnp.square(_ctx_1024t)) + 1e-12) * 0.953939
        ctx_1024 = 4.13588e-05 + 0.999923 * (_ctx_1024t + 0.3 * jax.random.normal(jax.random.fold_in(_rk, 611), (32, 257, 512), jnp.float32))
        fside_SxS2_0 = 0.00086875 + 0.999764 * jax.random.normal(jax.random.fold_in(_rk, 12), (32, 257), jnp.float32)
        _validS = jnp.arange(32)[None, :] < _lenS[:, None]
        _validS2 = jnp.arange(257)[None, :] < _lenS2[:, None]
        _causal = jnp.tril(jnp.ones((32, 32), dtype=bool))
        mask_BxSxS2_ik0 = jnp.where(jnp.broadcast_to(_validS2[:, None, :], (32, 32, 257)), 0, 1).astype(jnp.int32)
        return (x, ctx_1024, fside_SxS2_0, mask_BxSxS2_ik0)
    x, ctx_1024, fside_SxS2_0, mask_BxSxS2_ik0 = _rec_inputs()

    def _L0_xattn_setup():
        import jax, jax.numpy as jnp
        import numpy as np
        NUM_HEADS = 16
        EPS = 1e-12
        MAX_SCALE_MUL = float(np.log(100.0))

        def _l2norm(t):
            n = jnp.sqrt(jnp.sum(t * t, axis=-1, keepdims=True))
            return t / jnp.maximum(n, EPS)
        key = jax.random.key(seed)
        ks = jax.random.split(key, 10)
        B, Lq, Ly, C = (4, 512, 1024, 512)
        s = 1.0 / np.sqrt(C)
        return {'x': jax.random.normal(ks[0], (B, Lq, C), jnp.float32), 'y': jax.random.normal(ks[1], (B, Ly, C), jnp.float32), 'attn_bias': jax.random.normal(ks[2], (Lq, Ly), jnp.float32), 'Wq': jax.random.normal(ks[3], (C, C), jnp.float32) * s, 'bq': jnp.zeros((C,), jnp.float32), 'Wk': jax.random.normal(ks[4], (C, C), jnp.float32) * s, 'Wv': jax.random.normal(ks[5], (C, C), jnp.float32) * s, 'Wo': jax.random.normal(ks[6], (C, C), jnp.float32) * s, 'bo': jnp.zeros((C,), jnp.float32), 'scale_mul_log': jnp.full((1, NUM_HEADS, 1, 1), np.log(4.0), jnp.float32)}
    _L0_xattn_all = _L0_xattn_setup()
    _L0_xattn_in = {k: v for k, v in _L0_xattn_all.items() if k in ('Wq', 'bq', 'Wk', 'Wv', 'Wo', 'bo', 'scale_mul_log')}
    del _L0_xattn_all

    def _L0_attn_setup():
        import jax, jax.numpy as jnp
        import numpy as np
        B, S, D, K = (4, 2048, 512, 64)
        key = jax.random.key(seed)
        kx, kq, kk, kv, ko = jax.random.split(key, 5)
        scale = 1.0 / np.sqrt(D)
        return {'x': jax.random.normal(kx, (B, S, D), dtype=jnp.float32), 'Wq': jax.random.uniform(kq, (K, D), dtype=jnp.float32, minval=-scale, maxval=scale), 'Wk': jax.random.uniform(kk, (K, D), dtype=jnp.float32, minval=-scale, maxval=scale), 'Wv': jax.random.uniform(kv, (K, D), dtype=jnp.float32, minval=-scale, maxval=scale), 'Wo': jax.random.uniform(ko, (D, K), dtype=jnp.float32, minval=-1.0 / np.sqrt(K), maxval=1.0 / np.sqrt(K))}
    _L0_attn_all = _L0_attn_setup()
    _L0_attn_in = {k: v for k, v in _L0_attn_all.items() if k in ('Wq', 'Wk', 'Wv', 'Wo')}
    del _L0_attn_all

    def _L0_ffn_setup():
        import jax, jax.numpy as jnp
        import numpy as np
        D = 512
        H = 512
        E = 8
        K = 2
        I = 2 * 512
        ROUTE_SCALE = 1.0
        key = jax.random.key(seed)
        ks = jax.random.split(key, 12)
        s = lambda *sh: 1.0 / np.sqrt(sh[-1])
        return {'x': jax.random.normal(ks[0], (1, 1024, D), jnp.float32), 'gate_w': jax.random.normal(ks[1], (E, D), jnp.float32) * s(E, D), 'w1': jax.random.normal(ks[2], (E, H, D), jnp.float32) * s(H, D), 'b1': jax.random.normal(ks[3], (E, H), jnp.float32) * 0.01, 'w2': jax.random.normal(ks[4], (E, D, H), jnp.float32) * s(D, H), 'b2': jax.random.normal(ks[5], (E, D), jnp.float32) * 0.01, 'w3': jax.random.normal(ks[6], (E, H, D), jnp.float32) * s(H, D), 'b3': jax.random.normal(ks[7], (E, H), jnp.float32) * 0.01, 'sw1': jax.random.normal(ks[8], (I, D), jnp.float32) * s(I, D), 'sw2': jax.random.normal(ks[9], (I, D), jnp.float32) * s(I, D), 'sw3': jax.random.normal(ks[10], (D, I), jnp.float32) * s(D, I)}
    _L0_ffn_all = _L0_ffn_setup()
    _L0_ffn_in = {k: v for k, v in _L0_ffn_all.items() if k in ('gate_w', 'w1', 'b1', 'w2', 'b2', 'w3', 'b3', 'sw1', 'sw2', 'sw3')}
    del _L0_ffn_all

    def _L1_xattn_setup():
        import jax, jax.numpy as jnp
        import numpy as np
        import math
        B, S, E = (4, 1024, 512)
        key = jax.random.key(seed)
        ks = jax.random.split(key, 12)
        scale = 1.0 / math.sqrt(E)
        inp = {'query': jax.random.normal(ks[0], (B, S, E), jnp.float32), 'key_': jax.random.normal(ks[1], (B, S, E), jnp.float32), 'value': jax.random.normal(ks[2], (B, S, E), jnp.float32), 'mask': jnp.broadcast_to(jnp.tril(jnp.ones((S, S), jnp.int32)), (B, S, S)), 'Wq': jax.random.uniform(ks[3], (E, E), jnp.float32, -scale, scale), 'bq': jax.random.uniform(ks[4], (E,), jnp.float32, -scale, scale), 'Wk': jax.random.uniform(ks[5], (E, E), jnp.float32, -scale, scale), 'bk': jax.random.uniform(ks[6], (E,), jnp.float32, -scale, scale), 'Wv': jax.random.uniform(ks[7], (E, E), jnp.float32, -scale, scale), 'bv': jax.random.uniform(ks[8], (E,), jnp.float32, -scale, scale), 'Wo': jax.random.uniform(ks[9], (E, E), jnp.float32, -scale, scale), 'bo': jax.random.uniform(ks[10], (E,), jnp.float32, -scale, scale)}
        return inp
    _L1_xattn_all = _L1_xattn_setup()
    _L1_xattn_in = {k: v for k, v in _L1_xattn_all.items() if k in ('Wq', 'bq', 'Wk', 'bk', 'Wv', 'bv', 'Wo', 'bo')}
    del _L1_xattn_all

    def _L1_attn_setup():
        import jax, jax.numpy as jnp
        import numpy as np
        import math
        E = 512
        H = 64
        B = 4
        S = 1024
        key = jax.random.key(seed)
        ks = jax.random.split(key, 9)
        x = jax.random.normal(ks[0], (B, S, E), dtype=jnp.float32)

        def he(k, fan_in, shape):
            return jax.random.normal(k, shape, dtype=jnp.float32) * jnp.sqrt(2.0 / fan_in)
        wq = he(ks[1], E, (E, H))
        bq = jnp.zeros((H,), jnp.float32)
        wk = he(ks[2], E, (E, H))
        bk = jnp.zeros((H,), jnp.float32)
        wv = he(ks[3], E, (E, H))
        bv = jnp.zeros((H,), jnp.float32)
        wo = he(ks[4], H, (H, E))
        bo = jnp.zeros((E,), jnp.float32)
        return {'x': x, 'wq': wq, 'bq': bq, 'wk': wk, 'bk': bk, 'wv': wv, 'bv': bv, 'wo': wo, 'bo': bo}
    _L1_attn_all = _L1_attn_setup()
    _L1_attn_in = {k: v for k, v in _L1_attn_all.items() if k in ('wq', 'bq', 'wk', 'bk', 'wv', 'bv', 'wo', 'bo')}
    del _L1_attn_all

    def _L1_ffn_setup():
        import jax, jax.numpy as jnp
        import numpy as np
        BLOCK = 16
        _GRID = jnp.array([0.0, 0.5, 1.0, 1.5, 2.0, 3.0, 4.0, 6.0], dtype=jnp.float32)
        _MID = jnp.array([0.25, 0.75, 1.25, 1.75, 2.5, 3.5, 5.0], dtype=jnp.float32)

        def fp4_quant_dequant(x):
            shape = x.shape
            xb = x.reshape(shape[:-1] + (shape[-1] // BLOCK, BLOCK))
            scale = jnp.max(jnp.abs(xb), axis=-1, keepdims=True) / 6.0
            scale = jnp.maximum(scale, jnp.float32(1e-12))
            xn = xb / scale
            idx = jnp.searchsorted(_MID, jnp.abs(xn))
            q = _GRID[idx] * jnp.sign(xn) * scale
            return q.reshape(shape)

        def fp4_linear(x, w):
            xq = fp4_quant_dequant(x)
            wq = fp4_quant_dequant(w)
            return jnp.einsum('bsk,nk->bsn', xq, wq)
        key = jax.random.key(seed)
        k1, k2, k3, k4 = jax.random.split(key, 4)
        H, I = (512, 1408)
        x = jax.random.normal(k1, (4, 2048, H), dtype=jnp.float32)
        w_gate = jax.random.normal(k2, (I, H), dtype=jnp.float32) * 0.02
        w_up = jax.random.normal(k3, (I, H), dtype=jnp.float32) * 0.02
        w_down = jax.random.normal(k4, (H, I), dtype=jnp.float32) * 0.02
        return {'x': x, 'w_gate': w_gate, 'w_up': w_up, 'w_down': w_down}
    _L1_ffn_all = _L1_ffn_setup()
    _L1_ffn_in = {k: v for k, v in _L1_ffn_all.items() if k in ('w_gate', 'w_up', 'w_down')}
    del _L1_ffn_all
    return {'x': x, 'ctx_1024': ctx_1024, 'fside_SxS2_0': fside_SxS2_0, 'mask_BxSxS2_ik0': mask_BxSxS2_ik0, 'L0_xattn_Wq': _L0_xattn_in['Wq'], 'L0_xattn_bq': _L0_xattn_in['bq'], 'L0_xattn_Wk': _L0_xattn_in['Wk'], 'L0_xattn_Wv': _L0_xattn_in['Wv'], 'L0_xattn_Wo': _L0_xattn_in['Wo'], 'L0_xattn_bo': _L0_xattn_in['bo'], 'L0_xattn_scale_mul_log': _L0_xattn_in['scale_mul_log'], 'L0_attn_Wq': _L0_attn_in['Wq'], 'L0_attn_Wk': _L0_attn_in['Wk'], 'L0_attn_Wv': _L0_attn_in['Wv'], 'L0_attn_Wo': _L0_attn_in['Wo'], 'L0_ffn_gate_w': _L0_ffn_in['gate_w'], 'L0_ffn_w1': _L0_ffn_in['w1'], 'L0_ffn_b1': _L0_ffn_in['b1'], 'L0_ffn_w2': _L0_ffn_in['w2'], 'L0_ffn_b2': _L0_ffn_in['b2'], 'L0_ffn_w3': _L0_ffn_in['w3'], 'L0_ffn_b3': _L0_ffn_in['b3'], 'L0_ffn_sw1': _L0_ffn_in['sw1'], 'L0_ffn_sw2': _L0_ffn_in['sw2'], 'L0_ffn_sw3': _L0_ffn_in['sw3'], 'L1_xattn_Wq': _L1_xattn_in['Wq'], 'L1_xattn_bq': _L1_xattn_in['bq'], 'L1_xattn_Wk': _L1_xattn_in['Wk'], 'L1_xattn_bk': _L1_xattn_in['bk'], 'L1_xattn_Wv': _L1_xattn_in['Wv'], 'L1_xattn_bv': _L1_xattn_in['bv'], 'L1_xattn_Wo': _L1_xattn_in['Wo'], 'L1_xattn_bo': _L1_xattn_in['bo'], 'L1_attn_wq': _L1_attn_in['wq'], 'L1_attn_bq': _L1_attn_in['bq'], 'L1_attn_wk': _L1_attn_in['wk'], 'L1_attn_bk': _L1_attn_in['bk'], 'L1_attn_wv': _L1_attn_in['wv'], 'L1_attn_bv': _L1_attn_in['bv'], 'L1_attn_wo': _L1_attn_in['wo'], 'L1_attn_bo': _L1_attn_in['bo'], 'L1_ffn_w_gate': _L1_ffn_in['w_gate'], 'L1_ffn_w_up': _L1_ffn_in['w_up'], 'L1_ffn_w_down': _L1_ffn_in['w_down']}

def reference(x, ctx_1024, fside_SxS2_0, mask_BxSxS2_ik0, L0_xattn_Wq, L0_xattn_bq, L0_xattn_Wk, L0_xattn_Wv, L0_xattn_Wo, L0_xattn_bo, L0_xattn_scale_mul_log, L0_attn_Wq, L0_attn_Wk, L0_attn_Wv, L0_attn_Wo, L0_ffn_gate_w, L0_ffn_w1, L0_ffn_b1, L0_ffn_w2, L0_ffn_b2, L0_ffn_w3, L0_ffn_b3, L0_ffn_sw1, L0_ffn_sw2, L0_ffn_sw3, L1_xattn_Wq, L1_xattn_bq, L1_xattn_Wk, L1_xattn_bk, L1_xattn_Wv, L1_xattn_bv, L1_xattn_Wo, L1_xattn_bo, L1_attn_wq, L1_attn_bq, L1_attn_wk, L1_attn_bk, L1_attn_wv, L1_attn_bv, L1_attn_wo, L1_attn_bo, L1_ffn_w_gate, L1_ffn_w_up, L1_ffn_w_down):
    import jax
    import jax.numpy as jnp

    def _L0_xattn_ref(x, y, attn_bias, Wq, bq, Wk, Wv, Wo, bo, scale_mul_log):
        import jax, jax.numpy as jnp
        import numpy as np
        NUM_HEADS = 16
        EPS = 1e-12
        MAX_SCALE_MUL = float(np.log(100.0))

        def _l2norm(t):
            n = jnp.sqrt(jnp.sum(t * t, axis=-1, keepdims=True))
            return t / jnp.maximum(n, EPS)
        B, Lq, C = x.shape
        Ly = y.shape[1]
        H = NUM_HEADS
        D = C // H
        q = (x @ Wq + bq).reshape(B, Lq, H, D).transpose(0, 2, 1, 3)
        k = (y @ Wk).reshape(B, Ly, H, D).transpose(0, 2, 1, 3)
        v = (y @ Wv).reshape(B, Ly, H, D).transpose(0, 2, 1, 3)
        scale_mul = jnp.exp(jnp.minimum(scale_mul_log, MAX_SCALE_MUL))
        q = _l2norm(q) * scale_mul
        k = _l2norm(k)
        attn = jnp.einsum('bhqd,bhkd->bhqk', q, k) + attn_bias
        attn = jax.nn.softmax(attn, axis=-1)
        oup = jnp.einsum('bhqk,bhkd->bhqd', attn, v)
        oup = oup.transpose(0, 2, 1, 3).reshape(B, Lq, C)
        return oup @ Wo + bo

    def _L0_attn_ref(x, Wq, Wk, Wv, Wo):
        import jax, jax.numpy as jnp
        import numpy as np
        B, S, D, K = (4, 2048, 512, 64)
        Q = jax.nn.elu(x @ Wq.T) + 1.0
        Kf = jax.nn.elu(x @ Wk.T) + 1.0
        V = x @ Wv.T
        KV_sum = jnp.cumsum(Kf[..., :, None] * V[..., None, :], axis=1)
        K_sum = jnp.cumsum(Kf, axis=1)
        num = jnp.einsum('bsk,bskm->bsm', Q, KV_sum)
        den = jnp.einsum('bsk,bsk->bs', Q, K_sum)[..., None]
        out = num / (den + 1e-06)
        return out @ Wo.T

    def _L0_ffn_ref(x, gate_w, w1, b1, w2, b2, w3, b3, sw1, sw2, sw3):
        import jax, jax.numpy as jnp
        import numpy as np
        D = 512
        H = 512
        E = 8
        K = 2
        I = 2 * 512
        ROUTE_SCALE = 1.0
        B, S, _ = x.shape
        xt = x.reshape(-1, D)
        logits = xt @ gate_w.T
        scores = jax.nn.softmax(logits.astype(jnp.float32), axis=-1)
        top_vals, idx = jax.lax.top_k(scores, K)
        weights = jnp.take_along_axis(scores, idx, axis=1).astype(x.dtype) * ROUTE_SCALE
        xs = xt[:, None, :] * weights[:, :, None]
        y = jnp.zeros_like(xt)
        for e in range(E):
            mask = (idx == e).astype(x.dtype)
            h = jax.nn.silu(jnp.einsum('tkd,hd->tkh', xs, w1[e]) + b1[e])
            x2 = jnp.einsum('tkh,dh->tkd', h, w2[e]) + b2[e]
            x3 = jnp.einsum('tkd,hd->tkh', xs, w3[e]) + b3[e]
            y = y + jnp.sum(x2 * x3 * mask[:, :, None], axis=1)
        z = jax.nn.silu(xt @ sw1.T) * (xt @ sw2.T) @ sw3.T
        return (y + z).reshape(B, S, D)

    def _L1_xattn_ref(query, key_, value, mask, Wq, bq, Wk, bk, Wv, bv, Wo, bo):
        import jax, jax.numpy as jnp
        import numpy as np
        import math
        B, S, E = (4, 1024, 512)
        Q = jnp.einsum('bse,fe->bsf', query, Wq) + bq
        K = jnp.einsum('bse,fe->bsf', key_, Wk) + bk
        V = jnp.einsum('bse,fe->bsf', value, Wv) + bv
        scores = jnp.einsum('bqe,bke->bqk', Q, K) / jnp.sqrt(jnp.asarray(E, Q.dtype))
        scores = jnp.where(mask == 0, -jnp.inf, scores)
        attn = jax.nn.softmax(scores, axis=-1)
        attn_out = jnp.einsum('bqk,bke->bqe', attn, V)
        return jnp.einsum('bse,fe->bsf', attn_out, Wo) + bo

    def _L1_attn_ref(x, wq, bq, wk, bk, wv, bv, wo, bo):
        import jax, jax.numpy as jnp
        import numpy as np
        import math
        E = 512
        H = 64
        B = 4
        S = 1024
        q = x @ wq + bq
        k = x @ wk + bk
        v = x @ wv + bv
        scale = 1.0 / math.sqrt(H)
        w = jnp.einsum('bqh,bkh->bqk', q, k) * scale
        seq = x.shape[1]
        mask = jnp.triu(jnp.ones((1, seq, seq), dtype=w.dtype), 1) * -100000000000.0
        w = w + mask
        w = jax.nn.softmax(w, axis=-1)
        z = jnp.einsum('bqk,bkh->bqh', w, v)
        z = z @ wo + bo
        return z

    def _L1_ffn_ref(x, w_gate, w_up, w_down):
        import jax, jax.numpy as jnp
        import numpy as np
        BLOCK = 16
        _GRID = jnp.array([0.0, 0.5, 1.0, 1.5, 2.0, 3.0, 4.0, 6.0], dtype=jnp.float32)
        _MID = jnp.array([0.25, 0.75, 1.25, 1.75, 2.5, 3.5, 5.0], dtype=jnp.float32)

        def fp4_quant_dequant(x):
            shape = x.shape
            xb = x.reshape(shape[:-1] + (shape[-1] // BLOCK, BLOCK))
            scale = jnp.max(jnp.abs(xb), axis=-1, keepdims=True) / 6.0
            scale = jnp.maximum(scale, jnp.float32(1e-12))
            xn = xb / scale
            idx = jnp.searchsorted(_MID, jnp.abs(xn))
            q = _GRID[idx] * jnp.sign(xn) * scale
            return q.reshape(shape)

        def fp4_linear(x, w):
            xq = fp4_quant_dequant(x)
            wq = fp4_quant_dequant(w)
            return jnp.einsum('bsk,nk->bsn', xq, wq)
        gate = fp4_linear(x, w_gate)
        y = fp4_linear(x, w_up)
        h = jax.nn.silu(gate) * y
        return fp4_linear(h, w_down)
    x = x + _L0_xattn_ref(_layernorm(x, axis=-1), ctx_1024, fside_SxS2_0, L0_xattn_Wq, L0_xattn_bq, L0_xattn_Wk, L0_xattn_Wv, L0_xattn_Wo, L0_xattn_bo, L0_xattn_scale_mul_log)
    x = x + _L0_attn_ref(_layernorm(x, axis=-1), L0_attn_Wq, L0_attn_Wk, L0_attn_Wv, L0_attn_Wo)
    x = x + _L0_ffn_ref(_layernorm(x, axis=-1), L0_ffn_gate_w, L0_ffn_w1, L0_ffn_b1, L0_ffn_w2, L0_ffn_b2, L0_ffn_w3, L0_ffn_b3, L0_ffn_sw1, L0_ffn_sw2, L0_ffn_sw3)
    x = x + _L1_xattn_ref(_layernorm(x, axis=-1), ctx_1024, ctx_1024, mask_BxSxS2_ik0, L1_xattn_Wq, L1_xattn_bq, L1_xattn_Wk, L1_xattn_bk, L1_xattn_Wv, L1_xattn_bv, L1_xattn_Wo, L1_xattn_bo)
    x = x + _L1_attn_ref(_layernorm(x, axis=-1), L1_attn_wq, L1_attn_bq, L1_attn_wk, L1_attn_bk, L1_attn_wv, L1_attn_bv, L1_attn_wo, L1_attn_bo)
    x = x + _L1_ffn_ref(_layernorm(x, axis=-1), L1_ffn_w_gate, L1_ffn_w_up, L1_ffn_w_down)
    return x

_drawn_inputs = setup_inputs


def setup_inputs(seed=0):
    import zlib

    import numpy as np

    out = dict(_drawn_inputs(seed))
    spreads = {'L0_xattn_bq': (0.0, 0.393),
     'L0_xattn_bo': (0.0, 0.1),
     'L0_xattn_scale_mul_log': (1.3862943649291992, 0.2),
     'L1_attn_bq': (0.0, 0.1),
     'L1_attn_bk': (0.0, 2.0),
     'L1_attn_bv': (0.0, 0.1),
     'L1_attn_bo': (0.0, 0.1)}
    factors = {'L0_attn_Wq': 21.871,
     'L0_attn_Wk': 7.112,
     'L0_ffn_b1': 23.055,
     'L0_ffn_b2': 8.0,
     'L0_ffn_b3': 21.592,
     'L1_xattn_bq': 38.019,
     'L1_xattn_bk': 64.0,
     'L1_xattn_bv': 3.677}
    for name, (base, spread) in spreads.items():
        noise = np.random.default_rng([zlib.crc32(name.encode()), seed]).standard_normal(out[name].shape)
        drawn = base * np.exp(spread * noise) if base else spread * noise
        out[name] = jnp.asarray(drawn.astype(out[name].dtype))
    for name, factor in factors.items():
        out[name] = (out[name] * factor).astype(out[name].dtype)
    return out
```

```python
from contextlib import ExitStack

import numpy as np
import concourse.bass as bass
from concourse import mybir

F32 = mybir.dt.float32
F32R = mybir.dt.float32r
BF16 = mybir.dt.bfloat16
I32 = mybir.dt.int32
ALU = mybir.AluOpType
ACT = mybir.ActivationFunctionType
AX = mybir.AxisListType

P = 128
B, LQ, LK, D = 32, 32, 257, 512
T = B * LQ
TILES = T // P
BT = P // LQ
C = D // P
H, DH = 16, 32
G = H // BT
HK = 64
E = 8
I1 = 1024
FF = 1408
FC = FF // P
BLK = 16
KH = 2
NORM2_MIN = 1e-24


def turn_before(m, u):
    return m if u == 0 else m - 1


class Steps:

    def __init__(self, eng, sem):
        self.eng, self.sem, self.n = eng, sem, 0

    def restart(self):
        self.eng.sem_clear(self.sem)
        self.n = 0

    def __call__(self, ins):
        self.n += 1
        ins.then_inc(self.sem, 1)
        self.eng.wait_ge(self.sem, self.n)


def product3(pe, out, lhs, rhs, start, stop):
    (lh, ll), (rh, rl) = lhs, rhs
    pe.matmul(out, ll, rh, start=start, stop=False)
    pe.matmul(out, lh, rl, start=False, stop=False)
    return pe.matmul(out, lh, rh, start=False, stop=stop)


def cast(x):
    return x.bitcast(F32)



MISC = ["wo", "xT1", "q", "xT2", "qT", "qkv", "am", "num", "z", "xT3", "log", "wT"]
MISC_LAST = [u for u in MISC if u not in ("xT1", "q", "qT")]
MISC_FIRST = ["xT1", "q", "qT"]
UNITS = BT * G


def phase_a(nc, A, X, XN3T, w_dram):
    with ExitStack() as ctx:
        sb = lambda n, s, d=F32: ctx.enter_context(nc.sbuf_tensor("pa_" + n, s, d))
        sem = lambda n: ctx.enter_context(nc.semaphore(n))
        wk = [sb("wk_hi", [P, C, D], F32R), sb("wk_lo", [P, C, D], F32R)]
        wv = [sb("wv_hi", [P, C, D], F32R), sb("wv_lo", [P, C, D], F32R)]
        wq = sb("wq", [P, C, D])
        wo = sb("wo", [P, C, D])
        ident = sb("ident", [P, P])
        ctx_raw = [sb(f"ctx_raw{r}", [P, C, KH * P]) for r in range(2)]
        ctx_hi = [sb(f"ctx_hi{r}", [P, C, KH * P], F32R) for r in range(2)]
        ctx_lo = [sb(f"ctx_lo{r}", [P, C, KH * P], F32R) for r in range(2)]
        ctx_tail = sb("ctx_tail", [P, C, B])
        keysT = [sb(f"keysT{j}", [P, C, LK]) for j in range(BT)]
        vals = [[sb(f"vals{j}_{h}", [P, D]) for h in range(KH)] for j in range(BT)]
        vtail = sb("vtail", [B, D])
        ktailT = sb("ktailT", [P, C, B])
        kraw = [sb(f"kraw{r}", [P, D]) for r in range(2)]
        ksq = [sb(f"ksq{r}", [P, D]) for r in range(2)]
        khat = [sb(f"khat{r}", [P, D]) for r in range(2)]
        kn2 = [sb(f"kn2_{r}", [P, H]) for r in range(2)]
        kinv = [sb(f"kinv{r}", [P, H]) for r in range(2)]
        qblock = sb("qblock", [P, G, BT, P])
        w_raw = qblock[:].rearrange("p g j q -> p g (j q)")
        qs = sb("qs", [P, D])
        qsq = sb("qsq", [P, D])
        qn2 = sb("qn2", [P, H])
        qinv = sb("qinv", [P, H])
        qscale = sb("qscale", [P, H])
        oT = sb("oT", [P, G, P])
        bias = sb("bias", [P, LK])
        logit = [sb(f"logit{r}", [P, LK]) for r in range(2)]
        nmax = [sb(f"nmax{r}", [P, 1]) for r in range(2)]
        prob = [sb(f"prob{r}", [P, LK]) for r in range(2)]
        psum_ = [sb(f"psum_{r}", [P, 1]) for r in range(2)]
        rsum = [sb(f"rsum{r}", [P, 1]) for r in range(2)]
        pn = [sb(f"pn{r}", [P, KH * P + B]) for r in range(2)]
        pT = [sb(f"pT{r}", [P, KH * P]) for r in range(2)]
        pTtail = [sb(f"pTtail{r}", [B, P]) for r in range(2)]
        onehot = sb("onehot", [P, B, B])
        bq = sb("bq", [P, D])
        bo = sb("bo", [P, D])
        xn = sb("xn", [P, D])
        xnT1 = sb("xnT1", [P, C, P])
        xnT = sb("xnT", [P, C, P])
        stats = sb("stats", [P, 6])
        mv = sb("mv", [P, 2])
        veps = sb("veps", [P, 1])
        rstd = sb("rstd", [P, 1])
        mhalf = sb("mhalf", [P, H])
        eps = sb("eps", [P, 1])
        fence = sb("fence", [P, 3])
        aq = sb("aq", [P, C, HK])
        ak = sb("ak", [P, C, HK])
        av = sb("av", [P, C, HK])
        ao = sb("ao", [HK, D])
        gate = sb("gate", [P, C, E])
        elmin = sb("elmin", [HK, 2 * P])
        elexp = sb("elexp", [HK, 2 * P])
        qk = sb("qk", [HK, 2 * P])
        va = sb("va", [P, HK])
        cmaskT = sb("cmaskT", [P, P])
        am = sb("am", [P, P])
        ones = sb("ones", [P, 1])
        numT = sb("numT", [HK, P])
        den = sb("den", [P, 1])
        rden = sb("rden", [P, 1])
        lg = sb("lg", [P, E])
        lgmax = sb("lgmax", [P, 1])
        lgexp = sb("lgexp", [P, E])
        lgsum = sb("lgsum", [P, 1])
        lgr = sb("lgr", [P, 1])
        score = sb("score", [P, E])
        above = sb("above", [P, E, E])
        tie = sb("tie", [P, E, E])
        lower = sb("lower", [P, E, E])
        rank = sb("rank", [P, E])
        sel = sb("sel", [P, E])
        wsel = sb("wsel", [P, E])
        wT = sb("wT", [E, T])
        bank = [ctx.enter_context(nc.psum_tensor(f"pa{b}", [P, 512], F32)) for b in range(8)]
        k_ps, v_ps, kt_ps, s_ps, pt_ps, pv_ps, misc = bank[0], bank[1], bank[2], bank[3:5], bank[5], bank[6], bank[7]

        w_in = sem("a_w_in")
        wkv_in = sem("a_wkv_in")
        w_hi = sem("a_w_hi")
        w_lo = sem("a_w_lo")
        x_in = sem("a_x_in")
        init = sem("a_init")
        scale_ready = sem("a_scale_ready")
        ctx_in = [sem(f"a_ctx_in{r}") for r in range(2)]
        ctx_hi_ready = sem("a_ctx_hi")
        ctx_lo_ready = sem("a_ctx_lo")
        k_full, k_sq, k_free = sem("a_k_full"), sem("a_k_sq"), sem("a_k_free")
        v_full, v_free = sem("a_v_full"), sem("a_v_free")
        kn2_ready, kinv_ready, khat_ready = sem("a_kn2"), sem("a_kinv"), sem("a_khat")
        kt_full, kt_free = sem("a_kt_full"), sem("a_kt_free")
        ktail_ready = sem("a_ktail")
        tail_in, tail_full, tail_done = sem("a_tail_in"), sem("a_tail_full"), sem("a_tail_done")
        tail_n2, tail_inv, tail_hat, tail_t = sem("a_tail_n2"), sem("a_tail_inv"), sem("a_tail_hat"), sem("a_tail_t")
        s_full, l_ready, p_ready, pn_ready = sem("a_s_full"), sem("a_l_ready"), sem("a_p_ready"), sem("a_pn_ready")
        pt_full, pt_copied, pt_tail = sem("a_pt_full"), sem("a_pt_copied"), sem("a_pt_tail")
        pv_done, pv_free = sem("a_pv_done"), sem("a_pv_free")
        misc_full, misc_free = sem("a_misc_full"), sem("a_misc_free")
        mv_ready, rstd_ready, xn_ready = sem("a_mv"), sem("a_rstd"), sem("a_xn")
        qn2_ready, qinv_ready, qhat_ready = sem("a_qn2"), sem("a_qinv"), sem("a_qhat")
        qblock_ready = sem("a_qblock")
        elmin_ready, elexp_ready = sem("a_elmin"), sem("a_elexp")
        lg_ready, lgexp_ready, wsel_ready = sem("a_lg"), sem("a_lgexp"), sem("a_wsel")
        xn3_stored = sem("a_xn3")
        w_out = sem("a_w_out")
        v_steps, s_steps, p_steps = sem("a_vsteps"), sem("a_ssteps"), sem("a_psteps")

        def use(i, name, last=False):
            if i is None:
                return MISC_FIRST.index(name)
            return len(MISC_FIRST) + len(MISC) * i + (MISC_LAST if last else MISC).index(name)

        def ln_turn(i, which):
            return 0 if i is None else 1 + 3 * i + which

        consts = [(ident, A["ident"]), (wq, A["l0_wq"]), (wo, A["l0_wo"]), (bias, A["attn_bias"]),
                  (onehot, A["onehot"]), (bq, A["l0_bq"]), (bo, A["l0_bo"]), (aq, A["a_wq"]),
                  (ak, A["a_wk"]), (av, A["a_wv"]), (ao, A["a_wo"]), (gate, A["gate"]),
                  (cmaskT, A["cmaskT"]), (lower, A["lower"]), (qscale, A["scale_log"])]

        with nc.Block() as block:

            @block.sync
            def _(sp):
                sp.dma_start(w_raw, A["l0_wk"]).then_inc(wkv_in, 16)
                sp.dma_start(ctx_tail[:], A["ctx_tail"]).then_inc(tail_in, 16)

                def load_ctx(t, j):
                    n = 4 * t + j
                    if not (isinstance(n, int) and n < 2):
                        sp.wait_ge(ctx_lo_ready, n - 1)
                    sp.dma_start(ctx_raw[j % 2][:], A["ctxT"][bass.ds(n, 1)].rearrange("o p c k -> (o p) c k")[:, :, 0:KH * P]).then_inc(ctx_in[j % 2], 16)

                load_ctx(0, 0)
                load_ctx(0, 1)
                sp.dma_start(X[:], A["x"]).then_inc(x_in, 16)
                for dst, src in consts:
                    sp.dma_start(dst[:], src).then_inc(w_in, 16)
                sp.wait_ge(w_lo, 1)
                sp.dma_start(w_raw, A["l0_wv"]).then_inc(wkv_in, 16)
                load_ctx(0, 2)
                load_ctx(0, 3)
                with sp.Fori(0, TILES - 1) as i:
                    for j in range(BT):
                        load_ctx(i + 1, j)
                sp.wait_ge(misc_free, use(TILES - 1, "wT", True) + 1)
                sp.dma_start(w_dram[:], wT[:]).then_inc(w_out, 16)
                sp.wait_ge(w_out, 16)

            @block.tensor
            def _(pe):
                def kv_half(t, j, h):
                    n = 8 * t + 2 * j + h
                    r = j % 2
                    if h == 0:
                        pe.wait_ge(ctx_lo_ready, 4 * t + j + 1)
                    ks = slice(h * P, (h + 1) * P)
                    for w, ps, full, free in ((wk, k_ps, k_full, k_free), (wv, v_ps, v_full, v_free)):
                        pe.wait_ge(free, n)
                        for c in range(C):
                            mm = product3(pe, ps[:], (ctx_hi[r][:, c, ks], ctx_lo[r][:, c, ks]),
                                          (w[0][:, c, :], w[1][:, c, :]), c == 0, c == C - 1)
                        mm.then_inc(full, 1)

                def kt_half(t, j, h):
                    n = 8 * t + 2 * j + h
                    pe.wait_ge(khat_ready, n + 1)
                    pe.wait_ge(kt_free, n)
                    for c in range(C):
                        tr = pe.transpose(kt_ps[:, c * P:(c + 1) * P], khat[h][:, c * P:(c + 1) * P], ident[:])
                    tr.then_inc(kt_full, 1)

                def kv(t, j):
                    kv_half(t, j, 0)
                    kv_half(t, j, 1)
                    kt_half(t, j, 0)

                def turn(i, name, last, src, ready=None, dst=None):
                    pe.wait_ge(misc_free, use(i, name, last))
                    for c in range(C):
                        tr = pe.transpose(misc[:, c * P:(c + 1) * P], src[:, c * P:(c + 1) * P], ident[:])
                    tr.then_inc(misc_full, 1)

                def project_q(i):
                    pe.wait_ge(misc_free, use(i, "q"))
                    for c in range(C):
                        mm = pe.matmul(misc[:], xnT1[:, c, :], wq[:, c, :], start=c == 0, stop=c == C - 1)
                    mm.then_inc(misc_full, 1)

                def q_transposed(i):
                    n = 0 if i is None else i + 1
                    pe.wait_ge(qhat_ready, n + 1)
                    turn(i, "qT", False, qs)

                def scores(i, u):
                    j, g, m = u // G, u % G, UNITS * i + u
                    if g == 0:
                        pe.wait_ge(kt_free, 8 * i + 2 * j + 2)
                        pe.wait_ge(ktail_ready, BT * i + j + 1)
                    if u == 0:
                        pe.wait_ge(qblock_ready, i + 1)
                    pe.wait_ge(l_ready, turn_before(m, u))
                    pe.matmul(s_ps[u % 2][:, 0:LK], qblock[:, g, j, :], keysT[j][:, g, :],
                              start=True, stop=True).then_inc(s_full, 1)

                def probs_transposed(i, u):
                    m = UNITS * i + u
                    pe.wait_ge(pn_ready, m + 1)
                    pe.wait_ge(pt_copied, m)
                    pe.wait_ge(pt_tail, m)
                    src = pn[u % 2]
                    pe.transpose(pt_ps[:, 0:P], src[:, 0:P], ident[:])
                    pe.transpose(pt_ps[:, P:2 * P], src[:, P:2 * P], ident[:])
                    pe.transpose(pt_ps[0:B, 2 * P:3 * P], src[:, 2 * P:2 * P + B], ident[:]).then_inc(pt_full, 1)

                def values(i, u):
                    j, g, m = u // G, u % G, UNITS * i + u
                    pe.wait_ge(pt_copied, m + 1)
                    pe.wait_ge(pt_tail, m + 1)
                    if g == 0:
                        pe.wait_ge(v_free, 8 * i + 2 * j + 2)
                        pe.wait_ge(pv_free, BT * i + j)
                    out, fs = pv_ps[:, g * P:(g + 1) * P], slice(g * P, (g + 1) * P)
                    pe.matmul(out, vals[j][0][:, fs], pT[u % 2][:, 0:P], start=True, stop=False)
                    pe.matmul(out, vals[j][1][:, fs], pT[u % 2][:, P:2 * P], start=False, stop=False)
                    pe.matmul(out, vtail[:, fs], pTtail[u % 2][:], start=False, stop=True).then_inc(pv_done, 1)

                def project(i, name, last, lhs, rhs):
                    pe.wait_ge(misc_free, use(i, name, last))
                    for k, (a, b) in enumerate(zip(lhs, rhs)):
                        mm = pe.matmul(misc[:], a, b, start=k == 0, stop=k == len(lhs) - 1)
                    mm.then_inc(misc_full, 1)

                def tile(i, last):
                    t = i + 1
                    for k in range(UNITS + 3):
                        if k < UNITS:
                            scores(i, k)
                        if 0 <= k - 2 < UNITS:
                            probs_transposed(i, k - 2)
                        if 0 <= k - 3:
                            values(i, k - 3)
                        if not last and k == 9:
                            kv(t, 0)
                        if not last and k == 14:
                            kt_half(t, 0, 1)
                            kv(t, 1)
                    pe.wait_ge(pv_free, BT * i + BT)
                    project(i, "wo", last, [oT[:, g, :] for g in range(G)], [wo[:, g, :] for g in range(G)])
                    if not last:
                        kt_half(t, 1, 1)
                        pe.wait_ge(xn_ready, ln_turn(i, 0) + 1)
                        turn(i, "xT1", False, xn)
                        project_q(i)
                        kv_half(t, 2, 0)
                    pe.wait_ge(xn_ready, (ln_turn(i, 1) if not last else ln_turn(i, 0)) + 1)
                    turn(i, "xT2", last, xn)
                    if not last:
                        q_transposed(i)
                        kv_half(t, 2, 1)
                        kt_half(t, 2, 0)
                    pe.wait_ge(misc_free, use(i, "qkv", last))
                    for w, col in ((aq, 0), (ak, P)):
                        for c in range(C):
                            pe.matmul(misc[0:HK, col:col + P], w[:, c, :], xnT[:, c, :], start=c == 0, stop=c == C - 1)
                    for c in range(C):
                        mm = pe.matmul(misc[:, 2 * P:2 * P + HK], xnT[:, c, :], av[:, c, :], start=c == 0, stop=c == C - 1)
                    mm.then_inc(misc_full, 1)
                    if not last:
                        kt_half(t, 2, 1)
                        kv_half(t, 3, 0)
                    pe.wait_ge(misc_free, use(i, "am", last))
                    pe.matmul(misc[:, 0:P], qk[:, P:2 * P], qk[:, 0:P], start=True, stop=True).then_inc(misc_full, 1)
                    pe.wait_ge(misc_free, use(i, "num", last))
                    pe.matmul(misc[0:HK, 0:P], va[:], am[:], start=True, stop=True)
                    pe.matmul(misc[:, P:P + 1], am[:], ones[:], start=True, stop=True).then_inc(misc_full, 1)
                    project(i, "z", last, [numT[:]], [ao[:]])
                    if not last:
                        kv_half(t, 3, 1)
                        kt_half(t, 3, 0)
                    pe.wait_ge(xn_ready, (ln_turn(i, 2) if not last else ln_turn(i, 1)) + 1)
                    turn(i, "xT3", last, xn)
                    pe.wait_ge(misc_free, use(i, "log", last))
                    for c in range(C):
                        mm = pe.matmul(misc[:, 0:E], xnT[:, c, :], gate[:, c, :], start=c == 0, stop=c == C - 1)
                    mm.then_inc(misc_full, 1)
                    if not last:
                        kt_half(t, 3, 1)
                    pe.wait_ge(wsel_ready, i + 1)
                    pe.wait_ge(misc_free, use(i, "wT", last))
                    pe.transpose(misc[0:E, 0:P], wsel[:], ident[:]).then_inc(misc_full, 1)

                pe.wait_ge(w_lo, 2)
                pe.wait_ge(tail_in, 16)
                pe.wait_ge(w_in, 16 * len(consts))
                pe.wait_ge(init, 4)
                for w, ps in ((wk, k_ps), (wv, v_ps)):
                    for half in range(2):
                        for c in range(C):
                            mm = pe.matmul(ps[0:B, :], ctx_tail[:, c, :], cast(w[half][:, c, :]),
                                           start=c == 0 and half == 0, stop=c == C - 1 and half == 1)
                mm.then_inc(tail_full, 1)
                pe.wait_ge(tail_hat, 1)
                for c in range(C):
                    tr = pe.transpose(kt_ps[:, c * B:(c + 1) * B], khat[0][0:B, c * P:(c + 1) * P], ident[0:B, 0:B])
                tr.then_inc(tail_t, 1)
                pe.wait_ge(tail_done, 1)
                pe.wait_ge(xn_ready, 1)
                turn(None, "xT1", False, xn)
                for j in range(BT):
                    kv(0, j)
                    if j == 0:
                        project_q(None)
                    if j == 1:
                        q_transposed(None)
                    kt_half(0, j, 1)
                with pe.Fori(0, TILES - 1) as i:
                    tile(i, False)
                tile(TILES - 1, True)

            @block.scalar
            def _(act):
                def split_ctx(t, j):
                    n = 4 * t + j
                    act.wait_ge(ctx_in[j % 2], 16 * (2 * t + j // 2) + 16)
                    if not (isinstance(n, int) and n < 2):
                        act.wait_ge(v_full, 2 * n - 2)
                    act.activation(ctx_hi[j % 2][:], ctx_raw[j % 2][:], ACT.Copy).then_inc(ctx_hi_ready, 1)

                def kv_half(t, j, h):
                    n = 8 * t + 2 * j + h
                    act.wait_ge(k_full, n + 1)
                    if not (isinstance(n, int) and n < 2):
                        act.wait_ge(khat_ready, n - 1)
                    act.activation(ksq[h][:], k_ps[:], ACT.Square).then_inc(k_sq, 1)
                    act.activation(kraw[h][:], k_ps[:], ACT.Copy).then_inc(k_free, 1)
                    act.wait_ge(v_full, n + 1)
                    if h == 0 and not (isinstance(t, int) and t == 0):
                        act.wait_ge(pv_done, UNITS * (t - 1) + G * j + G)
                    act.activation(vals[j][h][:], v_ps[:], ACT.Copy).then_inc(v_free, 1)

                def kt_half(t, j, h):
                    n = 8 * t + 2 * j + h
                    act.wait_ge(kt_full, n + 1)
                    if h == 0 and not (isinstance(t, int) and t == 0):
                        act.wait_ge(s_full, UNITS * (t - 1) + G * j + G)
                    act.activation(keysT[j][:, :, h * P:(h + 1) * P], kt_ps[:].rearrange("p (c k) -> p c k", c=C),
                                   ACT.Copy).then_inc(kt_free, 1)

                def kv(t, j):
                    kv_half(t, j, 0)
                    kv_half(t, j, 1)
                    kt_half(t, j, 0)

                def exps(i, u):
                    m, r = UNITS * i + u, u % 2
                    act.wait_ge(l_ready, m + 1)
                    act.wait_ge(pn_ready, turn_before(m, u))
                    act.activation(prob[r][:], logit[r][:], ACT.Exp, bias=nmax[r][:], scale=-1.0,
                                   accum_out=psum_[r][:]).then_inc(p_ready, 1)

                def probs_copy(i, u):
                    m, r = UNITS * i + u, u % 2
                    act.wait_ge(pt_full, m + 1)
                    act.wait_ge(pv_done, turn_before(m, u))
                    act.activation(pT[r][:], pt_ps[:, 0:KH * P], ACT.Copy).then_inc(pt_copied, 1)
                    act.activation(pTtail[r][:], pt_ps[0:B, KH * P:KH * P + P], ACT.Copy).then_inc(pt_tail, 1)

                def tile(i, last):
                    t = i + 1
                    for k in range(UNITS + 3):
                        if k < UNITS:
                            exps(i, k)
                        if 0 <= k - 2 < UNITS:
                            probs_copy(i, k - 2)
                        if not last and k == 7:
                            split_ctx(t, 0)
                        if not last and k == 9:
                            kv(t, 0)
                            split_ctx(t, 1)
                        if not last and k == 14:
                            kt_half(t, 0, 1)
                            kv(t, 1)
                            split_ctx(t, 2)
                    if not last:
                        kt_half(t, 1, 1)
                        kv_half(t, 2, 0)
                        kv_half(t, 2, 1)
                        split_ctx(t, 3)
                        kt_half(t, 2, 0)
                    act.wait_ge(elmin_ready, i + 1)
                    act.activation(elexp[:], elmin[:], ACT.Exp).then_inc(elexp_ready, 1)
                    if not last:
                        kt_half(t, 2, 1)
                        kv_half(t, 3, 0)
                        kv_half(t, 3, 1)
                        kt_half(t, 3, 0)
                    act.wait_ge(lg_ready, i + 1)
                    act.activation(lgexp[:], lg[:], ACT.Exp, bias=lgmax[:], accum_out=lgsum[:]).then_inc(lgexp_ready, 1)
                    if not last:
                        kt_half(t, 3, 1)

                act.wait_ge(wkv_in, 16)
                act.activation(wk[0][:], w_raw, ACT.Copy).then_inc(w_hi, 1)
                split_ctx(0, 0)
                act.wait_ge(wkv_in, 32)
                act.activation(wv[0][:], w_raw, ACT.Copy).then_inc(w_hi, 1)
                act.wait_ge(init, 3)
                act.activation(qscale[:], qscale[:], ACT.Exp).then_inc(scale_ready, 1)
                act.wait_ge(tail_full, 1)
                act.activation(ksq[0][0:B, :], k_ps[0:B, :], ACT.Square).then_inc(tail_n2, 1)
                for j in range(BT):
                    kv(0, j)
                    if j < BT - 1:
                        split_ctx(0, j + 1)
                    kt_half(0, j, 1)
                with act.Fori(0, TILES - 1) as i:
                    tile(i, False)
                tile(TILES - 1, True)

            @block.gpsimd
            def _(pool):
                step = Steps(pool, p_steps)

                def split_ctx(t, j):
                    n = 4 * t + j
                    pool.wait_ge(ctx_hi_ready, n + 1)
                    pool.tensor_tensor(ctx_lo[j % 2][:], ctx_raw[j % 2][:], cast(ctx_hi[j % 2][:]), ALU.subtract)\
                        .then_inc(ctx_lo_ready, 1)

                def inverse(src, dst, ready, done, n):
                    pool.wait_ge(ready, n + 1)
                    pool.tensor_tensor(dst, src, mhalf[0:src.shape[0], :], ALU.pow).then_inc(done, 1)

                def layer_norm(n):
                    pool.wait_ge(mv_ready, n + 1)
                    step(pool.tensor_tensor(veps[:], mv[:, 1:2], eps[:], ALU.add))
                    pool.tensor_tensor(rstd[:], veps[:], mhalf[:, 0:1], ALU.pow).then_inc(rstd_ready, 1)

                def k_half(t, j, h):
                    inverse(kn2[h][:], kinv[h][:], kn2_ready, kinv_ready, 8 * t + 2 * j + h)

                def tail_column(t, j):
                    if not (isinstance(t, int) and t == 0):
                        pool.wait_ge(s_full, UNITS * (t - 1) + G * j + G)
                    pool.tensor_copy(keysT[j][:, :, KH * P:LK], ktailT[:, :, bass.ds(4 * t + j, 1)]).then_inc(ktail_ready, 1)

                def q_norm(n):
                    inverse(qn2[:], qinv[:], qn2_ready, qinv_ready, n)

                def tile(i, last):
                    t = i + 1
                    step.restart()
                    if not last:
                        layer_norm(ln_turn(i, 0))
                        split_ctx(t, 0)
                        tail_column(t, 0)
                        k_half(t, 0, 0)
                        k_half(t, 0, 1)
                        split_ctx(t, 1)
                        tail_column(t, 1)
                        k_half(t, 1, 0)
                        k_half(t, 1, 1)
                        split_ctx(t, 2)
                        tail_column(t, 2)
                        layer_norm(ln_turn(i, 1))
                        q_norm(i + 1)
                        k_half(t, 2, 0)
                        k_half(t, 2, 1)
                        split_ctx(t, 3)
                        tail_column(t, 3)
                        k_half(t, 3, 0)
                        layer_norm(ln_turn(i, 2))
                        k_half(t, 3, 1)
                    else:
                        layer_norm(ln_turn(i, 0))
                        layer_norm(ln_turn(i, 1))
                    pool.wait_ge(misc_free, use(i, "xT3", last) + 1)
                    pool.tensor_copy(XN3T[:, :, bass.ds(i * P, P)], xnT[:]).then_inc(xn3_stored, 1)

                for k, (hi, lo) in enumerate((wk, wv)):
                    pool.wait_ge(w_hi, k + 1)
                    pool.tensor_tensor(lo[:], w_raw, cast(hi[:]), ALU.subtract).then_inc(w_lo, 1)
                    if k == 0:
                        split_ctx(0, 0)
                pool.wait_ge(init, 4)
                layer_norm(0)
                inverse(kn2[0][0:B, :], kinv[0][0:B, :], tail_n2, tail_inv, 1)
                pool.wait_ge(tail_done, 1)
                for j in range(BT):
                    k_half(0, j, 0)
                    k_half(0, j, 1)
                    if j == 0:
                        q_norm(0)
                    if j < BT - 1:
                        split_ctx(0, j + 1)
                    tail_column(0, j)
                with pool.Fori(0, TILES - 1) as i:
                    tile(i, False)
                tile(TILES - 1, True)

            @block.vector
            def _(dve):
                step = Steps(dve, v_steps)

                def heads(ap):
                    return ap.rearrange("p (h d) -> p h d", h=H)

                def spread(ap, n=P):
                    return ap.rearrange("p (h o) -> p h o", o=1).to_broadcast([n, H, DH])

                def norm2_of(squares, dst):
                    step(dve.tensor_reduce(dst, heads(squares), AX.X, ALU.add))
                    return dve.tensor_scalar(dst, dst, NORM2_MIN, None, ALU.max)

                def norm2(t, j, h):
                    n = 8 * t + 2 * j + h
                    dve.wait_ge(k_sq, n + 1)
                    norm2_of(ksq[h][:], kn2[h][:]).then_inc(kn2_ready, 1)

                def normalise(t, j, h):
                    n = 8 * t + 2 * j + h
                    dve.wait_ge(kinv_ready, n + 1)
                    dve.wait_ge(k_free, n + 1)
                    if not (isinstance(n, int) and n < 2):
                        dve.wait_ge(kt_full, n - 1)
                    dve.tensor_tensor(heads(khat[h][:]), heads(kraw[h][:]), spread(kinv[h][:]), ALU.mult)\
                        .then_inc(khat_ready, 1)

                def kv(t, j):
                    norm2(t, j, 0)
                    norm2(t, j, 1)
                    normalise(t, j, 0)

                def layer_norm(x, n):
                    step(dve.memset(fence[:, 2:3], 0.0))
                    step(dve.bn_stats(stats[:], x))
                    dve.bn_aggr(mv[:], stats[:]).then_inc(mv_ready, 1)
                    dve.wait_ge(rstd_ready, n + 1)
                    dve.tensor_scalar(xn[:], x, mv[:, 0:1], rstd[:], ALU.subtract, ALU.mult).then_inc(xn_ready, 1)

                def bank_full(i, name, last):
                    dve.wait_ge(misc_full, use(i, name, last) + 1)

                def turned(i, name, last, dst):
                    bank_full(i, name, last)
                    dve.tensor_copy(dst[:].rearrange("p c t -> p (c t)"), misc[:]).then_inc(misc_free, 1)

                def q_norms(i):
                    n = 0 if i is None else i + 1
                    bank_full(i, "q", False)
                    dve.tensor_tensor(qs[:], misc[:], bq[:], ALU.add).then_inc(misc_free, 1)
                    dve.wait_ge(misc_free, use(i, "q") + 1)
                    step(dve.tensor_tensor(qsq[:], qs[:], qs[:], ALU.mult))
                    norm2_of(qsq[:], qn2[:]).then_inc(qn2_ready, 1)

                def q_hat(i):
                    n = 0 if i is None else i + 1
                    dve.wait_ge(qinv_ready, n + 1)
                    step(dve.tensor_tensor(qinv[:], qinv[:], qscale[:], ALU.mult))
                    dve.tensor_tensor(heads(qs[:]), heads(qs[:]), spread(qinv[:]), ALU.mult).then_inc(qhat_ready, 1)

                def q_blocks(i):
                    n = 0 if i is None else i + 1
                    bank_full(i, "qT", False)
                    for h in range(BT):
                        rows = slice(h * DH, (h + 1) * DH)
                        cp = dve.tensor_copy(qblock[rows, :, :, h * LQ:(h + 1) * LQ],
                                             misc[rows, :].rearrange("p (g j q) -> p g j q", g=G, j=BT))
                        if h < BT - 1:
                            step(cp)
                    cp.then_inc(qblock_ready, 1)
                    dve.wait_ge(qblock_ready, n + 1)
                    dve.sem_inc(misc_free, 1)

                def logits(i, u):
                    m, r = UNITS * i + u, u % 2
                    dve.wait_ge(s_full, m + 1)
                    dve.wait_ge(p_ready, turn_before(m, u))
                    dve.memset(fence[:, r:r + 1], 0.0)
                    dve.tensor_tensor_reduce(logit[r][:], s_ps[r][:, 0:LK], bias[:], -1.0, 3e38, ALU.add, ALU.min,
                                             nmax[r][:]).then_inc(l_ready, 1)

                def normed(i, u):
                    j, m, r = u // G, UNITS * i + u, u % 2
                    dve.wait_ge(p_ready, m + 1)
                    dve.wait_ge(pt_full, turn_before(m, u))
                    step(dve.reciprocal(rsum[r][:], psum_[r][:]))
                    step(dve.tensor_scalar(pn[r][:, KH * P:], onehot[:, bass.ds(BT * i + j, 1), :].rearrange("p o b -> p (o b)"),
                                           prob[r][:, KH * P:LK], rsum[r][:], ALU.mult, ALU.mult))
                    dve.tensor_scalar(pn[r][:, 0:KH * P], prob[r][:, 0:KH * P], rsum[r][:], None, ALU.mult)\
                        .then_inc(pn_ready, 1)

                def outputs(i, j):
                    dve.wait_ge(pv_done, UNITS * i + G * j + G)
                    for h in range(BT):
                        rows = slice(h * DH, (h + 1) * DH)
                        cp = dve.tensor_copy(oT[rows, :, j * LQ:(j + 1) * LQ],
                                             pv_ps[rows, :].rearrange("p (g q) -> p g q", g=G)[:, :, h * LQ:(h + 1) * LQ])
                    cp.then_inc(pv_free, 1)

                def tile(i, last):
                    t = i + 1
                    step.restart()
                    x = X[:, bass.ds(i, 1), :].rearrange("p o d -> p (o d)")
                    if not last:
                        x1 = X[:, bass.ds(i + 1, 1), :].rearrange("p o d -> p (o d)")
                        layer_norm(x1, ln_turn(i, 0))
                    for k in range(UNITS + 3):
                        if k < UNITS:
                            logits(i, k)
                        if 0 <= k - 1 < UNITS:
                            normed(i, k - 1)
                        if 0 <= k - 3 and (k - 3) % G == G - 1:
                            outputs(i, (k - 3) // G)
                        if not last and k == 9:
                            kv(t, 0)
                        if not last and k == 14:
                            normalise(t, 0, 1)
                            kv(t, 1)
                    bank_full(i, "wo", last)
                    dve.tensor_tensor(x, misc[:], x, ALU.add).then_inc(misc_free, 1)
                    dve.wait_ge(misc_free, use(i, "wo", last) + 1)
                    step(dve.tensor_tensor(x, x, bo[:], ALU.add))
                    if not last:
                        normalise(t, 1, 1)
                        turned(i, "xT1", False, xnT1)
                        layer_norm(x, ln_turn(i, 1))
                        q_norms(i)
                        dve.wait_ge(xn3_stored, i)
                        turned(i, "xT2", last, xnT)
                        q_hat(i)
                        q_blocks(i)
                        norm2(t, 2, 0)
                        norm2(t, 2, 1)
                        normalise(t, 2, 0)
                    else:
                        layer_norm(x, ln_turn(i, 0))
                        dve.wait_ge(xn3_stored, i)
                        turned(i, "xT2", last, xnT)
                    bank_full(i, "qkv", last)
                    dve.tensor_scalar(elmin[:], misc[0:HK, 0:2 * P], 0.0, None, ALU.min).then_inc(elmin_ready, 1)
                    step(dve.tensor_copy(va[:], misc[:, 2 * P:2 * P + HK]))
                    dve.wait_ge(elexp_ready, i + 1)
                    dve.scalar_tensor_tensor(out=qk[:], in0=misc[0:HK, 0:2 * P], scalar=0.0, in1=elexp[:],
                                             op0=ALU.max, op1=ALU.add).then_inc(misc_free, 1)
                    if not last:
                        normalise(t, 2, 1)
                        norm2(t, 3, 0)
                    bank_full(i, "am", last)
                    dve.tensor_tensor(am[:], misc[:, 0:P], cmaskT[:], ALU.mult).then_inc(misc_free, 1)
                    bank_full(i, "num", last)
                    step(dve.tensor_scalar(den[:], misc[:, P:P + 1], 1e-6, None, ALU.add))
                    step(dve.reciprocal(rden[:], den[:]))
                    dve.tensor_copy(numT[:], misc[0:HK, 0:P]).then_inc(misc_free, 1)
                    bank_full(i, "z", last)
                    dve.scalar_tensor_tensor(out=x, in0=misc[:], scalar=rden[:], in1=x,
                                             op0=ALU.mult, op1=ALU.add).then_inc(misc_free, 1)
                    if not last:
                        normalise(t, 3, 0)
                        dve.wait_ge(misc_free, use(i, "z", last) + 1)
                        layer_norm(x, ln_turn(i, 2))
                        norm2(t, 3, 1)
                    else:
                        dve.wait_ge(misc_free, use(i, "z", last) + 1)
                        layer_norm(x, ln_turn(i, 1))
                    turned(i, "xT3", last, xnT)
                    if not last:
                        normalise(t, 3, 1)
                    bank_full(i, "log", last)
                    dve.tensor_copy(lg[:], misc[:, 0:E]).then_inc(misc_free, 1)
                    dve.wait_ge(misc_free, use(i, "log", last) + 1)
                    dve.tensor_reduce(lgmax[:], lg[:], AX.X, ALU.max, negate=True).then_inc(lg_ready, 1)
                    dve.wait_ge(lgexp_ready, i + 1)
                    step(dve.reciprocal(lgr[:], lgsum[:]))
                    step(dve.tensor_scalar(score[:], lgexp[:], lgr[:], None, ALU.mult))
                    other = score[:].rearrange("p (o e) -> p o e", o=1).to_broadcast([P, E, E])
                    own = score[:].rearrange("p (e o) -> p e o", o=1).to_broadcast([P, E, E])
                    step(dve.tensor_tensor(above[:], other, own, ALU.is_gt))
                    step(dve.tensor_tensor(tie[:], other, own, ALU.is_equal))
                    step(dve.tensor_tensor(tie[:], tie[:], lower[:], ALU.mult))
                    step(dve.tensor_tensor(above[:], above[:], tie[:], ALU.add))
                    step(dve.tensor_reduce(rank[:], above[:], AX.X, ALU.add))
                    step(dve.tensor_scalar(sel[:], rank[:], 1.5, None, ALU.is_lt))
                    step(dve.tensor_tensor(score[:], score[:], sel[:], ALU.mult))
                    dve.scalar_tensor_tensor(out=wsel[:], in0=sel[:], scalar=-1.0, in1=score[:],
                                             op0=ALU.add, op1=ALU.add).then_inc(wsel_ready, 1)
                    bank_full(i, "wT", last)
                    dve.tensor_copy(wT[:, bass.ds(i * P, P)], misc[0:E, 0:P]).then_inc(misc_free, 1)

                dve.wait_ge(w_lo, 2)
                dve.memset(qblock[:], 0.0).then_inc(init, 1)
                step(dve.memset(eps[:], 1e-5))
                dve.memset(mhalf[:], -0.5).then_inc(init, 1)
                dve.wait_ge(w_in, 16 * len(consts))
                dve.tensor_scalar(qscale[:], qscale[:], float(np.log(100.0)), None, ALU.min).then_inc(init, 1)
                dve.memset(ones[:], 1.0).then_inc(init, 1)
                dve.wait_ge(init, 4)
                dve.wait_ge(x_in, 16)
                layer_norm(X[:, 0, :], 0)
                dve.wait_ge(tail_n2, 1)
                norm2_of(ksq[0][0:B, :], kn2[0][0:B, :]).then_inc(tail_n2, 1)
                dve.wait_ge(tail_inv, 1)
                dve.tensor_tensor(heads(khat[0][0:B, :]), heads(k_ps[0:B, :]), spread(kinv[0][0:B, :], B), ALU.mult)\
                   .then_inc(tail_hat, 1)
                step(dve.tensor_copy(vtail[:], v_ps[0:B, :]))
                dve.wait_ge(tail_t, 1)
                dve.tensor_copy(ktailT[:].rearrange("p c b -> p (c b)"), kt_ps[:, 0:C * B]).then_inc(tail_done, 1)
                turned(None, "xT1", False, xnT1)
                dve.wait_ge(scale_ready, 1)
                for j in range(BT):
                    kv(0, j)
                    if j == 0:
                        q_norms(None)
                        q_hat(None)
                    if j == 1:
                        q_blocks(None)
                    normalise(0, j, 1)
                with dve.Fori(0, TILES - 1) as i:
                    tile(i, False)
                tile(TILES - 1, True)



STEPS_1 = (0.25, 0.75, 1.25, 1.75)
STEPS_2 = (2.5, 3.5)
STEP_4 = 5.0
FFN_TILES = 3 * FC
QS = 4


def blocks(ap, f):
    return ap.rearrange("p (n b) -> p n b", b=BLK) if f else ap


def spread_blocks(ap, n):
    return ap.rearrange("p (n o) -> p n o", o=1).to_broadcast([P, n, BLK])


def quant_scaled(dve, step, src, f, half_scale, inverse, y):
    n = f // BLK
    step(dve.tensor_reduce(half_scale, blocks(src, f), AX.X, ALU.max, apply_absolute_value=True))
    step(dve.tensor_scalar(half_scale, half_scale, 1.0 / 6.0, 1e-12, ALU.mult, ALU.max))
    step(dve.reciprocal(inverse, half_scale))
    step(dve.tensor_scalar(half_scale, half_scale, 0.5, None, ALU.mult))
    return dve.tensor_tensor(blocks(y, f), blocks(src, f), spread_blocks(inverse, n), ALU.mult)


def quant_rounded(dve, step, mag, sign, low, high, half_scale, f, out):
    step(dve.tensor_scalar(low, mag, STEPS_1[0], None, ALU.is_gt))
    step(dve.tensor_scalar(high, mag, STEP_4, 2.0, ALU.is_gt, ALU.mult))
    for m in STEPS_1[1:]:
        step(dve.scalar_tensor_tensor(out=low, in0=mag, scalar=m, in1=low, op0=ALU.is_gt, op1=ALU.add))
    for m in STEPS_2:
        step(dve.scalar_tensor_tensor(out=high, in0=mag, scalar=m, in1=high, op0=ALU.is_gt, op1=ALU.add))
    step(dve.scalar_tensor_tensor(out=low, in0=high, scalar=2.0, in1=low, op0=ALU.mult, op1=ALU.add))
    step(dve.tensor_tensor(low, low, sign, ALU.mult))
    return dve.tensor_tensor(blocks(out, f), blocks(low, f), spread_blocks(half_scale, f // BLK), ALU.mult)


SCALE_AT = (0, 5, 10, 15)
ROUND_AT = (4, 8, 13, 17)
TURN_AT = (9, 14, 19, 23)
TURN_BACK = 5

SHARED = I1 // D
PASSES = SHARED + E
TB = T // 512
FILLS = TB * C


def phase_b(nc, A, X, XN3T, w_dram, q_dram):
    with ExitStack() as ctx:
        sb = lambda n, s, d=F32: ctx.enter_context(nc.sbuf_tensor("pb_" + n, s, d))
        sem = lambda n: ctx.enter_context(nc.semaphore("b_" + n))
        Y = XN3T
        xn = [sb("xn_hi", [P, C, T], F32R), sb("xn_lo", [P, C, T], F32R)]
        hid = [sb("hid_hi", [P, C, T], F32R), sb("hid_lo", [P, C, T], F32R)]
        w = [[sb(f"w{m}_hi", [P, C, D], F32R), sb(f"w{m}_lo", [P, C, D], F32R)] for m in range(3)]
        raw = sb("raw", [P, C, D])
        q_raw, q_y, q_mag, q_val = (sb(n, [P, D]) for n in ("q_raw", "q_y", "q_mag", "q_val"))
        q_turn = sb("q_turn", [P, D])
        q_sign, q_low, q_high = (sb(n, [P, D], BF16) for n in ("q_sign", "q_low", "q_high"))
        q_scale, q_inv = sb("q_scale", [P, D // BLK]), sb("q_inv", [P, D // BLK])
        gated = sb("gated", [P, FILLS, 512])
        scaled = [sb(f"scaled{r}", [P, 512]) for r in range(2)]
        act_out = [sb(f"act_out{r}", [P, 512]) for r in range(2)]
        wrow = sb("wrow", [P, T])
        weight = sb("weight", [P, T])
        mask = sb("mask", [P, T])
        b1, b2, b3 = (sb(f"b{m}", [P, E, C]) for m in (1, 2, 3))
        b1_now = sb("b1_now", [P, C])
        ident = sb("ident", [P, P])
        bank = [ctx.enter_context(nc.psum_tensor(f"pb{b}", [P, 512], F32)) for b in range(8)]

        w_in = sem("w_in")
        q_in, q_y_ready, q_mag_ready, q_val_ready = sem("q_in"), sem("q_y"), sem("q_mag"), sem("q_val")
        q_turned, q_copied, q_out = sem("q_turned"), sem("q_copied"), sem("q_out")
        w_hi = [sem(f"w_hi{m}") for m in range(3)]
        w_lo = [sem(f"w_lo{m}") for m in range(3)]
        c_in = sem("c_in")
        row_in = sem("row_in")
        row_used = sem("row_used")
        xn_hi, xn_lo = sem("xn_hi"), sem("xn_lo")
        full = [sem(f"full{m}") for m in range(3)]
        free = [sem(f"free{m}") for m in range(3)]
        act_ready = sem("act_ready")
        hid_hi, hid_lo = sem("hid_hi"), sem("hid_lo")
        y_added = sem("y_added")
        turned, x_added = sem("turned"), sem("x_added")
        v_steps, s_steps = sem("vsteps"), sem("ssteps")

        def ks(k):
            return slice((k // C) * 512, (k // C) * 512 + 512)

        with nc.Block() as block:

            @block.sync
            def _(sp):
                def load(n, m):
                    if m > 0:
                        sp.wait_ge(w_lo[m - 1], n + 1)
                    elif not (isinstance(n, int) and n == 0):
                        sp.wait_ge(w_lo[2], n)
                    sp.dma_start(raw[:], A["experts"][bass.ds(3 * n + m, 1)].rearrange("o p c d -> (o p) c d"))\
                      .then_inc(w_in, 16)

                def load_row(n):
                    e = n - SHARED
                    sp.wait_ge(row_used, e)
                    sp.dma_start(wrow[:], w_dram[bass.ds(e, 1), :].to_broadcast([P, T])).then_inc(row_in, 16)

                load(0, 0)
                for dst, name in ((b1, "b1"), (b2, "b2"), (b3, "b3"), (ident, "ident")):
                    sp.dma_start(dst[:], A[name]).then_inc(c_in, 16)
                load(0, 1)
                load(0, 2)
                for n in range(1, SHARED):
                    for m in range(3):
                        load(n, m)
                with sp.Fori(SHARED, PASSES) as n:
                    load_row(n)
                    for m in range(3):
                        load(n, m)

            @block.tensor
            def _(pe):
                def quantised_turned(t, b):
                    pe.wait_ge(q_val_ready, t + 1)
                    for c in range(C):
                        tr = pe.transpose(bank[b][:, c * P:(c + 1) * P], q_val[:, c * P:(c + 1) * P], ident[:])
                    tr.then_inc(q_turned, 1)

                AFTER = {TURN_AT[s]: s for s in range(QS)}
                BEFORE = {TURN_AT[s] - TURN_BACK + FILLS: s for s in range(QS)}

                def products(n, m, tiles):
                    t0 = (1 + QS * (n - SHARED)) if tiles == QS else 0
                    first = isinstance(n, int) and n == 0
                    pe.wait_ge(w_lo[m], n + 1)
                    for k in range(FILLS):
                        f = FILLS * m + k
                        if BEFORE.get(f, QS) < tiles:
                            pe.wait_ge(q_copied, t0 + BEFORE[f] + 1)
                        if tiles == QS and f + 3 * FILLS in BEFORE:
                            pe.wait_ge(q_copied, t0)
                        if m == 2 and k % C == 0:
                            pe.wait_ge(hid_lo, FILLS * n + k + C)
                        if m > 0:
                            pe.wait_ge(free[m - 1], FILLS * n + k + 1)
                        elif not first:
                            pe.wait_ge(free[2], FILLS * (n - 1) + k + 1)
                        src = hid if m == 2 else xn
                        o = k % C
                        for c in range(C):
                            mm = product3(pe, bank[k][:], [x[:, c, o * P:(o + 1) * P] for x in w[m]],
                                          [x[:, c, ks(k)] for x in src], c == 0, c == C - 1)
                        mm.then_inc(full[m], 1)
                        s = AFTER.get(f, QS)
                        if s < tiles:
                            b = (f - TURN_BACK) % FILLS
                            pe.wait_ge(free[(f - TURN_BACK) // FILLS], FILLS * n + b + 1)
                            quantised_turned(t0 + s, b)

                pe.wait_ge(xn_lo, C)
                pe.wait_ge(c_in, 64)
                for n in range(SHARED):
                    for m in range(3):
                        products(n, m, int(n == SHARED - 1))
                with pe.Fori(SHARED, PASSES) as n:
                    for m in range(3):
                        products(n, m, QS)
                pe.wait_ge(q_copied, FFN_TILES)
                pe.wait_ge(y_added, FILLS * E)
                for t in range(TILES):
                    for c in range(C):
                        tr = pe.transpose(bank[t][:, c * P:(c + 1) * P], Y[:, c, t * P:(t + 1) * P], ident[:])
                    tr.then_inc(turned, 1)

            @block.scalar
            def _(act):
                step = Steps(act, s_steps)

                def high(n, m):
                    act.wait_ge(w_in, 16 * (3 * n + m) + 16)
                    if not (isinstance(n, int) and n == 0):
                        act.wait_ge(full[m], FILLS * n)
                    act.activation(w[m][0][:], raw[:], ACT.Copy).then_inc(w_hi[m], 1)

                def hidden_high(n, k):
                    act.activation(hid[0][:, k % C, ks(k)], act_out[k % 2][:], ACT.Copy).then_inc(hid_hi, 1)

                def load_tile(t):
                    act.dma_start(q_raw[:], A["ffn_w"][bass.ds(t, 1)].rearrange("o p d -> (o p) d")).then_inc(q_in, 16)

                def magnitude(t, last=False):
                    act.wait_ge(q_y_ready, t + 1)
                    if not last:
                        load_tile(t + 1)
                    act.wait_ge(q_val_ready, t)
                    act.activation(q_mag[:], q_y[:], ACT.Abs)
                    act.activation(q_sign[:], q_y[:], ACT.Sign).then_inc(q_mag_ready, 1)

                def tile_out(t, s):
                    b = (TURN_AT[s] - TURN_BACK) % FILLS
                    act.wait_ge(q_turned, t + 1)
                    act.wait_ge(q_out, 16 * t)
                    act.activation(q_turn[:], bank[b][:], ACT.Copy).then_inc(q_copied, 1)
                    act.wait_ge(q_copied, t + 1)
                    act.dma_start(q_dram[bass.ds(t, 1)].rearrange("o p d -> (o p) d"), q_turn[:]).then_inc(q_out, 16)

                def shared(n):
                    for k in range(FILLS):
                        act.wait_ge(full[0], FILLS * n + k + 1)
                        act.activation(gated[:, k, :], bank[k][:], ACT.Silu).then_inc(free[0], 1)
                        if n == SHARED - 1 and k == 0:
                            magnitude(0)
                    if n == SHARED - 1:
                        tile_out(0, 0)
                    high(n, 2)
                    for k in range(FILLS):
                        act.wait_ge(act_ready, FILLS * n + k + 1)
                        hidden_high(n, k)
                    high(n + 1, 0)
                    high(n + 1, 1)

                def expert(n, last):
                    e = n - SHARED
                    t0 = 1 + QS * e
                    step.restart()
                    step(act.activation(b1_now[:], b1[:, bass.ds(e, 1), :].rearrange("p e c -> p (e c)"), ACT.Copy))
                    high(n, 2)
                    for k in range(FILLS):
                        act.wait_ge(act_ready, FILLS * n + k + 1)
                        act.wait_ge(hid_lo, FILLS * n + max(k - 1, 0))
                        step(act.activation(act_out[k % 2][:], scaled[k % 2][:], ACT.Silu,
                                            bias=b1_now[:, k % C:k % C + 1]))
                        hidden_high(n, k)
                        if k - 1 in SCALE_AT:
                            magnitude(t0 + SCALE_AT.index(k - 1))
                    tile_out(t0, 0)
                    if not last:
                        high(n + 1, 0)
                    magnitude(t0 + 2)
                    tile_out(t0 + 1, 1)
                    if not last:
                        high(n + 1, 1)
                    magnitude(t0 + 3, last)
                    tile_out(t0 + 2, 2)
                    tile_out(t0 + 3, 3)

                load_tile(0)
                for c in range(C):
                    act.activation(xn[0][:, c, :], XN3T[:, c, :], ACT.Copy).then_inc(xn_hi, 1)
                    if c == 0:
                        high(0, 0)
                high(0, 1)
                act.wait_ge(c_in, 64)
                for n in range(SHARED):
                    shared(n)
                with act.Fori(SHARED, PASSES - 1) as n:
                    expert(n, False)
                expert(PASSES - 1, True)
                act.wait_ge(q_out, 16 * FFN_TILES)

            @block.gpsimd
            def _(pool):
                def low(n, m):
                    pool.wait_ge(w_hi[m], n + 1)
                    pool.tensor_tensor(w[m][1][:], raw[:], cast(w[m][0][:]), ALU.subtract).then_inc(w_lo[m], 1)

                def hidden_low(n, k):
                    pool.wait_ge(hid_hi, FILLS * n + k + 1)
                    pool.tensor_tensor(hid[1][:, k % C, ks(k)], act_out[k % 2][:], cast(hid[0][:, k % C, ks(k)]),
                                       ALU.subtract).then_inc(hid_lo, 1)

                def shared(n):
                    low(n, 2)
                    for k in range(FILLS):
                        hidden_low(n, k)
                    low(n + 1, 0)
                    low(n + 1, 1)

                def expert(n, last):
                    e = n - SHARED
                    low(n, 2)
                    for k in range(FILLS):
                        hidden_low(n, k)
                    if not last:
                        low(n + 1, 0)
                        low(n + 1, 1)
                    for k in range(FILLS):
                        pool.wait_ge(free[2], FILLS * n + k + 1)
                        y = Y[:, k % C, ks(k)]
                        pool.tensor_tensor(y, y, scaled[k % 2][:], ALU.add).then_inc(y_added, 1)

                low(0, 0)
                for c in range(C):
                    pool.wait_ge(xn_hi, c + 1)
                    pool.tensor_tensor(xn[1][:, c, :], XN3T[:, c, :], cast(xn[0][:, c, :]), ALU.subtract).then_inc(xn_lo, 1)
                low(0, 1)
                for n in range(SHARED):
                    shared(n)
                with pool.Fori(SHARED, PASSES - 1) as n:
                    expert(n, False)
                expert(PASSES - 1, True)

            @block.vector
            def _(dve):
                step = Steps(dve, v_steps)

                def tile_scaled(t):
                    dve.wait_ge(q_in, 16 * t + 16)
                    dve.wait_ge(q_mag_ready, t)
                    quant_scaled(dve, step, q_raw[:], D, q_scale[:], q_inv[:], q_y[:]).then_inc(q_y_ready, 1)

                def tile_rounded(t):
                    dve.wait_ge(q_mag_ready, t + 1)
                    dve.wait_ge(q_turned, t)
                    quant_rounded(dve, step, q_mag[:], q_sign[:], q_low[:], q_high[:], q_scale[:], D, q_val[:])\
                        .then_inc(q_val_ready, 1)

                def shared(n):
                    if n == SHARED - 1:
                        tile_scaled(0)
                        tile_rounded(0)
                    for k in range(FILLS):
                        dve.wait_ge(full[1], FILLS * n + k + 1)
                        dve.wait_ge(free[0], FILLS * n + k + 1)
                        dve.wait_ge(hid_lo, FILLS * n + max(k - 1, 0))
                        step(dve.tensor_tensor(act_out[k % 2][:], bank[k][:], gated[:, k, :], ALU.mult))
                        dve.sem_inc(act_ready, 1)
                        dve.sem_inc(free[1], 1)
                    for k in range(FILLS):
                        dve.wait_ge(full[2], FILLS * n + k + 1)
                        y = Y[:, k % C, ks(k)]
                        if n == 0:
                            dve.wait_ge(xn_lo, C)
                            dve.tensor_copy(y, bank[k][:]).then_inc(free[2], 1)
                        else:
                            dve.tensor_tensor(y, y, bank[k][:], ALU.add).then_inc(free[2], 1)

                def quantise(t0, f):
                    if f in SCALE_AT:
                        tile_scaled(t0 + SCALE_AT.index(f))
                    if f in ROUND_AT:
                        tile_rounded(t0 + ROUND_AT.index(f))

                def expert(n):
                    e = n - SHARED
                    t0 = 1 + QS * e
                    step.restart()
                    dve.wait_ge(row_in, 16 * e + 16)
                    step(dve.tensor_scalar(mask[:], wrow[:], 0.0, None, ALU.is_ge))
                    step(dve.tensor_scalar(weight[:], wrow[:], 0.0, None, ALU.max))
                    dve.sem_inc(row_used, 1)
                    for k in range(FILLS):
                        dve.wait_ge(full[0], FILLS * n + k + 1)
                        if k >= 2:
                            dve.wait_ge(hid_hi, FILLS * n + k - 1)
                        else:
                            dve.wait_ge(y_added, FILLS * e)
                        step(dve.tensor_tensor(scaled[k % 2][:], bank[k][:], weight[:, ks(k)], ALU.mult))
                        dve.sem_inc(act_ready, 1)
                        dve.sem_inc(free[0], 1)
                        quantise(t0, k)
                    for k in range(FILLS):
                        dve.wait_ge(full[1], FILLS * n + k + 1)
                        g = gated[:, k, :]
                        dve.tensor_tensor(g, bank[k][:], weight[:, ks(k)], ALU.mult).then_inc(free[1], 1)
                        dve.wait_ge(free[1], FILLS * n + k + 1)
                        step(dve.scalar_tensor_tensor(out=g, in0=g,
                                                      scalar=b3[:, bass.ds(e, 1), k % C:k % C + 1].rearrange("p e c -> p (e c)"),
                                                      in1=mask[:, ks(k)], op0=ALU.add, op1=ALU.mult))
                        quantise(t0, 1 * FILLS + k)
                    for k in range(FILLS):
                        dve.wait_ge(full[2], FILLS * n + k + 1)
                        if k >= 2:
                            dve.wait_ge(y_added, FILLS * e + k - 1)
                        else:
                            dve.wait_ge(hid_hi, FILLS * n + FILLS)
                        dve.scalar_tensor_tensor(out=scaled[k % 2][:], in0=bank[k][:],
                                                 scalar=b2[:, bass.ds(e, 1), k % C:k % C + 1].rearrange("p e c -> p (e c)"),
                                                 in1=gated[:, k, :], op0=ALU.add, op1=ALU.mult).then_inc(free[2], 1)
                        quantise(t0, 2 * FILLS + k)

                dve.wait_ge(c_in, 64)
                for n in range(SHARED):
                    shared(n)
                with dve.Fori(SHARED, PASSES) as n:
                    expert(n)
                for t in range(TILES):
                    dve.wait_ge(turned, t + 1)
                    dve.tensor_tensor(X[:, t, :], X[:, t, :], bank[t][:], ALU.add).then_inc(x_added, 1)



FILLS_C = ["xT4", "q", "g", "s", "pT", "o", "oT", "v", "z", "xT5", "qkv", "s2", "pT2", "zT", "z2"]
NC = len(FILLS_C)
PAIRS = TILES // 2
HIDDEN = -1e38


def phase_c(nc, A, X):
    with ExitStack() as ctx:
        sb = lambda n, s, d=F32: ctx.enter_context(nc.sbuf_tensor("pc_" + n, s, d))
        two = lambda n, s, d=F32: [sb(f"{n}{r}", s, d) for r in range(2)]
        sem = lambda n: ctx.enter_context(nc.semaphore("c_" + n))
        sems = lambda n: [sem(f"{n}{r}") for r in range(2)]
        wq, wk, wv, wo = (sb(n, [P, C, D]) for n in ("wq", "wk", "wv", "wo"))
        bq, bk, bv = (sb(n, [P, C]) for n in ("bq", "bk", "bv"))
        bo, bo2 = sb("bo", [P, D]), sb("bo2", [P, D])
        ident = sb("ident", [P, P])
        aq, ak, av = (sb(n, [P, C, HK]) for n in ("aq", "ak", "av"))
        ao = sb("ao", [HK, D])
        aqk_b = sb("aqk_b", [HK, 2])
        av_b = sb("av_b", [HK, 1])
        causal = sb("causal", [P, P])
        own_batch = sb("own_batch", [P, TILES, B])
        ctx_tail = sb("ctx_tail", [B, D])
        ctxT = two("ctxT", [P, BT, C, LK])
        keys = two("keys", [P, BT, KH, D])
        mask = two("mask", [P, LK], I32)
        hidden = two("hidden", [P, LK])
        stats, mv, veps, rstd = two("stats", [P, 6]), two("mv", [P, 2]), two("veps", [P, 1]), two("rstd", [P, 1])
        xn, xnT = two("xn", [P, D]), two("xnT", [P, C, P])
        qT, gT = two("qT", [P, C, P]), two("gT", [P, C, P])
        krow = two("krow", [P, 1])
        logit, prob = two("logit", [P, LK]), two("prob", [P, LK])
        nmax, total, inv = two("nmax", [P, 1]), two("total", [P, 1]), two("inv", [P, 1])
        pn = two("pn", [P, KH * P + B])
        pT, pTtail = two("pT", [P, KH * P]), two("pTtail", [B, P])
        o, oT, vT = two("o", [P, D]), two("oT", [P, C, P]), two("vT", [P, C, P])
        qk, va = two("qk", [HK, 2, P]), two("va", [P, HK])
        zT = two("zT", [HK, P])
        eps, mhalf = sb("eps", [P, 1]), sb("mhalf", [P, 1])
        fence = two("fence", [P, 1])
        bank = [ctx.enter_context(nc.psum_tensor(f"pc{b}", [P, 512], F32)) for b in range(2)]

        w_in = sem("w_in")
        init = sem("init")
        ctx_in = sems("ctx_in")
        mv_ready, rstd_ready, xn_ready = sems("mv"), sems("rstd"), sems("xn")
        full, freed = sems("full"), sems("freed")
        l_ready, p_ready, pn_ready = sems("l"), sems("p"), sems("pn")
        v_steps, s_steps, p_steps = sem("vsteps"), sem("ssteps"), sem("psteps")

        scale = float(D) ** -0.5
        scale2 = float(HK) ** -0.5
        consts = [(wq, "l1_wq"), (wk, "l1_wk"), (wv, "l1_wv"), (wo, "l1_wo"), (bq, "l1_bq"), (bk, "l1_bk"),
                  (bv, "l1_bv"), (bo, "l1_bo"), (bo2, "s_bo"), (ident, "ident"), (aq, "s_wq"), (ak, "s_wk"),
                  (av, "s_wv"), (ao, "s_wo"), (aqk_b, "s_bqk"), (av_b, "s_bv"), (causal, "causal"),
                  (own_batch, "own_batch"), (ctx_tail, "ctx_tail_rows")]

        def turn(i, name):
            return NC * i + FILLS_C.index(name)

        with nc.Block() as block:

            @block.sync
            def _(sp):
                def load(i, r):
                    t = 2 * i + r
                    sp.dma_start(ctxT[r][:], A["ctxT"][bass.ds(BT * t, BT)].rearrange("j p c k -> p j c k"))\
                      .then_inc(ctx_in[r], 16)
                    for j in range(BT):
                        sp.dma_start(keys[r][:, j], A["ctx"][bass.ds(BT * t + j, 1), 0:KH * P, :]
                                     .rearrange("o (h p) d -> p (o h) d", p=P)).then_inc(ctx_in[r], 16)
                    sp.dma_start(mask[r][:], A["mask"][bass.ds(t, 1)].rearrange("o p k -> (o p) k")).then_inc(ctx_in[r], 16)

                for n, (dst, name) in enumerate(consts):
                    sp.dma_start(dst[:], A[name]).then_inc(w_in, 16)
                    if n == 1:
                        load(0, 0)
                        load(0, 1)
                with sp.Fori(1, PAIRS) as i:
                    for r in range(2):
                        sp.wait_ge(freed[r], NC * (i - 1) + FILLS_C.index("o") + 1)
                        load(i, r)

            @block.tensor
            def _(pe):
                def take(i, r, name):
                    pe.wait_ge(freed[r], turn(i, name))

                def transposes(i, r, name, src):
                    take(i, r, name)
                    for c in range(C):
                        tr = pe.transpose(bank[r][:, c * P:(c + 1) * P], src[:, c * P:(c + 1) * P], ident[:])
                    tr.then_inc(full[r], 1)

                def narrow(i, r, name, w, src):
                    take(i, r, name)
                    for n in range(C):
                        for c in range(C):
                            mm = pe.matmul(bank[r][:, n * P:(n + 1) * P], w[:, c, n * P:(n + 1) * P], src[:, c, :],
                                           start=c == 0, stop=c == C - 1)
                    mm.then_inc(full[r], 1)

                def stage(name, i, r):
                    ps = bank[r]
                    if name == "xT4":
                        pe.wait_ge(xn_ready[r], 2 * i + 1)
                        transposes(i, r, name, xn[r])
                    if name == "q":
                        narrow(i, r, name, wq, xnT[r])
                    if name == "g":
                        narrow(i, r, name, wk, qT[r])
                    if name == "s":
                        take(i, r, name)
                        pe.wait_ge(ctx_in[r], 16 * (BT + 2) * i + 16 * (BT + 2))
                        for c in range(C):
                            pe.matmul(ps[:, 300:301], qT[r][:, c, :], bk[:, c:c + 1], start=c == 0, stop=c == C - 1)
                        for c in range(C):
                            for j in range(BT):
                                mm = pe.matmul(ps[j * LQ:(j + 1) * LQ, 0:LK], gT[r][:, c, j * LQ:(j + 1) * LQ],
                                               ctxT[r][:, j, c, :], start=c == 0, stop=c == C - 1,
                                               tile_position=(0, j * LQ))
                        mm.then_inc(full[r], 1)
                    if name == "pT":
                        pe.wait_ge(pn_ready[r], 2 * i + 1)
                        take(i, r, name)
                        pe.transpose(ps[:, 0:P], pn[r][:, 0:P], ident[:])
                        pe.transpose(ps[:, P:2 * P], pn[r][:, P:2 * P], ident[:])
                        pe.transpose(ps[0:B, 2 * P:3 * P], pn[r][:, 2 * P:], ident[:]).then_inc(full[r], 1)
                    if name == "o":
                        take(i, r, name)
                        pe.matmul(ps[:], pTtail[r][:], ctx_tail[:], start=True, stop=False, skip_group_check=True)
                        for h in range(KH):
                            for j in range(BT):
                                mm = pe.matmul(ps[j * LQ:(j + 1) * LQ, :], pT[r][:, h * P + j * LQ:h * P + (j + 1) * LQ],
                                               keys[r][:, j, h, :], start=False, stop=h == KH - 1,
                                               tile_position=(0, j * LQ), skip_group_check=True)
                        mm.then_inc(full[r], 1)
                    if name == "oT":
                        transposes(i, r, name, o[r])
                    if name == "v":
                        narrow(i, r, name, wv, oT[r])
                    if name == "z":
                        take(i, r, name)
                        for c in range(C):
                            mm = pe.matmul(ps[:], vT[r][:, c, :], wo[:, c, :], start=c == 0, stop=c == C - 1)
                        mm.then_inc(full[r], 1)
                    if name == "xT5":
                        pe.wait_ge(xn_ready[r], 2 * i + 2)
                        transposes(i, r, name, xn[r])
                    if name == "qkv":
                        take(i, r, name)
                        for w, col in ((aq, 0), (ak, P)):
                            for c in range(C):
                                pe.matmul(ps[0:HK, col:col + P], w[:, c, :], xnT[r][:, c, :], start=c == 0, stop=c == C - 1)
                        for c in range(C):
                            mm = pe.matmul(ps[:, 2 * P:2 * P + HK], xnT[r][:, c, :], av[:, c, :], start=c == 0, stop=c == C - 1)
                        mm.then_inc(full[r], 1)
                    if name == "s2":
                        take(i, r, name)
                        pe.matmul(ps[:, 0:P], qk[r][:, 0, :], qk[r][:, 1, :], start=True, stop=True).then_inc(full[r], 1)
                    if name == "pT2":
                        pe.wait_ge(pn_ready[r], 2 * i + 2)
                        take(i, r, name)
                        pe.transpose(ps[:, 0:P], pn[r][:, 0:P], ident[:]).then_inc(full[r], 1)
                    if name == "zT":
                        take(i, r, name)
                        pe.matmul(ps[0:HK, 0:P], va[r][:], pT[r][:, 0:P], start=True, stop=True).then_inc(full[r], 1)
                    if name == "z2":
                        take(i, r, name)
                        pe.matmul(ps[:], zT[r][:], ao[:], start=True, stop=True).then_inc(full[r], 1)

                pe.wait_ge(w_in, 16 * len(consts))
                with pe.Fori(0, PAIRS) as i:
                    for name in FILLS_C:
                        for r in range(2):
                            stage(name, i, r)

            @block.scalar
            def _(act):
                def stage(name, i, r):
                    ps = bank[r]
                    if name == "g":
                        act.wait_ge(full[r], turn(i, name) + 1)
                        act.activation(gT[r][:].rearrange("p c t -> p (c t)"), ps[:], ACT.Copy, scale=scale).then_inc(freed[r], 1)
                    if name == "s":
                        act.wait_ge(l_ready[r], 2 * i + 1)
                        act.activation(prob[r][:], logit[r][:], ACT.Exp, bias=nmax[r][:],
                                       accum_out=total[r][:]).then_inc(p_ready[r], 1)
                    if name == "pT":
                        act.wait_ge(full[r], turn(i, name) + 1)
                        act.activation(pT[r][:], ps[:, 0:KH * P], ACT.Copy)
                        act.activation(pTtail[r][:], ps[0:B, KH * P:KH * P + P], ACT.Copy).then_inc(freed[r], 1)
                    if name == "o":
                        act.wait_ge(full[r], turn(i, name) + 1)
                        act.activation(o[r][:], ps[:], ACT.Copy).then_inc(freed[r], 1)
                    if name == "s2":
                        act.wait_ge(l_ready[r], 2 * i + 2)
                        act.activation(prob[r][:, 0:P], logit[r][:, 0:P], ACT.Exp, bias=nmax[r][:],
                                       accum_out=total[r][:]).then_inc(p_ready[r], 1)
                    if name == "pT2":
                        act.wait_ge(full[r], turn(i, name) + 1)
                        act.activation(pT[r][:, 0:P], ps[:, 0:P], ACT.Copy).then_inc(freed[r], 1)

                with act.Fori(0, PAIRS) as i:
                    for name in FILLS_C:
                        for r in range(2):
                            stage(name, i, r)

            @block.gpsimd
            def _(pool):
                step = Steps(pool, p_steps)

                def inverse_deviation(n, r):
                    pool.wait_ge(mv_ready[r], n + 1)
                    step(pool.tensor_tensor(veps[r][:], mv[r][:, 1:2], eps[:], ALU.add))
                    pool.tensor_tensor(rstd[r][:], veps[r][:], mhalf[:], ALU.pow).then_inc(rstd_ready[r], 1)

                pool.wait_ge(init, 2)
                with pool.Fori(0, PAIRS) as i:
                    step.restart()
                    for n in range(2):
                        for r in range(2):
                            inverse_deviation(2 * i + n, r)

            @block.vector
            def _(dve):
                step = Steps(dve, v_steps)

                def tile_of_x(i, r):
                    return X[:, bass.ds(2 * i + r, 1), :].rearrange("p o d -> p (o d)")

                def filled(i, r, name):
                    dve.wait_ge(full[r], turn(i, name) + 1)

                def statistics(i, r):
                    step(dve.memset(fence[r][:], 0.0))
                    step(dve.bn_stats(stats[r][:], tile_of_x(i, r)))
                    dve.bn_aggr(mv[r][:], stats[r][:]).then_inc(mv_ready[r], 1)

                def normalise(i, r, n):
                    dve.wait_ge(rstd_ready[r], 2 * i + n + 1)
                    dve.tensor_scalar(xn[r][:], tile_of_x(i, r), mv[r][:, 0:1], rstd[r][:],
                                      ALU.subtract, ALU.mult).then_inc(xn_ready[r], 1)

                def add_product(i, r, name, bias):
                    filled(i, r, name)
                    x = tile_of_x(i, r)
                    dve.tensor_tensor(x, ps_of(r), x, ALU.add).then_inc(freed[r], 1)
                    dve.wait_ge(freed[r], turn(i, name) + 1)
                    step(dve.tensor_tensor(x, x, bias[:], ALU.add))

                def ps_of(r):
                    return bank[r][:]

                def chunks(ap):
                    return ap.rearrange("p (c t) -> p c t", c=C)

                def per_chunk(b):
                    return b[:].rearrange("p (c o) -> p c o", o=1).to_broadcast([P, C, P])

                def stage(name, i, r):
                    ps = bank[r]
                    if name == "hide":
                        dve.wait_ge(ctx_in[r], 16 * (BT + 2) * i + 16 * (BT + 2))
                        step(dve.tensor_scalar(hidden[r][:], mask[r][:], 0.0, HIDDEN, ALU.is_equal, ALU.mult))
                    if name in ("xT4", "xT5"):
                        filled(i, r, name)
                        dve.tensor_copy(xnT[r][:].rearrange("p c t -> p (c t)"), ps[:]).then_inc(freed[r], 1)
                    if name == "q":
                        filled(i, r, name)
                        dve.tensor_tensor(qT[r][:], chunks(ps[:]), per_chunk(bq), ALU.add).then_inc(freed[r], 1)
                    if name == "s":
                        filled(i, r, name)
                        step(dve.tensor_scalar(krow[r][:], ps[:, 300:301], scale, None, ALU.mult))
                        dve.scalar_tensor_tensor(out=logit[r][:], in0=ps[:, 0:LK], scalar=krow[r][:], in1=hidden[r][:],
                                                 op0=ALU.add, op1=ALU.add).then_inc(freed[r], 1)
                        dve.wait_ge(freed[r], turn(i, name) + 1)
                        dve.tensor_reduce(nmax[r][:], logit[r][:], AX.X, ALU.max, negate=True).then_inc(l_ready[r], 1)
                    if name == "norm":
                        dve.wait_ge(p_ready[r], 2 * i + 1)
                        step(dve.scalar_tensor_tensor(out=total[r][:], in0=nmax[r][:], scalar=-HIDDEN / 10,
                                                      in1=total[r][:], op0=ALU.is_lt, op1=ALU.mult))
                        step(dve.reciprocal(inv[r][:], total[r][:]))
                        step(dve.tensor_scalar(pn[r][:, KH * P:], own_batch[:, bass.ds(2 * i + r, 1), :].rearrange("p o b -> p (o b)"),
                                               prob[r][:, KH * P:LK], inv[r][:], ALU.mult, ALU.mult))
                        dve.tensor_scalar(pn[r][:, 0:KH * P], prob[r][:, 0:KH * P], inv[r][:], None, ALU.mult)\
                           .then_inc(pn_ready[r], 1)
                    if name == "oT":
                        filled(i, r, name)
                        dve.tensor_copy(oT[r][:].rearrange("p c t -> p (c t)"), ps[:]).then_inc(freed[r], 1)
                    if name == "v":
                        filled(i, r, name)
                        dve.tensor_tensor(vT[r][:], chunks(ps[:]), per_chunk(bv), ALU.add).then_inc(freed[r], 1)
                    if name == "z":
                        add_product(i, r, name, bo)
                        statistics(i, r)
                    if name == "qkv":
                        filled(i, r, name)
                        step(dve.tensor_tensor(qk[r][:], ps[0:HK, 0:2 * P].rearrange("p (n t) -> p n t", n=2),
                                               aqk_b[:].rearrange("p (n o) -> p n o", o=1).to_broadcast([HK, 2, P]), ALU.add))
                        dve.tensor_copy(va[r][:], ps[:, 2 * P:2 * P + HK]).then_inc(freed[r], 1)
                    if name == "s2":
                        filled(i, r, name)
                        dve.scalar_tensor_tensor(out=logit[r][:, 0:P], in0=ps[:, 0:P], scalar=scale2, in1=causal[:],
                                                 op0=ALU.mult, op1=ALU.add).then_inc(freed[r], 1)
                        dve.wait_ge(freed[r], turn(i, name) + 1)
                        dve.tensor_reduce(nmax[r][:], logit[r][:, 0:P], AX.X, ALU.max, negate=True).then_inc(l_ready[r], 1)
                    if name == "norm2":
                        dve.wait_ge(p_ready[r], 2 * i + 2)
                        step(dve.reciprocal(inv[r][:], total[r][:]))
                        dve.tensor_scalar(pn[r][:, 0:P], prob[r][:, 0:P], inv[r][:], None, ALU.mult).then_inc(pn_ready[r], 1)
                    if name == "zT":
                        filled(i, r, name)
                        dve.tensor_scalar(zT[r][:], ps[0:HK, 0:P], av_b[:], None, ALU.add).then_inc(freed[r], 1)
                    if name == "z2":
                        add_product(i, r, name, bo2)

                dve.memset(eps[:], 1e-5).then_inc(init, 1)
                dve.memset(mhalf[:], -0.5).then_inc(init, 1)
                dve.wait_ge(w_in, 16 * len(consts))
                with dve.Fori(0, PAIRS) as i:
                    step.restart()
                    for r in range(2):
                        statistics(i, r)
                    for r in range(2):
                        normalise(i, r, 0)
                    for name in ("xT4", "hide", "q", "s", "norm", "oT", "v", "z"):
                        for r in range(2):
                            stage(name, i, r)
                    for r in range(2):
                        normalise(i, r, 1)
                    for name in ("xT5", "qkv", "s2", "norm2", "zT", "z2"):
                        for r in range(2):
                            stage(name, i, r)



PIECES = 4
PW = FF // PIECES
FILLS_T = [list(range(f, min(f + 4, FC))) for f in range(0, FC, 4)]
NF = len(FILLS_T)


def phase_d(nc, A, X, XN3T, q_dram, out):
    with ExitStack() as ctx:
        sb = lambda n, s, d=F32: ctx.enter_context(nc.sbuf_tensor("pd_" + n, s, d))
        sem = lambda n: ctx.enter_context(nc.semaphore("d_" + n))
        wgu = [sb("wgu_hi", [P, 2, C, FF], F32R), sb("wgu_lo", [P, 2, C, FF], F32R)]
        wd = [sb("wd_hi", [P, FC, D], F32R), sb("wd_lo", [P, FC, D], F32R)]
        hT_both = sb("hT", [P, 2, FC, P], F32R)
        hT = [hT_both[:, s] for s in range(2)]
        raw = [sb("raw", [P, 3, D])[:],
               hT_both[:].rearrange("p s k t -> p (s k t)")[:, 0:3 * D].rearrange("p (m d) -> p m d", m=3)]
        xT = [sb("xT_hi", [P, C, P], F32R), sb("xT_lo", [P, C, P], F32R)]
        flat = XN3T[:].rearrange("p c t -> p (c t)")
        h, hy = flat[:, 0:FF], flat[:, FF:2 * FF]
        xn, xy = flat[:, 2 * FF:2 * FF + D], flat[:, 2 * FF + D:2 * FF + 2 * D]
        hsign, low, high = (sb(n, [P, FF], BF16) for n in ("hsign", "low", "high"))
        xsign = sb("xsign", [P, D], BF16)
        hscale, hinv = sb("hscale", [P, FF // BLK]), sb("hinv", [P, FF // BLK])
        xscale, xinv = sb("xscale", [P, D // BLK]), sb("xinv", [P, D // BLK])
        silu = [sb(f"silu{r}", [P, PW]) for r in range(2)]
        ident = sb("ident", [P, P])
        stats, mv, veps, rstd = sb("stats", [P, 6]), sb("mv", [P, 2]), sb("veps", [P, 1]), sb("rstd", [P, 1])
        eps, mhalf, fence = sb("eps", [P, 1]), sb("mhalf", [P, 1]), sb("fence", [P, 1])
        bank = [ctx.enter_context(nc.psum_tensor(f"pd{b}", [P, 512], F32)) for b in range(8)]
        g_ps, u_ps, ht_ps, xt_ps, d_ps = bank[0:2], bank[2:4], bank[4:6], bank[6], bank[7]

        c_in, init = sem("c_in"), sem("init")
        raw_in = [sem(f"raw_in{r}") for r in range(2)]
        w_hi, g_lo, w_lo = sem("w_hi"), sem("g_lo"), sem("w_lo")
        mv_ready, rstd_ready = sem("mv"), sem("rstd")
        xy_ready, xmag_ready, xval_ready = sem("xy"), sem("xmag"), sem("xval")
        xt_full, xt_hi, xt_lo = sem("xt_full"), sem("xt_hi"), sem("xt_lo")
        g_full, u_full, silu_ready, h_piece = sem("g_full"), sem("u_full"), sem("silu"), sem("h_piece")
        hy_ready, hmag_ready, hval_ready = sem("hy"), sem("hmag"), sem("hval")
        ht_full, ht_hi, ht_lo = sem("ht_full"), sem("ht_hi"), sem("ht_lo")
        d_full, x_done, x_out = sem("d_full"), sem("x_done"), sem("x_out")
        v_steps, p_steps = sem("vsteps"), sem("psteps")

        def all_steps(eng, body):
            body(0, True, True, False)
            with eng.Fori(1, TILES - 1) as i:
                body(i, True, True, True)
            body(TILES - 1, False, True, True)
            body(TILES, False, False, True)

        def all_chunks(eng, body):
            body(0, 0)
            with eng.Fori(0, FC // 2) as b:
                body(2 * b + 1, 1)
                body(2 * b + 2, 0)

        with nc.Block() as block:

            @block.sync
            def _(sp):
                def load(a, r):
                    if not (isinstance(a, int) and a == 0):
                        sp.wait_ge(g_lo, a - 1)
                        sp.wait_ge(w_lo, a - 1)
                    sp.dma_start(raw[r] if r == 0 else cast(raw[r]),
                                 q_dram[bass.ds(3 * a, 3)].rearrange("m p d -> p m d")).then_inc(raw_in[r], 16)

                sp.dma_start(ident[:], A["ident"]).then_inc(c_in, 16)
                all_chunks(sp, load)
                with sp.Fori(0, TILES) as t:
                    sp.wait_ge(x_done, t + 1)
                    sp.dma_start(out[bass.ds(t, 1)].rearrange("o p d -> (o p) d"),
                                 X[:, bass.ds(t, 1), :].rearrange("p o d -> p (o d)")).then_inc(x_out, 16)
                sp.wait_ge(x_out, 16 * TILES)

            @block.tensor
            def _(pe):
                def gate_up(i, p):
                    n = PIECES * i + p
                    if p == 0:
                        pe.wait_ge(xt_lo, i + 1)
                    if isinstance(i, int) and i == 0:
                        need = -(-PW * (p + 1) // P)
                        pe.wait_ge(g_lo, need)
                        pe.wait_ge(w_lo, need)
                    cols = slice(p * PW, (p + 1) * PW)
                    for m, ps, full, free in ((0, g_ps, g_full, silu_ready), (1, u_ps, u_full, h_piece)):
                        pe.wait_ge(free, n if p == 0 else n - 1)
                        for c in range(C):
                            mm = product3(pe, ps[p % 2][:, 0:PW], [x[:, c, :] for x in xT],
                                          [w[:, m, c, cols] for w in wgu], c == 0, c == C - 1)
                        mm.then_inc(full, 1)

                def hidden_transposed(i):
                    pe.wait_ge(hval_ready, i + 1)
                    for f, chunks in enumerate(FILLS_T):
                        n = NF * i + f
                        pe.wait_ge(ht_lo, n if f == 0 else n - 1)
                        for s, k in enumerate(chunks):
                            tr = pe.transpose(ht_ps[f % 2][:, s * P:(s + 1) * P], hy[:, k * P:(k + 1) * P], ident[:])
                        tr.then_inc(ht_full, 1)

                def down(i):
                    pe.wait_ge(ht_lo, NF * i + NF)
                    pe.wait_ge(x_done, i)
                    for k in range(FC):
                        mm = product3(pe, d_ps[:], [x[:, k, :] for x in hT], [w[:, k, :] for w in wd], k == 0, k == FC - 1)
                    mm.then_inc(d_full, 1)

                def tokens_transposed(i):
                    pe.wait_ge(xval_ready, i + 1)
                    pe.wait_ge(xt_lo, i)
                    for c in range(C):
                        tr = pe.transpose(xt_ps[:, c * P:(c + 1) * P], xy[:, c * P:(c + 1) * P], ident[:])
                    tr.then_inc(xt_full, 1)

                def step_of(i, nxt, cur, prev):
                    if cur:
                        gate_up(i, 0)
                        gate_up(i, 1)
                    if prev:
                        hidden_transposed(i - 1)
                    if cur:
                        gate_up(i, 2)
                        gate_up(i, 3)
                    if prev:
                        down(i - 1)
                    if nxt:
                        tokens_transposed(i + 1)

                pe.wait_ge(c_in, 16)
                tokens_transposed(0)
                all_steps(pe, step_of)

            @block.scalar
            def _(act):
                def chunk(a, count, r):
                    src = raw[0] if r == 0 else cast(raw[1])
                    act.wait_ge(raw_in[r], 16 * count)
                    act.activation(wgu[0][:, :, :, bass.ds(P * a, P)], src[:, 0:2, :].rearrange("p m (c o) -> p m c o", c=C),
                                   ACT.Copy)
                    act.activation(wd[0][:, bass.ds(a, 1), :].rearrange("p o d -> p (o d)"), src[:, 2, :], ACT.Copy)\
                       .then_inc(w_hi, 1)

                def magnitudes(i, y_ready, y, sign, mag, mag_ready):
                    act.wait_ge(y_ready, i + 1)
                    act.activation(sign, y, ACT.Sign)
                    act.activation(mag, y, ACT.Abs).then_inc(mag_ready, 1)

                def x_magnitudes(i):
                    magnitudes(i, xy_ready, xy, xsign[:], xn, xmag_ready)

                def silu_of(i, p):
                    n = PIECES * i + p
                    act.wait_ge(g_full, n + 1)
                    act.wait_ge(h_piece, n if p == 0 else n - 1)
                    act.activation(silu[p % 2][:], g_ps[p % 2][:, 0:PW], ACT.Silu).then_inc(silu_ready, 1)

                def tokens_high(i):
                    act.wait_ge(xt_full, i + 1)
                    act.wait_ge(u_full, PIECES * i)
                    act.activation(xT[0][:].rearrange("p c t -> p (c t)"), xt_ps[:], ACT.Copy).then_inc(xt_hi, 1)

                def hidden_high(i):
                    act.wait_ge(d_full, i)
                    act.wait_ge(g_lo, FC)
                    act.wait_ge(w_lo, FC)
                    for f, chunks in enumerate(FILLS_T):
                        act.wait_ge(ht_full, NF * i + f + 1)
                        act.activation(hT[0][:, chunks[0]:chunks[-1] + 1, :].rearrange("p k t -> p (k t)"),
                                       ht_ps[f % 2][:, 0:P * len(chunks)], ACT.Copy).then_inc(ht_hi, 1)

                def step_of(i, nxt, cur, prev):
                    if cur:
                        silu_of(i, 0)
                        silu_of(i, 1)
                    if prev:
                        hidden_high(i - 1)
                    if nxt:
                        x_magnitudes(i + 1)
                    if cur:
                        silu_of(i, 2)
                        silu_of(i, 3)
                        magnitudes(i, hy_ready, hy, hsign[:], h, hmag_ready)
                    if nxt:
                        tokens_high(i + 1)

                x_magnitudes(0)
                tokens_high(0)
                chunk(0, 1, 0)
                with act.Fori(0, FC // 2) as b:
                    chunk(2 * b + 1, b + 1, 1)
                    chunk(2 * b + 2, b + 2, 0)
                all_steps(act, step_of)

            @block.gpsimd
            def _(pool):
                step = Steps(pool, p_steps)

                def inverse_deviation(i):
                    pool.wait_ge(mv_ready, i + 1)
                    step(pool.tensor_tensor(veps[:], mv[:, 1:2], eps[:], ALU.add))
                    pool.tensor_tensor(rstd[:], veps[:], mhalf[:], ALU.pow).then_inc(rstd_ready, 1)

                def split_low(a, r):
                    src = raw[0] if r == 0 else cast(raw[1])
                    pool.wait_ge(w_hi, a + 1)
                    pool.tensor_tensor(wgu[1][:, 1, :, bass.ds(P * a, P)], src[:, 1, :].rearrange("p (c o) -> p c o", c=C),
                                       cast(wgu[0][:, 1, :, bass.ds(P * a, P)]), ALU.subtract)
                    pool.tensor_tensor(wd[1][:, bass.ds(a, 1), :].rearrange("p o d -> p (o d)"), src[:, 2, :],
                                       cast(wd[0][:, bass.ds(a, 1), :].rearrange("p o d -> p (o d)")), ALU.subtract)\
                        .then_inc(w_lo, 1)

                pool.wait_ge(init, 2)
                inverse_deviation(0)
                all_chunks(pool, split_low)
                inverse_deviation(1)
                with pool.Fori(2, TILES) as i:
                    step.restart()
                    inverse_deviation(i)

            @block.vector
            def _(dve):
                step = Steps(dve, v_steps)

                def tile_of_x(i):
                    return X[:, bass.ds(i, 1), :].rearrange("p o d -> p (o d)")

                def statistics(i):
                    step(dve.memset(fence[:], 0.0))
                    step(dve.bn_stats(stats[:], tile_of_x(i)))
                    dve.bn_aggr(mv[:], stats[:]).then_inc(mv_ready, 1)

                def tokens_scaled(i):
                    dve.wait_ge(rstd_ready, i + 1)
                    step(dve.tensor_scalar(xn, tile_of_x(i), mv[:, 0:1], rstd[:], ALU.subtract, ALU.mult))
                    quant_scaled(dve, step, xn, D, xscale[:], xinv[:], xy).then_inc(xy_ready, 1)

                def tokens_rounded(i):
                    dve.wait_ge(xmag_ready, i + 1)
                    quant_rounded(dve, step, xn, xsign[:], low[:, 0:D], high[:, 0:D], xscale[:], D, xy).then_inc(xval_ready, 1)

                def tokens_low(i):
                    dve.wait_ge(xt_hi, i + 1)
                    dve.tensor_tensor(xT[1][:].rearrange("p c t -> p (c t)"), xt_ps[:],
                                      cast(xT[0][:].rearrange("p c t -> p (c t)")), ALU.subtract).then_inc(xt_lo, 1)

                def hidden_piece(i, p):
                    n = PIECES * i + p
                    dve.wait_ge(silu_ready, n + 1)
                    dve.wait_ge(u_full, n + 1)
                    dve.tensor_tensor(h[:, p * PW:(p + 1) * PW], u_ps[p % 2][:, 0:PW], silu[p % 2][:], ALU.mult)\
                       .then_inc(h_piece, 1)

                def hidden_scaled(i):
                    dve.wait_ge(h_piece, PIECES * i + PIECES)
                    quant_scaled(dve, step, h, FF, hscale[:], hinv[:], hy).then_inc(hy_ready, 1)

                def hidden_rounded(i):
                    dve.wait_ge(hmag_ready, i + 1)
                    quant_rounded(dve, step, h, hsign[:], low[:], high[:], hscale[:], FF, hy).then_inc(hval_ready, 1)

                def hidden_low(i):
                    for f, chunks in enumerate(FILLS_T):
                        n = NF * i + f
                        ks = slice(chunks[0], chunks[-1] + 1)
                        dve.wait_ge(ht_hi, n + 1)
                        dve.tensor_tensor(hT[1][:, ks, :].rearrange("p k t -> p (k t)"), ht_ps[f % 2][:, 0:P * len(chunks)],
                                          cast(hT[0][:, ks, :].rearrange("p k t -> p (k t)")), ALU.subtract).then_inc(ht_lo, 1)

                def add_product(i):
                    dve.wait_ge(d_full, i + 1)
                    dve.tensor_tensor(tile_of_x(i), tile_of_x(i), d_ps[:], ALU.add).then_inc(x_done, 1)

                def split_low(a, r):
                    src = raw[0] if r == 0 else cast(raw[1])
                    dve.wait_ge(w_hi, a + 1)
                    dve.tensor_tensor(wgu[1][:, 0, :, bass.ds(P * a, P)], src[:, 0, :].rearrange("p (c o) -> p c o", c=C),
                                      cast(wgu[0][:, 0, :, bass.ds(P * a, P)]), ALU.subtract).then_inc(g_lo, 1)

                def step_of(i, nxt, cur, prev):
                    step.restart()
                    if nxt:
                        statistics(i + 1)
                    if cur:
                        hidden_piece(i, 0)
                        hidden_piece(i, 1)
                    if prev:
                        hidden_low(i - 1)
                    if nxt:
                        tokens_scaled(i + 1)
                    if cur:
                        hidden_piece(i, 2)
                        hidden_piece(i, 3)
                        hidden_scaled(i)
                    if nxt:
                        tokens_rounded(i + 1)
                    if prev:
                        add_product(i - 1)
                    if nxt:
                        tokens_low(i + 1)
                    if cur:
                        hidden_rounded(i)

                dve.memset(eps[:], 1e-5).then_inc(init, 1)
                dve.memset(mhalf[:], -0.5).then_inc(init, 1)
                statistics(0)
                tokens_scaled(0)
                tokens_rounded(0)
                tokens_low(0)
                all_chunks(dve, split_low)
                all_steps(dve, step_of)


def laid_out(np_, x):
    c_ = np_.ascontiguousarray
    rows = lambda w: c_(w.reshape(-1, P, w.shape[1]).transpose(1, 0, 2))
    cols = lambda w: rows(w.T)
    wide = lambda v: c_(np_.broadcast_to(v.reshape(1, -1), (P, v.size)))
    tall = lambda v: c_(v.reshape(-1, P).T)
    per = lambda v: c_(v.reshape(E, C, P).transpose(2, 0, 1))
    ctx = x["ctx_1024"]
    eye = np_.eye(P, dtype=np_.float32)
    batch = np_.arange(P) // LQ
    same = batch[:, None] == batch[None, :]
    order = np_.arange(P)[:, None] <= np_.arange(P)[None, :]
    e32 = np_.eye(B, dtype=np_.float32)
    out = {
        "x": c_(x["x"].reshape(TILES, P, D).transpose(1, 0, 2)),
        "ctxT": c_(ctx.reshape(B, LK, C, P).transpose(0, 3, 2, 1)),
        "ctx_tail": c_(ctx[:, LK - 1].reshape(B, C, P).transpose(2, 1, 0)),
        "attn_bias": c_(np_.tile(x["fside_SxS2_0"], (BT, 1))),
        "l0_wq": rows(x["L0_xattn_Wq"]), "l0_wk": rows(x["L0_xattn_Wk"]), "l0_wv": rows(x["L0_xattn_Wv"]),
        "l0_wo": rows(x["L0_xattn_Wo"]), "l0_bq": wide(x["L0_xattn_bq"]), "l0_bo": wide(x["L0_xattn_bo"]),
        "scale_log": wide(x["L0_xattn_scale_mul_log"]),
        "a_wq": cols(x["L0_attn_Wq"]), "a_wk": cols(x["L0_attn_Wk"]), "a_wv": cols(x["L0_attn_Wv"]),
        "a_wo": c_(x["L0_attn_Wo"].T), "gate": cols(x["L0_ffn_gate_w"]),
        "experts": c_(np_.stack([m for n in range(SHARED) for m in (
                        cols(x["L0_ffn_sw1"][n * D:(n + 1) * D]), cols(x["L0_ffn_sw2"][n * D:(n + 1) * D]),
                        cols(x["L0_ffn_sw3"][:, n * D:(n + 1) * D]))]
                        + [cols(x["L0_ffn_" + k][e]) for e in range(E) for k in ("w1", "w3", "w2")])),
        "b1": per(x["L0_ffn_b1"]), "b2": per(x["L0_ffn_b2"]), "b3": per(x["L0_ffn_b3"]),
        "ffn_w": c_(np_.stack([x["L1_ffn_w_gate"].reshape(FC, P, D), x["L1_ffn_w_up"].reshape(FC, P, D),
                               x["L1_ffn_w_down"].reshape(C, P, FC, P).transpose(2, 1, 0, 3).reshape(FC, P, D)], 1)
                     .reshape(FFN_TILES, P, D)),
        "ctx": ctx, "ctx_tail_rows": c_(ctx[:, LK - 1]), "mask": x["mask_BxSxS2_ik0"].reshape(TILES, P, LK),
        "l1_wq": cols(x["L1_xattn_Wq"]), "l1_wk": rows(x["L1_xattn_Wk"]), "l1_wv": cols(x["L1_xattn_Wv"]),
        "l1_wo": cols(x["L1_xattn_Wo"]), "l1_bq": tall(x["L1_xattn_bq"]), "l1_bk": tall(x["L1_xattn_bk"]),
        "l1_bv": tall(x["L1_xattn_bv"]), "l1_bo": wide(x["L1_xattn_bo"]),
        "s_wq": rows(x["L1_attn_wq"]), "s_wk": rows(x["L1_attn_wk"]), "s_wv": rows(x["L1_attn_wv"]),
        "s_wo": x["L1_attn_wo"], "s_bqk": c_(np_.stack([x["L1_attn_bq"], x["L1_attn_bk"]], 1)),
        "s_bv": x["L1_attn_bv"].reshape(HK, 1), "s_bo": wide(x["L1_attn_bo"]),
        "ident": eye,
        "onehot": c_(np_.broadcast_to(e32, (P, B, B))),
        "causal": np_.where(same, np_.where(order.T, 0.0, -1e11), -1e30).astype(np_.float32),
        "own_batch": c_((np_.arange(B)[None, None, :] == (BT * np_.arange(TILES)[None, :, None] + batch[:, None, None]))
                        .astype(np_.float32)),
        "cmaskT": (same & order).astype(np_.float32),
        "lower": c_(np_.broadcast_to(np_.tril(np_.ones((E, E), np_.float32), -1), (P, E, E))),
    }
    return out


def program(nc, A, out):
    w_dram = nc.dram_tensor("router_weights", [E, T], F32, kind="Internal").ap()
    q_dram = nc.dram_tensor("quantised", [FFN_TILES, P, D], F32, kind="Internal").ap()
    with ExitStack() as ctx:
        X = ctx.enter_context(nc.sbuf_tensor("X", [P, TILES, D], F32))
        XN3T = ctx.enter_context(nc.sbuf_tensor("XN3T", [P, C, T], F32))
        phase_a(nc, A, X, XN3T, w_dram)
        phase_b(nc, A, X, XN3T, w_dram, q_dram)
        phase_c(nc, A, X)
        phase_d(nc, A, X, XN3T, q_dram, out)


def kernel(**inputs):
    import concourse.bacc as bacc
    from concourse.bass_utils import run_bass_kernel_spmd

    nc = bacc.Bacc("TRN2", target_bir_lowering=False, num_devices=1)
    arrays = laid_out(np, {name: np.ascontiguousarray(a) for name, a in inputs.items()})
    A = {name: nc.dram_tensor(name, a.shape, mybir.dt.from_np(a.dtype), kind="ExternalInput").ap()
         for name, a in arrays.items()}
    out = nc.dram_tensor("out", [TILES, P, D], F32, kind="ExternalOutput").ap()
    program(nc, A, out)
    result = run_bass_kernel_spmd(nc, [arrays], core_ids=[0])
    return result.results[0]["out"].reshape(B, LQ, D)
```

```python
from contextlib import ExitStack

import numpy as np
import concourse.bass as bass
from concourse import mybir

F32 = mybir.dt.float32
F32R = mybir.dt.float32r
BF16 = mybir.dt.bfloat16
I32 = mybir.dt.int32
ALU = mybir.AluOpType
ACT = mybir.ActivationFunctionType
AX = mybir.AxisListType

P = 128
B, LQ, LK, D = 32, 32, 257, 512
T = B * LQ
TILES = T // P
BT = P // LQ
C = D // P
H, DH = 16, 32
G = H // BT
HK = 64
E = 8
I1 = 1024
FF = 1408
FC = FF // P
BLK = 16
KH = 2
NORM2_MIN = 1e-24


def turn_before(m, u):
    return m if u == 0 else m - 1


class Steps:

    def __init__(self, eng, sem):
        self.eng, self.sem, self.n = eng, sem, 0

    def restart(self):
        self.eng.sem_clear(self.sem)
        self.n = 0

    def __call__(self, ins):
        self.n += 1
        ins.then_inc(self.sem, 1)
        self.eng.wait_ge(self.sem, self.n)


def product3(pe, out, lhs, rhs, start, stop):
    (lh, ll), (rh, rl) = lhs, rhs
    pe.matmul(out, ll, rh, start=start, stop=False)
    pe.matmul(out, lh, rl, start=False, stop=False)
    return pe.matmul(out, lh, rh, start=False, stop=stop)


def cast(x):
    return x.bitcast(F32)



CHAIN = ["wo", "xT2", "xT1", "q", "qkv", "am", "num", "z", "xT3", "log", "qT", "wT"]
QUERY = ["xT1", "q", "qT"]
AT = {"wo": 0, "norm2": 2, "xT2": 3, "norm1": 4, "xT1": 5, "q": 6, "qkv": 7, "qk": 8, "qhat": 8, "am": 9, "num": 10,
      "z": 11, "norm3": 13, "xT3": 14, "log": 15, "qT": 16, "rank": 17, "wT": 18}
SLOTS = 20
TAIL_AT = 5
KT_LATE = 4
UNITS = BT * G


HALVES = [*range(2 * KH, SLOTS - 1), SLOTS + 1]


def half_of(i, k, late, own, nxt):
    for s, t, there in ((k - late, i + 1, nxt), (k - late + SLOTS, i, own)):
        if there and s in HALVES:
            j, r = divmod(HALVES.index(s), 2 * KH)
            return t, j, "kv"[r % 2], r // 2
    return None


def phase_a(nc, A, X, XN3T, w_dram):
    with ExitStack() as ctx:
        sb = lambda n, s, d=F32: ctx.enter_context(nc.sbuf_tensor("pa_" + n, s, d))
        sem = lambda n: ctx.enter_context(nc.semaphore(n))
        wk = [sb("wk_hi", [P, C, D], F32R), sb("wk_lo", [P, C, D], F32R)]
        wv = [sb("wv_hi", [P, C, D], F32R), sb("wv_lo", [P, C, D], F32R)]
        wq = sb("wq", [P, C, D])
        wo = sb("wo", [P, C, D])
        ident = sb("ident", [P, P])
        ctx_raw = [sb(f"ctx_raw{r}", [P, C, KH * P]) for r in range(2)]
        ctx_hi = [sb(f"ctx_hi{r}", [P, C, KH * P], F32R) for r in range(2)]
        ctx_lo = [sb(f"ctx_lo{r}", [P, C, KH * P], F32R) for r in range(2)]
        ctx_tail = sb("ctx_tail", [P, C, B])
        keysT = [sb(f"keysT{j}", [P, C, LK]) for j in range(BT)]
        vals = [[sb(f"vals{j}_{h}", [P, D]) for h in range(KH)] for j in range(BT)]
        vtail = sb("vtail", [B, D])
        ktailT = sb("ktailT", [P, C, B])
        kraw = [sb(f"kraw{r}", [P, D]) for r in range(2)]
        ksq = [sb(f"ksq{r}", [P, D]) for r in range(2)]
        khat = [sb(f"khat{r}", [P, D]) for r in range(2)]
        kn2 = [sb(f"kn2_{r}", [P, H]) for r in range(2)]
        kinv = [sb(f"kinv{r}", [P, H]) for r in range(2)]
        qblock = sb("qblock", [P, G, BT, P])
        w_raw = [XN3T[:, :, m * D:(m + 1) * D] for m in range(2)]
        qs = sb("qs", [P, D])
        qsq = sb("qsq", [P, D])
        qn2 = sb("qn2", [P, H])
        qinv = sb("qinv", [P, H])
        qscale = sb("qscale", [P, H])
        oT = sb("oT", [P, G, P])
        bias = sb("bias", [P, LK])
        logit = [sb(f"logit{r}", [P, LK]) for r in range(2)]
        nmax = [sb(f"nmax{r}", [P, 1]) for r in range(2)]
        prob = [sb(f"prob{r}", [P, LK]) for r in range(2)]
        psum_ = [sb(f"psum_{r}", [P, 1]) for r in range(2)]
        rsum = [sb(f"rsum{r}", [P, 1]) for r in range(2)]
        pn = [sb(f"pn{r}", [P, KH * P + B]) for r in range(2)]
        pT = [sb(f"pT{r}", [P, KH * P]) for r in range(2)]
        pTtail = [sb(f"pTtail{r}", [B, P]) for r in range(2)]
        onehot = sb("onehot", [P, B, B])
        bq = sb("bq", [P, D])
        bo = sb("bo", [P, D])
        xn = sb("xn", [P, D])
        xnT1 = sb("xnT1", [P, C, P])
        xnT = sb("xnT", [P, C, P])
        stats = sb("stats", [P, 6])
        mv = sb("mv", [P, 2])
        veps = sb("veps", [P, 1])
        rstd = sb("rstd", [P, 1])
        mhalf = sb("mhalf", [P, H])
        eps = sb("eps", [P, 1])
        fence = sb("fence", [P, 3])
        aq = sb("aq", [P, C, HK])
        ak = sb("ak", [P, C, HK])
        av = sb("av", [P, C, HK])
        ao = sb("ao", [HK, D])
        gate = sb("gate", [P, C, E])
        elmin = sb("elmin", [HK, 2 * P])
        elexp = sb("elexp", [HK, 2 * P])
        qk = sb("qk", [HK, 2 * P])
        va = sb("va", [P, HK])
        cmaskT = sb("cmaskT", [P, P])
        am = sb("am", [P, P])
        ones = sb("ones", [P, 1])
        numT = sb("numT", [HK, P])
        den = sb("den", [P, 1])
        rden = sb("rden", [P, 1])
        lg = sb("lg", [P, E])
        lgmax = sb("lgmax", [P, 1])
        lgexp = sb("lgexp", [P, E])
        lgsum = sb("lgsum", [P, 1])
        lgr = sb("lgr", [P, 1])
        score = sb("score", [P, E])
        above = sb("above", [P, E, E])
        tie = sb("tie", [P, E, E])
        lower = sb("lower", [P, E, E])
        rank = sb("rank", [P, E])
        sel = sb("sel", [P, E])
        wsel = sb("wsel", [P, E])
        wT = sb("wT", [E, T])
        bank = [ctx.enter_context(nc.psum_tensor(f"pa{b}", [P, 512], F32)) for b in range(8)]
        k_ps, v_ps, kt_ps, s_ps, pt_ps, pv_ps, misc = bank[0], bank[1], bank[2], bank[3:5], bank[5], bank[6], bank[7]

        w_in = sem("a_w_in")
        wkv_in = [sem(f"a_wkv_in{m}") for m in range(2)]
        c_in = sem("a_c_in")
        w_hi = sem("a_w_hi")
        w_lo = sem("a_w_lo")
        x_in, x_rest_in = sem("a_x_in"), sem("a_x_rest_in")
        init = sem("a_init")
        scale_ready = sem("a_scale_ready")
        ctx_in = [sem(f"a_ctx_in{r}") for r in range(2)]
        ctx_hi_ready = sem("a_ctx_hi")
        ctx_lo_ready = sem("a_ctx_lo")
        k_full, k_sq, k_free = sem("a_k_full"), sem("a_k_sq"), sem("a_k_free")
        v_full, v_free = sem("a_v_full"), sem("a_v_free")
        kn2_ready, kinv_ready, khat_ready = sem("a_kn2"), sem("a_kinv"), sem("a_khat")
        kt_full, kt_free = sem("a_kt_full"), sem("a_kt_free")
        ktail_ready = sem("a_ktail")
        tail_full, tail_done = sem("a_tail_full"), sem("a_tail_done")
        tail_n2, tail_inv, tail_hat, tail_t = sem("a_tail_n2"), sem("a_tail_inv"), sem("a_tail_hat"), sem("a_tail_t")
        s_full, l_ready, p_ready, pn_ready = sem("a_s_full"), sem("a_l_ready"), sem("a_p_ready"), sem("a_pn_ready")
        pt_full, pt_copied, pt_tail = sem("a_pt_full"), sem("a_pt_copied"), sem("a_pt_tail")
        pv_done, pv_free = sem("a_pv_done"), sem("a_pv_free")
        misc_full, misc_free = sem("a_misc_full"), sem("a_misc_free")
        mv_ready, rstd_ready, xn_ready = sem("a_mv"), sem("a_rstd"), sem("a_xn")
        qn2_ready, qinv_ready, qhat_ready = sem("a_qn2"), sem("a_qinv"), sem("a_qhat")
        qblock_ready = sem("a_qblock")
        elmin_ready, elexp_ready = sem("a_elmin"), sem("a_elexp")
        lg_ready, lgexp_ready, wsel_ready = sem("a_lg"), sem("a_lgexp"), sem("a_wsel")
        xn3_stored = sem("a_xn3")
        w_out = sem("a_w_out")
        v_steps, s_steps, p_steps = sem("a_vsteps"), sem("a_ssteps"), sem("a_psteps")

        def uses_before(i):
            if isinstance(i, int) and i < 1:
                return len(QUERY) * (i + 1)
            return 2 * len(QUERY) + len(CHAIN) * (i - 1) - (len(QUERY) if isinstance(i, int) and i == TILES else 0)

        def use(i, name):
            if isinstance(i, int) and i < 1:
                return uses_before(i) + QUERY.index(name)
            names = CHAIN if not isinstance(i, int) or i < TILES - 1 else [u for u in CHAIN if u not in QUERY]
            return uses_before(i) + names.index(name)

        def norms(i, which):
            if isinstance(i, int) and i < 1:
                return i + 1
            if isinstance(i, int) and i >= TILES - 1:
                return 2 + 3 * (TILES - 2) + 2 * (i - TILES + 1) + (2, 3).index(which)
            return 2 + 3 * (i - 1) + (2, 1, 3).index(which)

        def iterations(eng, body):
            body(-1, own=False, nxt=True, past=False)
            body(0, own=True, nxt=True, past=False)
            with eng.Fori(1, TILES - 1) as i:
                body(i, own=True, nxt=True, past=True)
            body(TILES - 1, own=True, nxt=False, past=True)
            body(TILES, own=False, nxt=False, past=True)

        first_consts = [(ctx_tail, A["ctx_tail"]), (ident, A["ident"]), (qscale, A["scale_log"])]
        consts = [(bq, A["l0_bq"]), (wq, A["l0_wq"]), (bias, A["attn_bias"]), (onehot, A["onehot"]),
                  (wo, A["l0_wo"]), (bo, A["l0_bo"]), (aq, A["a_wq"]), (ak, A["a_wk"]), (av, A["a_wv"]),
                  (ao, A["a_wo"]), (gate, A["gate"]), (cmaskT, A["cmaskT"]), (lower, A["lower"])]

        with nc.Block() as block:

            @block.sync
            def _(sp):
                def load_ctx(t, j):
                    n = 4 * t + j
                    if not (isinstance(n, int) and n < 2):
                        sp.wait_ge(ctx_lo_ready, n - 1)
                    sp.dma_start(ctx_raw[j % 2][:], A["ctxT"][bass.ds(n, 1)].rearrange("o p c k -> (o p) c k")[:, :, 0:KH * P]).then_inc(ctx_in[j % 2], 16)

                for m, name in enumerate(("l0_wk", "l0_wv")):
                    sp.dma_start(w_raw[m], A[name]).then_inc(wkv_in[m], 16)
                    if m == 0:
                        load_ctx(0, 0)
                        for dst, src in first_consts:
                            sp.dma_start(dst[:], src).then_inc(c_in, 16)
                load_ctx(0, 1)
                sp.dma_start(X[:, 0:2, :], A["x"][:, 0:2, :]).then_inc(x_in, 16)
                for dst, src in consts:
                    sp.dma_start(dst[:], src).then_inc(w_in, 16)
                sp.dma_start(X[:, 2:, :], A["x"][:, 2:, :]).then_inc(x_rest_in, 16)
                load_ctx(0, 2)
                load_ctx(0, 3)
                with sp.Fori(0, TILES - 1) as i:
                    for j in range(BT):
                        load_ctx(i + 1, j)
                sp.wait_ge(misc_free, use(TILES, "wT") + 1)
                sp.dma_start(w_dram[:], wT[:]).then_inc(w_out, 16)
                sp.wait_ge(w_out, 16)

            @block.tensor
            def _(pe):
                def projected(t, j, kind, h):
                    n, r = 8 * t + 2 * j + h, j % 2
                    pe.wait_ge(ctx_lo_ready, 4 * t + j + 1)
                    w, ps, full, free = (wk, k_ps, k_full, k_free) if kind == "k" else (wv, v_ps, v_full, v_free)
                    pe.wait_ge(free, n)
                    ks = slice(h * P, (h + 1) * P)
                    for c in range(C):
                        mm = product3(pe, ps[:], (ctx_hi[r][:, c, ks], ctx_lo[r][:, c, ks]),
                                      (w[0][:, c, :], w[1][:, c, :]), c == 0, c == C - 1)
                    mm.then_inc(full, 1)

                def keys_transposed(t, j, h):
                    n = 8 * t + 2 * j + h
                    pe.wait_ge(khat_ready, n + 1)
                    pe.wait_ge(kt_free, n)
                    for c in range(C):
                        tr = pe.transpose(kt_ps[:, c * P:(c + 1) * P], khat[h][:, c * P:(c + 1) * P], ident[:])
                    tr.then_inc(kt_full, 1)

                def take(i, name):
                    pe.wait_ge(misc_free, use(i, name))

                def turn(i, name, src):
                    take(i, name)
                    for c in range(C):
                        tr = pe.transpose(misc[:, c * P:(c + 1) * P], src[:, c * P:(c + 1) * P], ident[:])
                    tr.then_inc(misc_full, 1)

                def scores(i, u):
                    j, g, m = u // G, u % G, UNITS * i + u
                    if g == 0:
                        pe.wait_ge(kt_free, 8 * i + 2 * j + 2)
                        pe.wait_ge(ktail_ready, BT * i + j + 1)
                    if u == 0:
                        pe.wait_ge(qblock_ready, i + 1)
                    pe.wait_ge(l_ready, turn_before(m, u))
                    pe.matmul(s_ps[u % 2][:, 0:LK], qblock[:, g, j, :], keysT[j][:, g, :],
                              start=True, stop=True).then_inc(s_full, 1)

                def probs_transposed(i, u):
                    m = UNITS * i + u
                    pe.wait_ge(pn_ready, m + 1)
                    pe.wait_ge(pt_copied, m)
                    pe.wait_ge(pt_tail, m)
                    src = pn[u % 2]
                    pe.transpose(pt_ps[:, 0:P], src[:, 0:P], ident[:])
                    pe.transpose(pt_ps[:, P:2 * P], src[:, P:2 * P], ident[:])
                    pe.transpose(pt_ps[0:B, 2 * P:3 * P], src[:, 2 * P:2 * P + B], ident[:]).then_inc(pt_full, 1)

                def values(i, u):
                    j, g, m = u // G, u % G, UNITS * i + u
                    pe.wait_ge(pt_copied, m + 1)
                    pe.wait_ge(pt_tail, m + 1)
                    if g == 0:
                        pe.wait_ge(v_free, 8 * i + 2 * j + 2)
                        pe.wait_ge(pv_free, BT * i + j)
                    out, fs = pv_ps[:, g * P:(g + 1) * P], slice(g * P, (g + 1) * P)
                    pe.matmul(out, vals[j][0][:, fs], pT[u % 2][:, 0:P], start=True, stop=False)
                    pe.matmul(out, vals[j][1][:, fs], pT[u % 2][:, P:2 * P], start=False, stop=False)
                    pe.matmul(out, vtail[:, fs], pTtail[u % 2][:], start=False, stop=True).then_inc(pv_done, 1)

                def project(i, name, lhs, rhs):
                    take(i, name)
                    for k, (a, b) in enumerate(zip(lhs, rhs)):
                        mm = pe.matmul(misc[:], a, b, start=k == 0, stop=k == len(lhs) - 1)
                    mm.then_inc(misc_full, 1)

                def chain(i, k):
                    if k == AT["wo"]:
                        pe.wait_ge(pv_free, BT * i)
                        project(i, "wo", [oT[:, g, :] for g in range(G)], [wo[:, g, :] for g in range(G)])
                    if k == AT["xT2"]:
                        pe.wait_ge(xn_ready, norms(i, 2) + 1)
                        turn(i, "xT2", xn)
                    if k == AT["qkv"]:
                        take(i, "qkv")
                        for w, col in ((aq, 0), (ak, P)):
                            for c in range(C):
                                pe.matmul(misc[0:HK, col:col + P], w[:, c, :], xnT[:, c, :], start=c == 0, stop=c == C - 1)
                        for c in range(C):
                            mm = pe.matmul(misc[:, 2 * P:2 * P + HK], xnT[:, c, :], av[:, c, :], start=c == 0, stop=c == C - 1)
                        mm.then_inc(misc_full, 1)
                    if k == AT["am"]:
                        take(i, "am")
                        pe.matmul(misc[:, 0:P], qk[:, P:2 * P], qk[:, 0:P], start=True, stop=True).then_inc(misc_full, 1)
                    if k == AT["num"]:
                        take(i, "num")
                        pe.matmul(misc[0:HK, 0:P], va[:], am[:], start=True, stop=True)
                        pe.matmul(misc[:, P:P + 1], am[:], ones[:], start=True, stop=True).then_inc(misc_full, 1)
                    if k == AT["z"]:
                        project(i, "z", [numT[:]], [ao[:]])
                    if k == AT["xT3"]:
                        pe.wait_ge(xn_ready, norms(i, 3) + 1)
                        turn(i, "xT3", xn)
                    if k == AT["log"]:
                        take(i, "log")
                        for c in range(C):
                            mm = pe.matmul(misc[:, 0:E], xnT[:, c, :], gate[:, c, :], start=c == 0, stop=c == C - 1)
                        mm.then_inc(misc_full, 1)
                    if k == AT["wT"]:
                        pe.wait_ge(wsel_ready, i)
                        take(i, "wT")
                        pe.transpose(misc[0:E, 0:P], wsel[:], ident[:]).then_inc(misc_full, 1)

                def queries(i, k):
                    if k == AT["xT1"]:
                        if isinstance(i, int) and i == -1:
                            pe.wait_ge(w_in, 16 * len(consts))
                            pe.wait_ge(init, 4)
                        pe.wait_ge(xn_ready, norms(i, 1) + 1)
                        turn(i, "xT1", xn)
                    if k == AT["q"]:
                        project(i, "q", [xnT1[:, c, :] for c in range(C)], [wq[:, c, :] for c in range(C)])
                    if k == AT["qT"]:
                        pe.wait_ge(qhat_ready, i + 2)
                        turn(i, "qT", qs)

                def tail_transposed():
                    pe.wait_ge(tail_hat, 1)
                    for c in range(C):
                        tr = pe.transpose(kt_ps[:, c * B:(c + 1) * B], qs[0:B, c * P:(c + 1) * P], ident[0:B, 0:B])
                    tr.then_inc(tail_t, 1)

                def iteration(i, own, nxt, past):
                    for k in range(SLOTS):
                        if own and k < UNITS:
                            scores(i, k)
                        if own and 0 <= k - 2 < UNITS:
                            probs_transposed(i, k - 2)
                        if own and 0 <= k - 3 < UNITS:
                            values(i, k - 3)
                        if past:
                            chain(i, k)
                        if nxt:
                            queries(i, k)
                        if not own and nxt and k == TAIL_AT:
                            tail_transposed()
                        half = half_of(i, k, KT_LATE, own, nxt)
                        if half and half[2] == "k":
                            if not own and nxt and k == 2 * KH + KT_LATE:
                                pe.wait_ge(tail_done, 1)
                            keys_transposed(half[0], half[1], half[3])
                        half = half_of(i, k, 0, own, nxt)
                        if half:
                            projected(*half)

                pe.wait_ge(w_lo, 2)
                pe.wait_ge(c_in, 16 * len(first_consts))
                for w, ps in ((wk, s_ps[0]), (wv, s_ps[1])):
                    for half in range(2):
                        for c in range(C):
                            mm = pe.matmul(ps[0:B, :], ctx_tail[:, c, :], cast(w[half][:, c, :]),
                                           start=c == 0 and half == 0, stop=c == C - 1 and half == 1)
                mm.then_inc(tail_full, 1)
                iterations(pe, iteration)

            @block.scalar
            def _(act):
                def split_ctx(t, j):
                    n = 4 * t + j
                    act.wait_ge(ctx_in[j % 2], 16 * (2 * t + j // 2) + 16)
                    if not (isinstance(n, int) and n < 2):
                        act.wait_ge(v_full, 2 * n - 2)
                    act.activation(ctx_hi[j % 2][:], ctx_raw[j % 2][:], ACT.Copy).then_inc(ctx_hi_ready, 1)

                def keys_square(t, j, h):
                    n = 8 * t + 2 * j + h
                    act.wait_ge(k_full, n + 1)
                    if not (isinstance(n, int) and n < 2):
                        act.wait_ge(khat_ready, n - 1)
                    act.activation(ksq[h][:], k_ps[:], ACT.Square).then_inc(k_sq, 1)

                def keys_copy(h):
                    act.activation(kraw[h][:], k_ps[:], ACT.Copy).then_inc(k_free, 1)

                def values_copy(t, j, h):
                    act.wait_ge(v_full, 8 * t + 2 * j + h + 1)
                    if h == 0 and not (isinstance(t, int) and t == 0):
                        act.wait_ge(pv_done, UNITS * (t - 1) + G * j + G)
                    act.activation(vals[j][h][:], v_ps[:], ACT.Copy).then_inc(v_free, 1)

                def turned_keys_copy(t, j, h):
                    n = 8 * t + 2 * j + h
                    act.wait_ge(kt_full, n + 1)
                    if h == 0 and not (isinstance(t, int) and t == 0):
                        act.wait_ge(s_full, UNITS * (t - 1) + G * j + G)
                    act.activation(keysT[j][:, :, h * P:(h + 1) * P], kt_ps[:].rearrange("p (c k) -> p c k", c=C),
                                   ACT.Copy).then_inc(kt_free, 1)

                def exps(i, u):
                    m, r = UNITS * i + u, u % 2
                    act.wait_ge(l_ready, m + 1)
                    act.wait_ge(pn_ready, turn_before(m, u))
                    act.activation(prob[r][:], logit[r][:], ACT.Exp, bias=nmax[r][:], scale=-1.0,
                                   accum_out=psum_[r][:]).then_inc(p_ready, 1)

                def probs_copy(i, u):
                    m, r = UNITS * i + u, u % 2
                    act.wait_ge(pt_full, m + 1)
                    act.wait_ge(pv_done, turn_before(m, u))
                    act.activation(pT[r][:], pt_ps[:, 0:KH * P], ACT.Copy).then_inc(pt_copied, 1)
                    act.activation(pTtail[r][:], pt_ps[0:B, KH * P:KH * P + P], ACT.Copy).then_inc(pt_tail, 1)

                def iteration(i, own, nxt, past):
                    for k in range(SLOTS):
                        if not own and nxt and k == 2:
                            act.wait_ge(tail_full, 1)
                            act.activation(qsq[0:B, :], s_ps[0][0:B, :], ACT.Square).then_inc(tail_n2, 1)
                        half = half_of(i, k, KT_LATE + 1, own, nxt)
                        if half and half[2] == "k":
                            turned_keys_copy(half[0], half[1], half[3])
                        half = half_of(i, k, 1, own, nxt)
                        if half and half[2] == "k":
                            keys_square(half[0], half[1], half[3])
                        if own and k < UNITS:
                            exps(i, k)
                        if own and 0 <= k - 2 < UNITS:
                            probs_copy(i, k - 2)
                        if half and half[2] == "k":
                            keys_copy(half[3])
                        if half and half[2] == "v":
                            values_copy(half[0], half[1], half[3])
                        if nxt and k % (2 * KH) == 1 and k // (2 * KH) < BT:
                            split_ctx(i + 1, k // (2 * KH))
                        if past and k == AT["qkv"]:
                            act.wait_ge(elmin_ready, i)
                            act.activation(elexp[:], elmin[:], ACT.Exp).then_inc(elexp_ready, 1)
                        if past and k == AT["log"]:
                            act.wait_ge(lg_ready, i)
                            act.activation(lgexp[:], lg[:], ACT.Exp, bias=lgmax[:], accum_out=lgsum[:]).then_inc(lgexp_ready, 1)

                for m, w in enumerate((wk, wv)):
                    act.wait_ge(wkv_in[m], 16)
                    act.activation(w[0][:], w_raw[m], ACT.Copy).then_inc(w_hi, 1)
                act.wait_ge(init, 4)
                act.activation(qscale[:], qscale[:], ACT.Exp).then_inc(scale_ready, 1)
                iterations(act, iteration)

            @block.gpsimd
            def _(pool):
                step = Steps(pool, p_steps)

                def split_ctx(t, j):
                    n = 4 * t + j
                    pool.wait_ge(ctx_hi_ready, n + 1)
                    pool.tensor_tensor(ctx_lo[j % 2][:], ctx_raw[j % 2][:], cast(ctx_hi[j % 2][:]), ALU.subtract)\
                        .then_inc(ctx_lo_ready, 1)

                def inverse(src, dst, ready, done, n):
                    pool.wait_ge(ready, n + 1)
                    pool.tensor_tensor(dst, src, mhalf[0:src.shape[0], :], ALU.pow).then_inc(done, 1)

                def layer_norm(n):
                    pool.wait_ge(mv_ready, n + 1)
                    step(pool.tensor_tensor(veps[:], mv[:, 1:2], eps[:], ALU.add))
                    pool.tensor_tensor(rstd[:], veps[:], mhalf[:, 0:1], ALU.pow).then_inc(rstd_ready, 1)

                def k_half(t, j, h):
                    inverse(kn2[h][:], kinv[h][:], kn2_ready, kinv_ready, 8 * t + 2 * j + h)

                def tail_column(t, j):
                    if isinstance(t, int) and t == 0:
                        pool.wait_ge(tail_done, 1)
                    else:
                        pool.wait_ge(s_full, UNITS * (t - 1) + G * j + G)
                    pool.tensor_copy(keysT[j][:, :, KH * P:LK], ktailT[:, :, bass.ds(4 * t + j, 1)]).then_inc(ktail_ready, 1)

                def q_norm(n):
                    inverse(qn2[:], qinv[:], qn2_ready, qinv_ready, n)

                def iteration(i, own, nxt, past):
                    step.restart()
                    for k in range(SLOTS):
                        if not own and nxt and k == AT["norm1"]:
                            inverse(qn2[0:B, :], qinv[0:B, :], tail_n2, tail_inv, 1)
                        if past and k == AT["wo"]:
                            layer_norm(norms(i, 2))
                        if nxt and k == AT["xT2"]:
                            layer_norm(norms(i, 1))
                        if past and k == AT["z"]:
                            layer_norm(norms(i, 3))
                        if past and k == AT["xT3"]:
                            pool.wait_ge(misc_free, use(i, "xT3") + 1)
                            pool.tensor_copy(XN3T[:, :, bass.ds((i - 1) * P, P)], xnT[:]).then_inc(xn3_stored, 1)
                        half = half_of(i, k, 1, own, nxt)
                        if half and half[2] == "k":
                            k_half(half[0], half[1], half[3])
                            if half[3] == 0:
                                tail_column(half[0], half[1])
                        if nxt and k == AT["q"]:
                            q_norm(i + 1)
                        if nxt and k % (2 * KH) == 1 and k // (2 * KH) < BT:
                            split_ctx(i + 1, k // (2 * KH))

                pool.sem_inc(xn3_stored, 1)
                pool.wait_ge(init, 4)
                iterations(pool, iteration)

            @block.vector
            def _(dve):
                step = Steps(dve, v_steps)

                def heads(ap):
                    return ap.rearrange("p (h d) -> p h d", h=H)

                def spread(ap, n=P):
                    return ap.rearrange("p (h o) -> p h o", o=1).to_broadcast([n, H, DH])

                def norm2_of(squares, dst):
                    step(dve.tensor_reduce(dst, heads(squares), AX.X, ALU.add))
                    return dve.tensor_scalar(dst, dst, NORM2_MIN, None, ALU.max)

                def norm2(t, j, h):
                    n = 8 * t + 2 * j + h
                    dve.wait_ge(k_sq, n + 1)
                    norm2_of(ksq[h][:], kn2[h][:]).then_inc(kn2_ready, 1)

                def normalise(t, j, h):
                    n = 8 * t + 2 * j + h
                    dve.wait_ge(kinv_ready, n + 1)
                    dve.wait_ge(k_free, n + 1)
                    if not (isinstance(n, int) and n < 2):
                        dve.wait_ge(kt_full, n - 1)
                    dve.tensor_tensor(heads(khat[h][:]), heads(kraw[h][:]), spread(kinv[h][:]), ALU.mult)\
                        .then_inc(khat_ready, 1)

                def statistics(x):
                    step(dve.memset(fence[:, 2:3], 0.0))
                    step(dve.bn_stats(stats[:], x))
                    dve.bn_aggr(mv[:], stats[:]).then_inc(mv_ready, 1)

                def layer_normed(x, n):
                    dve.wait_ge(rstd_ready, n + 1)
                    dve.tensor_scalar(xn[:], x, mv[:, 0:1], rstd[:], ALU.subtract, ALU.mult).then_inc(xn_ready, 1)

                def bank_full(i, name):
                    dve.wait_ge(misc_full, use(i, name) + 1)

                def bank_read(i, name):
                    dve.wait_ge(misc_free, use(i, name) + 1)

                def turned(i, name, dst):
                    bank_full(i, name)
                    dve.tensor_copy(dst[:].rearrange("p c t -> p (c t)"), misc[:]).then_inc(misc_free, 1)

                def q_norms(i):
                    bank_full(i, "q")
                    dve.tensor_tensor(qs[:], misc[:], bq[:], ALU.add).then_inc(misc_free, 1)
                    dve.wait_ge(misc_free, use(i, "q") + 1)
                    step(dve.tensor_tensor(qsq[:], qs[:], qs[:], ALU.mult))
                    norm2_of(qsq[:], qn2[:]).then_inc(qn2_ready, 1)

                def q_hat(i):
                    dve.wait_ge(qinv_ready, i + 2)
                    step(dve.tensor_tensor(qinv[:], qinv[:], qscale[:], ALU.mult))
                    dve.tensor_tensor(heads(qs[:]), heads(qs[:]), spread(qinv[:]), ALU.mult).then_inc(qhat_ready, 1)

                def q_blocks(i):
                    bank_full(i, "qT")
                    for h in range(BT):
                        rows = slice(h * DH, (h + 1) * DH)
                        cp = dve.tensor_copy(qblock[rows, :, :, h * LQ:(h + 1) * LQ],
                                             misc[rows, :].rearrange("p (g j q) -> p g j q", g=G, j=BT))
                        if h < BT - 1:
                            step(cp)
                    cp.then_inc(qblock_ready, 1)
                    dve.wait_ge(qblock_ready, i + 2)
                    dve.sem_inc(misc_free, 1)

                def logits(i, u):
                    m, r = UNITS * i + u, u % 2
                    dve.wait_ge(s_full, m + 1)
                    dve.wait_ge(p_ready, turn_before(m, u))
                    dve.memset(fence[:, r:r + 1], 0.0)
                    dve.tensor_tensor_reduce(logit[r][:], s_ps[r][:, 0:LK], bias[:], -1.0, 3e38, ALU.add, ALU.min,
                                             nmax[r][:]).then_inc(l_ready, 1)

                def normed(i, u):
                    j, m, r = u // G, UNITS * i + u, u % 2
                    dve.wait_ge(p_ready, m + 1)
                    dve.wait_ge(pt_full, turn_before(m, u))
                    step(dve.reciprocal(rsum[r][:], psum_[r][:]))
                    step(dve.tensor_scalar(pn[r][:, KH * P:], onehot[:, bass.ds(BT * i + j, 1), :].rearrange("p o b -> p (o b)"),
                                           prob[r][:, KH * P:LK], rsum[r][:], ALU.mult, ALU.mult))
                    dve.tensor_scalar(pn[r][:, 0:KH * P], prob[r][:, 0:KH * P], rsum[r][:], None, ALU.mult)\
                        .then_inc(pn_ready, 1)

                def outputs(i, j):
                    dve.wait_ge(pv_done, UNITS * i + G * j + G)
                    for h in range(BT):
                        rows = slice(h * DH, (h + 1) * DH)
                        cp = dve.tensor_copy(oT[rows, :, j * LQ:(j + 1) * LQ],
                                             pv_ps[rows, :].rearrange("p (g q) -> p g q", g=G)[:, :, h * LQ:(h + 1) * LQ])
                    cp.then_inc(pv_free, 1)

                def tile_of_x(t):
                    return X[:, bass.ds(t, 1), :].rearrange("p o d -> p (o d)")

                def chain(i, k):
                    x = tile_of_x(i - 1)
                    if k == AT["wo"]:
                        bank_full(i, "wo")
                        dve.tensor_tensor(x, misc[:], x, ALU.add).then_inc(misc_free, 1)
                        bank_read(i, "wo")
                        step(dve.tensor_tensor(x, x, bo[:], ALU.add))
                        statistics(x)
                    if k == AT["norm2"]:
                        layer_normed(x, norms(i, 2))
                    if k == AT["xT2"]:
                        dve.wait_ge(xn3_stored, i)
                        turned(i, "xT2", xnT)
                    if k == AT["qkv"]:
                        bank_full(i, "qkv")
                        dve.tensor_scalar(elmin[:], misc[0:HK, 0:2 * P], 0.0, None, ALU.min).then_inc(elmin_ready, 1)
                        step(dve.tensor_copy(va[:], misc[:, 2 * P:2 * P + HK]))
                    if k == AT["qk"]:
                        dve.wait_ge(elexp_ready, i)
                        dve.scalar_tensor_tensor(out=qk[:], in0=misc[0:HK, 0:2 * P], scalar=0.0, in1=elexp[:],
                                                 op0=ALU.max, op1=ALU.add).then_inc(misc_free, 1)
                    if k == AT["am"]:
                        bank_full(i, "am")
                        dve.tensor_tensor(am[:], misc[:, 0:P], cmaskT[:], ALU.mult).then_inc(misc_free, 1)
                    if k == AT["num"]:
                        bank_full(i, "num")
                        step(dve.tensor_scalar(den[:], misc[:, P:P + 1], 1e-6, None, ALU.add))
                        step(dve.reciprocal(rden[:], den[:]))
                        dve.tensor_copy(numT[:], misc[0:HK, 0:P]).then_inc(misc_free, 1)
                    if k == AT["z"]:
                        bank_full(i, "z")
                        dve.scalar_tensor_tensor(out=x, in0=misc[:], scalar=rden[:], in1=x,
                                                 op0=ALU.mult, op1=ALU.add).then_inc(misc_free, 1)
                        bank_read(i, "z")
                        statistics(x)
                    if k == AT["norm3"]:
                        layer_normed(x, norms(i, 3))
                    if k == AT["xT3"]:
                        turned(i, "xT3", xnT)
                    if k == AT["log"]:
                        bank_full(i, "log")
                        dve.tensor_copy(lg[:], misc[:, 0:E]).then_inc(misc_free, 1)
                        bank_read(i, "log")
                        dve.tensor_reduce(lgmax[:], lg[:], AX.X, ALU.max, negate=True).then_inc(lg_ready, 1)
                    if k == AT["rank"]:
                        choose(i)
                    if k == AT["wT"]:
                        bank_full(i, "wT")
                        dve.tensor_copy(wT[:, bass.ds((i - 1) * P, P)], misc[0:E, 0:P]).then_inc(misc_free, 1)

                def choose(i):
                    dve.wait_ge(lgexp_ready, i)
                    step(dve.reciprocal(lgr[:], lgsum[:]))
                    step(dve.tensor_scalar(score[:], lgexp[:], lgr[:], None, ALU.mult))
                    other = score[:].rearrange("p (o e) -> p o e", o=1).to_broadcast([P, E, E])
                    own = score[:].rearrange("p (e o) -> p e o", o=1).to_broadcast([P, E, E])
                    step(dve.tensor_tensor(above[:], other, own, ALU.is_gt))
                    step(dve.tensor_tensor(tie[:], other, own, ALU.is_equal))
                    step(dve.tensor_tensor(tie[:], tie[:], lower[:], ALU.mult))
                    step(dve.tensor_tensor(above[:], above[:], tie[:], ALU.add))
                    step(dve.tensor_reduce(rank[:], above[:], AX.X, ALU.add))
                    step(dve.tensor_scalar(sel[:], rank[:], 1.5, None, ALU.is_lt))
                    step(dve.tensor_tensor(score[:], score[:], sel[:], ALU.mult))
                    dve.scalar_tensor_tensor(out=wsel[:], in0=sel[:], scalar=-1.0, in1=score[:],
                                             op0=ALU.add, op1=ALU.add).then_inc(wsel_ready, 1)

                def queries(i, k):
                    x = tile_of_x(i + 1)
                    if k == AT["xT2"]:
                        if isinstance(i, int) and i == -1:
                            dve.wait_ge(x_in, 16)
                            dve.wait_ge(w_in, 16 * len(consts))
                        if isinstance(i, int) and i == 0:
                            dve.wait_ge(x_rest_in, 16)
                        statistics(x)
                    if k == AT["norm1"]:
                        layer_normed(x, norms(i, 1))
                    if k == AT["xT1"]:
                        turned(i, "xT1", xnT1)
                    if k == AT["q"]:
                        q_norms(i)
                    if k == AT["qhat"]:
                        q_hat(i)
                    if k == AT["qT"]:
                        q_blocks(i)

                def tail_norm():
                    dve.wait_ge(tail_n2, 1)
                    norm2_of(qsq[0:B, :], qn2[0:B, :]).then_inc(tail_n2, 1)
                    dve.wait_ge(tail_inv, 1)
                    dve.tensor_tensor(heads(qs[0:B, :]), heads(s_ps[0][0:B, :]), spread(qinv[0:B, :], B), ALU.mult)\
                       .then_inc(tail_hat, 1)
                    step(dve.tensor_copy(vtail[:], s_ps[1][0:B, :]))

                def iteration(i, own, nxt, past):
                    step.restart()
                    for k in range(SLOTS):
                        if own and k < UNITS:
                            logits(i, k)
                        if own and 0 <= k - 1 < UNITS:
                            normed(i, k - 1)
                        if own and 0 <= k - 3 < UNITS and (k - 3) % G == G - 1:
                            outputs(i, (k - 3) // G)
                        if past:
                            chain(i, k)
                        if nxt:
                            queries(i, k)
                        if not own and nxt and k == AT["norm1"]:
                            tail_norm()
                        if not own and nxt and k == TAIL_AT:
                            dve.wait_ge(tail_t, 1)
                            dve.tensor_copy(ktailT[:].rearrange("p c b -> p (c b)"), kt_ps[:, 0:C * B]).then_inc(tail_done, 1)
                        half = half_of(i, k, KT_LATE - 1, own, nxt)
                        if half and half[2] == "k":
                            normalise(half[0], half[1], half[3])
                        half = half_of(i, k, 1, own, nxt)
                        if half and half[2] == "k":
                            norm2(half[0], half[1], half[3])

                dve.memset(qblock[:], 0.0).then_inc(init, 1)
                step(dve.memset(eps[:], 1e-5))
                dve.memset(mhalf[:], -0.5).then_inc(init, 1)
                dve.memset(ones[:], 1.0).then_inc(init, 1)
                for m, (hi, lo) in enumerate((wk, wv)):
                    dve.wait_ge(w_hi, m + 1)
                    dve.tensor_tensor(lo[:], w_raw[m], cast(hi[:]), ALU.subtract).then_inc(w_lo, 1)
                dve.wait_ge(c_in, 16 * len(first_consts))
                dve.tensor_scalar(qscale[:], qscale[:], float(np.log(100.0)), None, ALU.min).then_inc(init, 1)
                dve.wait_ge(init, 4)
                dve.wait_ge(scale_ready, 1)
                iterations(dve, iteration)



STEPS_1 = (0.25, 0.75, 1.25, 1.75)
STEPS_2 = (2.5, 3.5)
STEP_4 = 5.0
FFN_TILES = 3 * FC
QS = 4


def blocks(ap, f):
    return ap.rearrange("p (n b) -> p n b", b=BLK) if f else ap


def spread_blocks(ap, n):
    return ap.rearrange("p (n o) -> p n o", o=1).to_broadcast([P, n, BLK])


def quant_scaled(dve, step, src, f, scale, inverse, y):
    n = f // BLK
    step(dve.tensor_reduce(scale, blocks(src, f), AX.X, ALU.max, apply_absolute_value=True))
    step(dve.tensor_scalar(scale, scale, 1.0 / 6.0, 1e-12, ALU.mult, ALU.max))
    step(dve.reciprocal(inverse, scale))
    return dve.tensor_tensor(blocks(y, f), blocks(src, f), spread_blocks(inverse, n), ALU.mult)


def halved(dve, scale, half_scale):
    return dve.tensor_scalar(half_scale, scale, 0.5, None, ALU.mult)


def quant_rounded(dve, step, mag, low, high, between=lambda n: None, begun=False):
    step(dve.tensor_scalar(low, mag, STEPS_1[0], None, ALU.is_gt))
    if not begun:
        step(dve.tensor_scalar(high, mag, STEP_4, 2.0, ALU.is_gt, ALU.mult))
    n = 2
    for group, total in ((STEPS_1[1:], low), (STEPS_2, high)):
        for m in group:
            step(dve.scalar_tensor_tensor(out=total, in0=mag, scalar=m, in1=total, op0=ALU.is_gt, op1=ALU.add))
            n += 1
            between(n)
    return dve.scalar_tensor_tensor(out=low, in0=high, scalar=2.0, in1=low, op0=ALU.mult, op1=ALU.add)


def quant_value(eng, step, low, sign, half_scale, f, out):
    step(eng.tensor_tensor(low, low, sign, ALU.mult))
    return eng.tensor_tensor(blocks(out, f), blocks(low, f), spread_blocks(half_scale, f // BLK), ALU.mult)


SCALE_AT = (0, 5, 10, 14)
ROUND_AT = (3, 8, 12, 17)
TURN_AT = (9, 14, 19, 23)
VALUE_AT = 1
TURN_BACK = 5

SHARED = I1 // D
PASSES = SHARED + E
TB = T // 512
FILLS = TB * C


def phase_b(nc, A, X, XN3T, w_dram, q_dram):
    with ExitStack() as ctx:
        sb = lambda n, s, d=F32: ctx.enter_context(nc.sbuf_tensor("pb_" + n, s, d))
        sem = lambda n: ctx.enter_context(nc.semaphore("b_" + n))
        Y = XN3T
        xn = [sb("xn_hi", [P, C, T], F32R), sb("xn_lo", [P, C, T], F32R)]
        hid = [sb("hid_hi", [P, C, T], F32R), sb("hid_lo", [P, C, T], F32R)]
        w = [[sb(f"w{m}_hi", [P, C, D], F32R), sb(f"w{m}_lo", [P, C, D], F32R)] for m in range(3)]
        raw = sb("raw", [P, C, D])
        q_raw, q_y, q_mag, q_val = (sb(n, [P, D]) for n in ("q_raw", "q_y", "q_mag", "q_val"))
        q_turn = sb("q_turn", [P, D])
        q_sign, q_low, q_high = (sb(n, [P, D], BF16) for n in ("q_sign", "q_low", "q_high"))
        q_scale, q_half, q_inv = (sb(n, [P, D // BLK]) for n in ("q_scale", "q_half", "q_inv"))
        gated = sb("gated", [P, FILLS, 512])
        scaled = [sb(f"scaled{r}", [P, 512]) for r in range(2)]
        act_out = [sb(f"act_out{r}", [P, 512]) for r in range(2)]
        wrow = sb("wrow", [P, T])
        weight = sb("weight", [P, T])
        mask = sb("mask", [P, T])
        b1, b2, b3 = (sb(f"b{m}", [P, E, C]) for m in (1, 2, 3))
        b1_now = sb("b1_now", [P, C])
        ident = sb("ident", [P, P])
        bank = [ctx.enter_context(nc.psum_tensor(f"pb{b}", [P, 512], F32)) for b in range(8)]

        w_in = sem("w_in")
        q_in, q_y_ready, q_mag_ready, q_val_ready = sem("q_in"), sem("q_y"), sem("q_mag"), sem("q_val")
        q_low_ready = sem("q_low")
        q_turned, q_copied, q_out = sem("q_turned"), sem("q_copied"), sem("q_out")
        w_hi = [sem(f"w_hi{m}") for m in range(3)]
        w_lo = [sem(f"w_lo{m}") for m in range(3)]
        c_in = sem("c_in")
        row_in = sem("row_in")
        row_used = sem("row_used")
        xn_hi, xn_lo = sem("xn_hi"), sem("xn_lo")
        full = [sem(f"full{m}") for m in range(3)]
        free = [sem(f"free{m}") for m in range(3)]
        act_ready = sem("act_ready")
        hid_hi, hid_lo = sem("hid_hi"), sem("hid_lo")
        y_added = sem("y_added")
        turned, x_added = sem("turned"), sem("x_added")
        v_steps, s_steps, p_steps = sem("vsteps"), sem("ssteps"), sem("psteps")

        def ks(k):
            return slice((k // C) * 512, (k // C) * 512 + 512)

        def tokens_low(eng, chunks):
            for c in chunks:
                eng.wait_ge(xn_hi, c + 1)
                eng.tensor_tensor(xn[1][:, c, :], XN3T[:, c, :], cast(xn[0][:, c, :]), ALU.subtract).then_inc(xn_lo, 1)

        with nc.Block() as block:

            @block.sync
            def _(sp):
                def load(n, m):
                    if m > 0:
                        sp.wait_ge(w_lo[m - 1], n + 1)
                    elif not (isinstance(n, int) and n == 0):
                        sp.wait_ge(w_lo[2], n)
                    sp.dma_start(raw[:], A["experts"][bass.ds(3 * n + m, 1)].rearrange("o p c d -> (o p) c d"))\
                      .then_inc(w_in, 16)

                def load_row(n):
                    e = n - SHARED
                    sp.wait_ge(row_used, e + 1)
                    sp.dma_start(wrow[:], w_dram[bass.ds(e, 1), :].to_broadcast([P, T])).then_inc(row_in, 16)

                load(0, 0)
                for dst, name in ((b1, "b1"), (b2, "b2"), (b3, "b3"), (ident, "ident")):
                    sp.dma_start(dst[:], A[name]).then_inc(c_in, 16)
                load(0, 1)
                load(0, 2)
                for n in range(1, SHARED):
                    for m in range(3):
                        load(n, m)
                with sp.Fori(SHARED, PASSES) as n:
                    load_row(n)
                    for m in range(3):
                        load(n, m)

            @block.tensor
            def _(pe):
                def quantised_turned(t, b):
                    pe.wait_ge(q_val_ready, t + 1)
                    for c in range(C):
                        tr = pe.transpose(bank[b][:, c * P:(c + 1) * P], q_val[:, c * P:(c + 1) * P], ident[:])
                    tr.then_inc(q_turned, 1)

                AFTER = {TURN_AT[s]: s for s in range(QS)}
                BEFORE = {TURN_AT[s] - TURN_BACK + FILLS: s for s in range(QS)}

                def products(n, m, tiles):
                    t0 = (1 + QS * (n - SHARED)) if tiles == QS else 0
                    first = isinstance(n, int) and n == 0
                    pe.wait_ge(w_lo[m], n + 1)
                    for k in range(FILLS):
                        f = FILLS * m + k
                        if BEFORE.get(f, QS) < tiles:
                            pe.wait_ge(q_copied, t0 + BEFORE[f] + 1)
                        if tiles == QS and f + 3 * FILLS in BEFORE:
                            pe.wait_ge(q_copied, t0)
                        if m == 2 and k % C == 0:
                            pe.wait_ge(hid_lo, FILLS * n + k + C)
                        if m > 0:
                            pe.wait_ge(free[m - 1], FILLS * n + k + 1)
                        elif not first:
                            pe.wait_ge(free[2], FILLS * (n - 1) + k + 1)
                        src = hid if m == 2 else xn
                        o = k % C
                        for c in range(C):
                            mm = product3(pe, bank[k][:], [x[:, c, o * P:(o + 1) * P] for x in w[m]],
                                          [x[:, c, ks(k)] for x in src], c == 0, c == C - 1)
                        mm.then_inc(full[m], 1)
                        s = AFTER.get(f, QS)
                        if s < tiles:
                            b = (f - TURN_BACK) % FILLS
                            pe.wait_ge(free[(f - TURN_BACK) // FILLS], FILLS * n + b + 1)
                            quantised_turned(t0 + s, b)

                pe.wait_ge(xn_lo, C)
                pe.wait_ge(c_in, 64)
                for n in range(SHARED):
                    for m in range(3):
                        products(n, m, int(n == SHARED - 1))
                with pe.Fori(SHARED, PASSES) as n:
                    for m in range(3):
                        products(n, m, QS)
                pe.wait_ge(q_copied, FFN_TILES)
                pe.wait_ge(y_added, FILLS * E + 1)
                for t in range(TILES):
                    for c in range(C):
                        tr = pe.transpose(bank[t][:, c * P:(c + 1) * P], Y[:, c, t * P:(t + 1) * P], ident[:])
                    tr.then_inc(turned, 1)

            @block.scalar
            def _(act):
                step = Steps(act, s_steps)

                def high(n, m):
                    act.wait_ge(w_in, 16 * (3 * n + m) + 16)
                    if not (isinstance(n, int) and n == 0):
                        act.wait_ge(full[m], FILLS * n)
                    act.activation(w[m][0][:], raw[:], ACT.Copy).then_inc(w_hi[m], 1)

                def hidden_high(n, k):
                    act.activation(hid[0][:, k % C, ks(k)], act_out[k % 2][:], ACT.Copy).then_inc(hid_hi, 1)

                def load_tile(t):
                    act.dma_start(q_raw[:], A["ffn_w"][bass.ds(t, 1)].rearrange("o p d -> (o p) d")).then_inc(q_in, 16)

                def magnitude(t, last=False):
                    act.wait_ge(q_y_ready, t + 1)
                    if not last:
                        load_tile(t + 1)
                    act.wait_ge(q_val_ready, t)
                    act.activation(q_mag[:], q_y[:], ACT.Abs)
                    act.activation(q_sign[:], q_y[:], ACT.Sign).then_inc(q_mag_ready, 1)

                def tile_out(t, s):
                    b = (TURN_AT[s] - TURN_BACK) % FILLS
                    act.wait_ge(q_turned, t + 1)
                    act.wait_ge(q_out, 16 * t)
                    act.activation(q_turn[:], bank[b][:], ACT.Copy).then_inc(q_copied, 1)
                    act.wait_ge(q_copied, t + 1)
                    act.dma_start(q_dram[bass.ds(t, 1)].rearrange("o p d -> (o p) d"), q_turn[:]).then_inc(q_out, 16)

                def shared(n):
                    for k in range(FILLS):
                        act.wait_ge(full[0], FILLS * n + k + 1)
                        act.activation(gated[:, k, :], bank[k][:], ACT.Silu).then_inc(free[0], 1)
                        if n == SHARED - 1 and k == 0:
                            magnitude(0)
                    if n == SHARED - 1:
                        tile_out(0, 0)
                    high(n, 2)
                    for k in range(FILLS):
                        act.wait_ge(act_ready, FILLS * n + k + 1)
                        hidden_high(n, k)
                    high(n + 1, 0)
                    high(n + 1, 1)

                def expert(n, last):
                    e = n - SHARED
                    t0 = 1 + QS * e
                    step.restart()
                    step(act.activation(b1_now[:], b1[:, bass.ds(e, 1), :].rearrange("p e c -> p (e c)"), ACT.Copy))
                    high(n, 2)
                    for k in range(FILLS):
                        act.wait_ge(act_ready, FILLS * n + k + 1)
                        act.wait_ge(hid_lo, FILLS * n + max(k - 1, 0))
                        step(act.activation(act_out[k % 2][:], scaled[k % 2][:], ACT.Silu,
                                            bias=b1_now[:, k % C:k % C + 1]))
                        hidden_high(n, k)
                        if k - 1 in SCALE_AT:
                            magnitude(t0 + SCALE_AT.index(k - 1))
                    tile_out(t0, 0)
                    if not last:
                        high(n + 1, 0)
                    magnitude(t0 + 2)
                    tile_out(t0 + 1, 1)
                    if not last:
                        high(n + 1, 1)
                    magnitude(t0 + 3, last)
                    tile_out(t0 + 2, 2)
                    tile_out(t0 + 3, 3)

                load_tile(0)
                for c in range(C):
                    act.activation(xn[0][:, c, :], XN3T[:, c, :], ACT.Copy).then_inc(xn_hi, 1)
                high(0, 0)
                high(0, 1)
                act.wait_ge(c_in, 64)
                for n in range(SHARED):
                    shared(n)
                with act.Fori(SHARED, PASSES - 1) as n:
                    expert(n, False)
                expert(PASSES - 1, True)
                act.wait_ge(q_out, 16 * FFN_TILES)

            @block.gpsimd
            def _(pool):
                step = Steps(pool, p_steps)

                def low(n, m):
                    pool.wait_ge(w_hi[m], n + 1)
                    pool.tensor_tensor(w[m][1][:], raw[:], cast(w[m][0][:]), ALU.subtract).then_inc(w_lo[m], 1)

                def hidden_low(n, k):
                    pool.wait_ge(hid_hi, FILLS * n + k + 1)
                    pool.tensor_tensor(hid[1][:, k % C, ks(k)], act_out[k % 2][:], cast(hid[0][:, k % C, ks(k)]),
                                       ALU.subtract).then_inc(hid_lo, 1)

                def tile_value(t):
                    pool.wait_ge(q_low_ready, t + 1)
                    pool.wait_ge(q_turned, t)
                    quant_value(pool, step, q_low[:], q_sign[:], q_half[:], D, q_val[:]).then_inc(q_val_ready, 1)

                def shared(n):
                    if n == SHARED - 1:
                        tile_value(0)
                    low(n, 2)
                    for k in range(FILLS):
                        hidden_low(n, k)
                    low(n + 1, 0)
                    low(n + 1, 1)

                def expert(n, last):
                    e = n - SHARED
                    t0 = 1 + QS * e
                    step.restart()
                    low(n, 2)
                    for k in range(FILLS):
                        hidden_low(n, k)
                        if k == SCALE_AT[1]:
                            tile_value(t0)
                    if not last:
                        low(n + 1, 0)
                    tile_value(t0 + 1)
                    if not last:
                        low(n + 1, 1)
                    tile_value(t0 + 2)
                    for k in range(FILLS):
                        pool.wait_ge(free[2], FILLS * n + k + 1)
                        y = Y[:, k % C, ks(k)]
                        pool.tensor_tensor(y, y, scaled[k % 2][:], ALU.add).then_inc(y_added, 1)
                        if k == VALUE_AT:
                            tile_value(t0 + 3)

                pool.sem_inc(y_added, 1)
                tokens_low(pool, range(C // 2))
                low(0, 1)
                for n in range(SHARED):
                    shared(n)
                with pool.Fori(SHARED, PASSES - 1) as n:
                    expert(n, False)
                expert(PASSES - 1, True)

            @block.vector
            def _(dve):
                step = Steps(dve, v_steps)

                def tile_scaled(t):
                    dve.wait_ge(q_in, 16 * t + 16)
                    dve.wait_ge(q_mag_ready, t)
                    quant_scaled(dve, step, q_raw[:], D, q_scale[:], q_inv[:], q_y[:]).then_inc(q_y_ready, 1)

                def tile_rounded(t):
                    dve.wait_ge(q_mag_ready, t + 1)
                    dve.wait_ge(q_val_ready, t)
                    step(halved(dve, q_scale[:], q_half[:]))
                    quant_rounded(dve, step, q_mag[:], q_low[:], q_high[:]).then_inc(q_low_ready, 1)

                def shared(n):
                    if n == SHARED - 1:
                        tile_scaled(0)
                        tile_rounded(0)
                    for k in range(FILLS):
                        dve.wait_ge(full[1], FILLS * n + k + 1)
                        dve.wait_ge(free[0], FILLS * n + k + 1)
                        dve.wait_ge(hid_lo, FILLS * n + max(k - 1, 0))
                        step(dve.tensor_tensor(act_out[k % 2][:], bank[k][:], gated[:, k, :], ALU.mult))
                        dve.sem_inc(act_ready, 1)
                        dve.sem_inc(free[1], 1)
                    for k in range(FILLS):
                        dve.wait_ge(full[2], FILLS * n + k + 1)
                        y = Y[:, k % C, ks(k)]
                        if n == 0:
                            dve.wait_ge(xn_lo, C)
                            dve.tensor_copy(y, bank[k][:]).then_inc(free[2], 1)
                        else:
                            dve.tensor_tensor(y, y, bank[k][:], ALU.add).then_inc(free[2], 1)

                def quantise(t0, f):
                    if f in SCALE_AT:
                        tile_scaled(t0 + SCALE_AT.index(f))
                    if f in ROUND_AT:
                        tile_rounded(t0 + ROUND_AT.index(f))

                def expert(n):
                    e = n - SHARED
                    t0 = 1 + QS * e
                    step.restart()
                    dve.wait_ge(row_in, 16 * e + 16)
                    step(dve.tensor_scalar(mask[:], wrow[:], 0.0, None, ALU.is_ge))
                    step(dve.tensor_scalar(weight[:], wrow[:], 0.0, None, ALU.max))
                    dve.sem_inc(row_used, 1)
                    for k in range(FILLS):
                        dve.wait_ge(full[0], FILLS * n + k + 1)
                        if k >= 2:
                            dve.wait_ge(hid_hi, FILLS * n + k - 1)
                        else:
                            dve.wait_ge(y_added, FILLS * e + 1)
                        step(dve.tensor_tensor(scaled[k % 2][:], bank[k][:], weight[:, ks(k)], ALU.mult))
                        dve.sem_inc(act_ready, 1)
                        dve.sem_inc(free[0], 1)
                        quantise(t0, k)
                    for k in range(FILLS):
                        dve.wait_ge(full[1], FILLS * n + k + 1)
                        g = gated[:, k, :]
                        dve.tensor_tensor(g, bank[k][:], weight[:, ks(k)], ALU.mult).then_inc(free[1], 1)
                        dve.wait_ge(free[1], FILLS * n + k + 1)
                        step(dve.scalar_tensor_tensor(out=g, in0=g,
                                                      scalar=b3[:, bass.ds(e, 1), k % C:k % C + 1].rearrange("p e c -> p (e c)"),
                                                      in1=mask[:, ks(k)], op0=ALU.add, op1=ALU.mult))
                        quantise(t0, 1 * FILLS + k)
                    for k in range(FILLS):
                        dve.wait_ge(full[2], FILLS * n + k + 1)
                        if k >= 2:
                            dve.wait_ge(y_added, FILLS * e + k)
                        else:
                            dve.wait_ge(hid_hi, FILLS * n + FILLS)
                        dve.scalar_tensor_tensor(out=scaled[k % 2][:], in0=bank[k][:],
                                                 scalar=b2[:, bass.ds(e, 1), k % C:k % C + 1].rearrange("p e c -> p (e c)"),
                                                 in1=gated[:, k, :], op0=ALU.add, op1=ALU.mult).then_inc(free[2], 1)
                        quantise(t0, 2 * FILLS + k)

                dve.sem_inc(row_used, 1)
                tokens_low(dve, range(C // 2, C))
                dve.wait_ge(w_hi[0], 1)
                dve.tensor_tensor(w[0][1][:], raw[:], cast(w[0][0][:]), ALU.subtract).then_inc(w_lo[0], 1)
                dve.wait_ge(c_in, 64)
                for n in range(SHARED):
                    shared(n)
                with dve.Fori(SHARED, PASSES) as n:
                    expert(n)
                for t in range(TILES):
                    dve.wait_ge(turned, t + 1)
                    dve.tensor_tensor(X[:, t, :], X[:, t, :], bank[t][:], ALU.add).then_inc(x_added, 1)




CROSS = ["xT4", "g", "s", "pT", "o", "oT", "z"]
SELF = ["xT5", "qkv", "s2", "pT2", "zT", "z2"]
STAGES = ["xT4", "norm5", "g", "xT5", "hide", "s", "qkv", "p", "s2", "pT", "p2", "pT2", "o", "zT", "stat4", "oT", "z2", "norm4", "z"]
OF_SELF = SELF + ["norm5", "p2"]
PAIRS = TILES // 2
HIDDEN = -1e38


def phase_c(nc, A, X, XN3T, prefetch):
    with ExitStack() as ctx:
        sb = lambda n, s, d=F32: ctx.enter_context(nc.sbuf_tensor("pc_" + n, s, d))
        two = lambda n, s, d=F32: [sb(f"{n}{r}", s, d) for r in range(2)]
        four = lambda n, s, d=F32: [sb(f"{n}{r}", s, d) for r in range(4)]
        late = lambda n, s, d=F32: [None] * 2 + [sb(f"{n}{r}", s, d) for r in range(2, 4)]
        sem = lambda n: ctx.enter_context(nc.semaphore("c_" + n))
        sems = lambda n: [sem(f"{n}{r}") for r in range(4)]
        wq, wk = (XN3T[:, :, m * D:(m + 1) * D] for m in range(2))
        wv, wo, wqk, wvo = (sb(n, [P, C, D]) for n in ("wv", "wo", "wqk", "wvo"))
        bq, bk, bv = (sb(n, [P, C]) for n in ("bq", "bk", "bv"))
        bq_wide, bv_wide = sb("bq_wide", [P, C, P]), sb("bv_wide", [P, C, P])
        g_b, k_b, row_b = sb("g_b", [P, C]), sb("k_b", [P, C]), sb("row_b", [P, 1])
        bo, bo2 = sb("bo", [P, D]), sb("bo2", [P, D])
        ident = sb("ident", [P, P])
        aq, ak, av = (sb(n, [P, C, HK]) for n in ("aq", "ak", "av"))
        ao = sb("ao", [HK, D])
        aqk_b = sb("aqk_b", [HK, 2])
        av_b = sb("av_b", [HK, 1])
        causal = sb("causal", [P, P])
        own_batch = sb("own_batch", [P, TILES, B])
        ctx_tail = sb("ctx_tail", [B, D])
        ctxT = two("ctxT", [P, BT, C, LK])
        keys = two("keys", [P, BT, KH, D])
        mask = two("mask", [P, LK], I32)
        hidden = two("hidden", [P, LK])
        stats, mv, veps, rstd = four("stats", [P, 6]), four("mv", [P, 2]), four("veps", [P, 1]), four("rstd", [P, 1])
        xn, xnT = four("xn", [P, D]), four("xnT", [P, C, P])
        gT = two("gT", [P, C, P])
        krow = two("krow", [P, 1])
        logit = two("logit", [P, LK]) + [sb(f"logit{r}", [P, P]) for r in (2, 3)]
        prob = two("prob", [P, LK]) + [sb(f"prob{r}", [P, P]) for r in (2, 3)]
        nmax, total, inv = four("nmax", [P, 1]), four("total", [P, 1]), four("inv", [P, 1])
        pn = two("pn", [P, KH * P + B]) + [sb(f"pn{r}", [P, P]) for r in (2, 3)]
        pT, pTtail = two("pT", [P, KH * P]) + [sb(f"pT{r}", [P, P]) for r in (2, 3)], two("pTtail", [B, P])
        o, oT = two("o", [P, D]), two("oT", [P, C, P])
        qk, va = late("qk", [HK, 2, P]), late("va", [P, HK])
        zT = late("zT", [HK, P])
        eps, mhalf = sb("eps", [P, 1]), sb("mhalf", [P, 1])
        fence = four("fence", [P, 1])
        bank = [ctx.enter_context(nc.psum_tensor(f"pc{b}", [P, 512], F32)) for b in range(8)]

        w_first, w_in = sem("w_first"), sem("w_in")
        wide = sem("wide")
        w_full, w_ready = sem("w_full"), sem("w_ready")
        b_full, b_ready = sem("b_full"), sem("b_ready")
        init = sem("init")
        ctx_in = sems("ctx_in")
        mv_ready, rstd_ready, xn_ready = sems("mv"), sems("rstd"), sems("xn")
        full, freed = sems("full"), sems("freed")
        l_ready, p_ready, pn_ready = sems("l"), sems("p"), sems("pn")
        v_steps, s_steps, p_steps = sem("vsteps"), sem("ssteps"), sem("psteps")

        scale = float(D) ** -0.5
        scale2 = float(HK) ** -0.5
        first_consts = [(ident, "ident"), (wq, "l1_wq"), (bq, "l1_bq"), (wk, "l1_wk"), (bk, "l1_bk"),
                        (bv, "l1_bv")]
        consts = [(own_batch, "own_batch"), (ctx_tail, "ctx_tail_rows"), (wv, "l1_wv"), (wo, "l1_wo"), (bo, "l1_bo"), (bo2, "s_bo"), (aq, "s_wq"), (ak, "s_wk"),
                  (av, "s_wv"), (ao, "s_wo"), (aqk_b, "s_bqk"), (av_b, "s_bv"), (causal, "causal")]

        def turn(i, name):
            fills = SELF if name in SELF else CROSS
            return len(fills) * i + fills.index(name)

        def iterations(eng, body):
            body(0, own=True, past=False)
            with eng.Fori(1, PAIRS) as i:
                body(i, own=True, past=True)
            body(PAIRS, own=False, past=True)

        def each(stage, i, own, past):
            for name in STAGES:
                if name in OF_SELF:
                    if past:
                        for r in (2, 3):
                            stage(name, i - 1, r)
                elif own:
                    for r in (0, 1):
                        stage(name, i, r)

        with nc.Block() as block:

            @block.sync
            def _(sp):
                def load(i, r):
                    t = 2 * i + r
                    sp.dma_start(ctxT[r][:], A["ctxT"][bass.ds(BT * t, BT)].rearrange("j p c k -> p j c k"))\
                      .then_inc(ctx_in[r], 16)
                    for j in range(BT):
                        sp.dma_start(keys[r][:, j], A["ctx"][bass.ds(BT * t + j, 1), 0:KH * P, :]
                                     .rearrange("o (h p) d -> p (o h) d", p=P)).then_inc(ctx_in[r], 16)
                    sp.dma_start(mask[r][:], A["mask"][bass.ds(t, 1)].rearrange("o p k -> (o p) k")).then_inc(ctx_in[r], 16)

                for dst, name in first_consts:
                    sp.dma_start(dst if name in ("l1_wq", "l1_wk") else dst[:], A[name]).then_inc(w_first, 16)
                load(0, 0)
                load(0, 1)
                for dst, name in consts:
                    sp.dma_start(dst[:], A[name]).then_inc(w_in, 16)
                sp.wait_ge(b_full, 1)
                with sp.Fori(1, PAIRS) as i:
                    for r in range(2):
                        sp.wait_ge(freed[r], turn(i - 1, "o") + 2)
                        load(i, r)
                prefetch(sp)

            @block.tensor
            def _(pe):
                def take(i, r, name):
                    pe.wait_ge(freed[r], turn(i, name) + 1)

                def transposes(i, r, name, src):
                    take(i, r, name)
                    for c in range(C):
                        tr = pe.transpose(bank[r][:, c * P:(c + 1) * P], src[:, c * P:(c + 1) * P], ident[:])
                    tr.then_inc(full[r], 1)

                def narrow(i, r, name, w, src):
                    take(i, r, name)
                    for n in range(C):
                        for c in range(C):
                            mm = pe.matmul(bank[r][:, n * P:(n + 1) * P], w[:, c, n * P:(n + 1) * P], src[:, c, :],
                                           start=c == 0, stop=c == C - 1)
                    mm.then_inc(full[r], 1)

                def weights_product(left, right):
                    for n in range(C):
                        for c in range(C):
                            mm = pe.matmul(bank[4 + n][:], left[:, c, n * P:(n + 1) * P], right[:, c, :],
                                           start=c == 0, stop=c == C - 1)
                        mm.then_inc(w_full, 1)

                def first_products():
                    weights_product(wq, wk)
                    for col, w, b in ((0, wk, bq), (C, wq, bk)):
                        for n in range(C):
                            for c in range(C):
                                pe.matmul(bank[3][:, col + n:col + n + 1], w[:, c, n * P:(n + 1) * P], b[:, c:c + 1],
                                          start=c == 0, stop=c == C - 1)
                    pe.wait_ge(wide, 2)
                    for c in range(C):
                        mm = pe.matmul(bank[3][:, 2 * C:2 * C + 1], bq_wide[:, c, :], bk[:, c:c + 1],
                                       start=c == 0, stop=c == C - 1)
                    mm.then_inc(b_full, 1)

                def second_products():
                    pe.wait_ge(w_in, 16 * len(consts))
                    pe.wait_ge(w_ready, C)
                    weights_product(wv, wo)
                    for c in range(C):
                        mm = pe.matmul(bank[2][:], bv_wide[:, c, :], wo[:, c, :], start=c == 0, stop=c == C - 1)
                    mm.then_inc(b_full, 1)

                def stage(name, i, r):
                    ps = bank[r]
                    if name == "xT4":
                        pe.wait_ge(xn_ready[r], i + 1)
                        transposes(i, r, name, xn[r])
                    if name == "g":
                        if isinstance(i, int) and i == 0:
                            pe.wait_ge(w_ready, C)
                        narrow(i, r, name, wqk, xnT[r])
                    if name == "s":
                        take(i, r, name)
                        pe.wait_ge(b_ready, 2)
                        pe.wait_ge(ctx_in[r], 16 * (BT + 2) * i + 16 * (BT + 2))
                        for c in range(C):
                            pe.matmul(ps[:, 300:301], xnT[r][:, c, :], k_b[:, c:c + 1], start=c == 0, stop=c == C - 1)
                        for c in range(C):
                            for j in range(BT):
                                mm = pe.matmul(ps[j * LQ:(j + 1) * LQ, 0:LK], gT[r][:, c, j * LQ:(j + 1) * LQ],
                                               ctxT[r][:, j, c, :], start=c == 0, stop=c == C - 1,
                                               tile_position=(0, j * LQ))
                        mm.then_inc(full[r], 1)
                    if name == "pT":
                        if isinstance(i, int) and i == 0 and r == 0:
                            second_products()
                        pe.wait_ge(pn_ready[r], i + 1)
                        take(i, r, name)
                        pe.transpose(ps[:, 0:P], pn[r][:, 0:P], ident[:])
                        pe.transpose(ps[:, P:2 * P], pn[r][:, P:2 * P], ident[:])
                        pe.transpose(ps[0:B, 2 * P:3 * P], pn[r][:, 2 * P:], ident[:]).then_inc(full[r], 1)
                    if name == "o":
                        take(i, r, name)
                        pe.matmul(ps[:], pTtail[r][:], ctx_tail[:], start=True, stop=False, skip_group_check=True)
                        for h in range(KH):
                            for j in range(BT):
                                mm = pe.matmul(ps[j * LQ:(j + 1) * LQ, :], pT[r][:, h * P + j * LQ:h * P + (j + 1) * LQ],
                                               keys[r][:, j, h, :], start=False, stop=h == KH - 1,
                                               tile_position=(0, j * LQ), skip_group_check=True)
                        mm.then_inc(full[r], 1)
                    if name == "oT":
                        transposes(i, r, name, o[r])
                    if name == "z":
                        if isinstance(i, int) and i == 0:
                            pe.wait_ge(w_ready, 2 * C)
                        take(i, r, name)
                        for c in range(C):
                            mm = pe.matmul(ps[:], oT[r][:, c, :], wvo[:, c, :], start=c == 0, stop=c == C - 1)
                        mm.then_inc(full[r], 1)
                    if name == "xT5":
                        pe.wait_ge(b_ready, 3)
                        pe.wait_ge(xn_ready[r], i + 1)
                        transposes(i, r, name, xn[r])
                    if name == "qkv":
                        take(i, r, name)
                        for w, col in ((aq, 0), (ak, P)):
                            for c in range(C):
                                pe.matmul(ps[0:HK, col:col + P], w[:, c, :], xnT[r][:, c, :], start=c == 0, stop=c == C - 1)
                        for c in range(C):
                            mm = pe.matmul(ps[:, 2 * P:2 * P + HK], xnT[r][:, c, :], av[:, c, :], start=c == 0, stop=c == C - 1)
                        mm.then_inc(full[r], 1)
                    if name == "s2":
                        take(i, r, name)
                        pe.matmul(ps[:, 0:P], qk[r][:, 0, :], qk[r][:, 1, :], start=True, stop=True).then_inc(full[r], 1)
                    if name == "pT2":
                        pe.wait_ge(pn_ready[r], i + 1)
                        take(i, r, name)
                        pe.transpose(ps[:, 0:P], pn[r][:, 0:P], ident[:]).then_inc(full[r], 1)
                    if name == "zT":
                        take(i, r, name)
                        pe.matmul(ps[0:HK, 0:P], va[r][:], pT[r][:, 0:P], start=True, stop=True).then_inc(full[r], 1)
                    if name == "z2":
                        take(i, r, name)
                        pe.matmul(ps[:], zT[r][:], ao[:], start=True, stop=True).then_inc(full[r], 1)

                pe.wait_ge(w_first, 16 * len(first_consts))
                first_products()
                iterations(pe, lambda i, own, past: each(stage, i, own, past))

            @block.scalar
            def _(act):
                def stage(name, i, r):
                    ps = bank[r]
                    if name == "s":
                        act.wait_ge(l_ready[r], i + 1)
                        act.activation(prob[r][:], logit[r][:], ACT.Exp, bias=nmax[r][:],
                                       accum_out=total[r][:]).then_inc(p_ready[r], 1)
                    if name == "pT":
                        act.wait_ge(full[r], turn(i, name) + 1)
                        act.activation(pT[r][:], ps[:, 0:KH * P], ACT.Copy)
                        act.activation(pTtail[r][:], ps[0:B, KH * P:KH * P + P], ACT.Copy).then_inc(freed[r], 1)
                    if name == "o":
                        act.wait_ge(full[r], turn(i, name) + 1)
                        act.activation(o[r][:], ps[:], ACT.Copy).then_inc(freed[r], 1)
                    if name == "s2":
                        act.wait_ge(l_ready[r], i + 1)
                        act.activation(prob[r][:, 0:P], logit[r][:, 0:P], ACT.Exp, bias=nmax[r][:],
                                       accum_out=total[r][:]).then_inc(p_ready[r], 1)
                    if name == "pT2":
                        act.wait_ge(full[r], turn(i, name) + 1)
                        act.activation(pT[r][:, 0:P], ps[:, 0:P], ACT.Copy).then_inc(freed[r], 1)

                iterations(act, lambda i, own, past: each(stage, i, own, past))

            @block.gpsimd
            def _(pool):
                step = Steps(pool, p_steps)

                def inverse_deviation(n, r):
                    pool.wait_ge(mv_ready[r], n + 1)
                    step(pool.tensor_tensor(veps[r][:], mv[r][:, 1:2], eps[:], ALU.add))
                    pool.tensor_tensor(rstd[r][:], veps[r][:], mhalf[:], ALU.pow).then_inc(rstd_ready[r], 1)

                pool.wait_ge(init, 2)
                def iteration(i, own, past):
                    step.restart()
                    if past:
                        for r in (2, 3):
                            inverse_deviation(i - 1, r)
                    if own and not (isinstance(i, int) and i == PAIRS - 1):
                        for r in (0, 1):
                            inverse_deviation(i + 1, r)

                step.restart()
                for r in (0, 1):
                    inverse_deviation(0, r)
                iteration(0, True, False)
                with pool.Fori(1, PAIRS - 1) as i:
                    iteration(i, True, True)
                iteration(PAIRS - 1, True, True)
                iteration(PAIRS, False, True)

            @block.vector
            def _(dve):
                step = Steps(dve, v_steps)

                def tile_of_x(i, r):
                    return X[:, bass.ds(2 * i + r % 2, 1), :].rearrange("p o d -> p (o d)")

                def filled(i, r, name):
                    dve.wait_ge(full[r], turn(i, name) + 1)

                def statistics(i, r):
                    step(dve.memset(fence[r][:], 0.0))
                    step(dve.bn_stats(stats[r][:], tile_of_x(i, r)))
                    dve.bn_aggr(mv[r][:], stats[r][:]).then_inc(mv_ready[r], 1)

                def normalise(i, r):
                    dve.wait_ge(rstd_ready[r], i + 1)
                    dve.tensor_scalar(xn[r][:], tile_of_x(i, r), mv[r][:, 0:1], rstd[r][:],
                                      ALU.subtract, ALU.mult).then_inc(xn_ready[r], 1)

                def add_product(i, r, name, bias):
                    filled(i, r, name)
                    x = tile_of_x(i, r)
                    dve.tensor_tensor(x, ps_of(r), x, ALU.add).then_inc(freed[r], 1)
                    dve.wait_ge(freed[r], turn(i, name) + 2)
                    step(dve.tensor_tensor(x, x, bias[:], ALU.add))

                def ps_of(r):
                    return bank[r][:]

                def chunks(ap):
                    return ap.rearrange("p (c t) -> p c t", c=C)

                def per_chunk(b):
                    return b[:].rearrange("p (c o) -> p c o", o=1).to_broadcast([P, C, P])

                def weights_out(dst, n, factor):
                    for c in range(C):
                        dve.wait_ge(w_full, C * n + c + 1)
                        dve.tensor_scalar(dst[:, c, :], bank[4 + c][:], factor, None, ALU.mult).then_inc(w_ready, 1)

                def stage(name, i, r):
                    ps = bank[r]
                    if name == "norm5":
                        normalise(i, r)
                    if name == "hide":
                        dve.wait_ge(ctx_in[r], 16 * (BT + 2) * i + 16 * (BT + 2))
                        step(dve.tensor_scalar(hidden[r][:], mask[r][:], 0.0, HIDDEN, ALU.is_equal, ALU.mult))
                    if name in ("xT4", "xT5"):
                        filled(i, r, name)
                        dve.tensor_copy(xnT[r][:].rearrange("p c t -> p (c t)"), ps[:]).then_inc(freed[r], 1)
                    if name == "g":
                        filled(i, r, name)
                        dve.tensor_tensor(gT[r][:], chunks(ps[:]), per_chunk(g_b), ALU.add).then_inc(freed[r], 1)
                    if name == "s":
                        filled(i, r, name)
                        step(dve.tensor_scalar(krow[r][:], ps[:, 300:301], row_b[:], scale, ALU.add, ALU.mult))
                        dve.scalar_tensor_tensor(out=logit[r][:], in0=ps[:, 0:LK], scalar=krow[r][:], in1=hidden[r][:],
                                                 op0=ALU.add, op1=ALU.add).then_inc(freed[r], 1)
                        dve.wait_ge(freed[r], turn(i, name) + 2)
                        dve.tensor_reduce(nmax[r][:], logit[r][:], AX.X, ALU.max, negate=True).then_inc(l_ready[r], 1)
                    if name == "p":
                        if isinstance(i, int) and i == 0:
                            dve.wait_ge(w_in, 16 * len(consts))
                        dve.wait_ge(p_ready[r], i + 1)
                        step(dve.scalar_tensor_tensor(out=total[r][:], in0=nmax[r][:], scalar=-HIDDEN / 10,
                                                      in1=total[r][:], op0=ALU.is_lt, op1=ALU.mult))
                        step(dve.reciprocal(inv[r][:], total[r][:]))
                        step(dve.tensor_scalar(pn[r][:, KH * P:], own_batch[:, bass.ds(2 * i + r, 1), :].rearrange("p o b -> p (o b)"),
                                               prob[r][:, KH * P:LK], inv[r][:], ALU.mult, ALU.mult))
                        dve.tensor_scalar(pn[r][:, 0:KH * P], prob[r][:, 0:KH * P], inv[r][:], None, ALU.mult)\
                           .then_inc(pn_ready[r], 1)
                        if isinstance(i, int) and i == 0 and r == 1:
                            weights_out(wvo, 1, 1.0)
                            dve.wait_ge(b_full, 2)
                            step(dve.tensor_tensor(bo[:], bank[2][:], bo[:], ALU.add))
                            dve.sem_inc(b_ready, 1)
                    if name == "oT":
                        filled(i, r, name)
                        dve.tensor_copy(oT[r][:].rearrange("p c t -> p (c t)"), ps[:]).then_inc(freed[r], 1)
                    if name == "z":
                        add_product(i, r, name, bo)
                        statistics(i, r + 2)
                    if name == "qkv":
                        filled(i, r, name)
                        step(dve.tensor_tensor(qk[r][:], ps[0:HK, 0:2 * P].rearrange("p (n t) -> p n t", n=2),
                                               aqk_b[:].rearrange("p (n o) -> p n o", o=1).to_broadcast([HK, 2, P]), ALU.add))
                        dve.tensor_copy(va[r][:], ps[:, 2 * P:2 * P + HK]).then_inc(freed[r], 1)
                    if name == "s2":
                        filled(i, r, name)
                        dve.scalar_tensor_tensor(out=logit[r][:, 0:P], in0=ps[:, 0:P], scalar=scale2, in1=causal[:],
                                                 op0=ALU.mult, op1=ALU.add).then_inc(freed[r], 1)
                        dve.wait_ge(freed[r], turn(i, name) + 2)
                        dve.tensor_reduce(nmax[r][:], logit[r][:, 0:P], AX.X, ALU.max, negate=True).then_inc(l_ready[r], 1)
                    if name == "p2":
                        dve.wait_ge(p_ready[r], i + 1)
                        step(dve.reciprocal(inv[r][:], total[r][:]))
                        dve.tensor_scalar(pn[r][:, 0:P], prob[r][:, 0:P], inv[r][:], None, ALU.mult).then_inc(pn_ready[r], 1)
                    if name == "zT":
                        filled(i, r, name)
                        dve.tensor_scalar(zT[r][:], ps[0:HK, 0:P], av_b[:], None, ALU.add).then_inc(freed[r], 1)
                    if name == "z2":
                        add_product(i, r, name, bo2)

                for r in range(4):
                    dve.sem_inc(freed[r], 1)
                dve.memset(eps[:], 1e-5).then_inc(init, 1)
                dve.memset(mhalf[:], -0.5).then_inc(init, 1)
                dve.wait_ge(w_first, 16 * len(first_consts))
                for dst, b in ((bq_wide, bq), (bv_wide, bv)):
                    dve.tensor_copy(dst[:], per_chunk(b)).then_inc(wide, 1)
                def iteration(i, own, past, nxt):
                    def at(name, i, r):
                        if name in ("stat4", "norm4"):
                            if nxt and name == "stat4":
                                statistics(i + 1, r)
                            elif nxt:
                                normalise(i + 1, r)
                        else:
                            stage(name, i, r)

                    step.restart()
                    each(at, i, own, past)

                for r in (0, 1):
                    statistics(0, r)
                for r in (0, 1):
                    normalise(0, r)
                weights_out(wqk, 0, scale)
                dve.wait_ge(b_full, 1)
                step(dve.tensor_scalar(g_b[:], bank[3][:, 0:C], scale, None, ALU.mult))
                step(dve.tensor_copy(k_b[:], bank[3][:, C:2 * C]))
                step(dve.tensor_copy(row_b[:], bank[3][:, 2 * C:2 * C + 1]))
                dve.sem_inc(b_ready, 2)
                iteration(0, True, False, True)
                with dve.Fori(1, PAIRS - 1) as i:
                    iteration(i, True, True, True)
                iteration(PAIRS - 1, True, True, False)
                iteration(PAIRS, False, True, False)



PIECES = 4
PW = FF // PIECES
SUM_AFTER = 6
PIECE_AFTER = (3, 4, 7)
FILLS_T = [list(range(f, min(f + 4, FC))) for f in range(0, FC, 4)]
NF = len(FILLS_T)


def raw_chunks(XN3T):
    flat = XN3T[:].rearrange("p c t -> p (c t)")
    return [flat[:, r * 3 * D:(r + 1) * 3 * D].rearrange("p (m d) -> p m d", m=3) for r in range(2)]


def load_chunk(sp, q_dram, raw, a, done):
    sp.dma_start(raw, q_dram[bass.ds(3 * a, 3)].rearrange("m p d -> p m d")).then_inc(done, 16)


def phase_d(nc, A, X, XN3T, q_dram, out, raw_in):
    with ExitStack() as ctx:
        sb = lambda n, s, d=F32: ctx.enter_context(nc.sbuf_tensor("pd_" + n, s, d))
        sems = []

        def sem(n):
            sems.append(ctx.enter_context(nc.semaphore("d_" + n)))
            return sems[-1]

        wgu = [sb("wgu_hi", [P, 2, C, FF], F32R), sb("wgu_lo", [P, 2, C, FF], F32R)]
        wd = [sb("wd_hi", [P, FC, D], F32R), sb("wd_lo", [P, FC, D], F32R)]
        hT = [sb("hT_hi", [P, FC, P], F32R), sb("hT_lo", [P, FC, P], F32R)]
        hT_raw = sb("hT_raw", [P, FC, P])
        xT = [sb("xT_hi", [P, C, P], F32R), sb("xT_lo", [P, C, P], F32R)]
        flat = XN3T[:].rearrange("p c t -> p (c t)")
        h, hy = flat[:, 0:FF], flat[:, FF:2 * FF]
        xn, xy = flat[:, 6 * D:7 * D], flat[:, 7 * D:8 * D]
        hval = sb("hval", [P, FF])
        raw = [(q[:, 0:2, :], q[:, 2, :]) for q in raw_chunks(XN3T)]
        raw += [(hval[:, 0:2 * D].rearrange("p (m d) -> p m d", m=2), hT_raw[:, 0:C, :].rearrange("p c o -> p (c o)"))]
        hsign, low, high = (sb(n, [P, FF], BF16) for n in ("hsign", "low", "high"))
        xsign, xlow, xhigh = (sb(n, [P, D], BF16) for n in ("xsign", "xlow", "xhigh"))
        hscale, hhalf, hinv = (sb(n, [P, FF // BLK]) for n in ("hscale", "hhalf", "hinv"))
        xscale, xinv = sb("xscale", [P, D // BLK]), sb("xinv", [P, D // BLK])
        silu = [sb(f"silu{r}", [P, PW]) for r in range(2)]
        ident = sb("ident", [P, P])
        stats, mv, veps, rstd = sb("stats", [P, 6]), sb("mv", [P, 2]), sb("veps", [P, 1]), sb("rstd", [P, 1])
        minus_last = sb("minus_last", [P, 1])
        eps, mhalf, fence = sb("eps", [P, 1]), sb("mhalf", [P, 1]), sb("fence", [P, 1])
        bank = [ctx.enter_context(nc.psum_tensor(f"pd{b}", [P, 512], F32)) for b in range(8)]
        g_ps, u_ps, ht_ps, xt_ps, d_ps = bank[0:2], bank[2:4], bank[4:6], bank[6], bank[7]

        c_in, init, third_in = sem("c_in"), sem("init"), sem("third_in")
        w_hi, g_lo, w_lo = sem("w_hi"), sem("g_lo"), sem("w_lo")
        mv_ready, rstd_ready = sem("mv"), sem("rstd")
        xy_ready, xmag_ready, xval_ready = sem("xy"), sem("xmag"), sem("xval")
        xt_full, xt_hi, xt_lo = sem("xt_full"), sem("xt_hi"), sem("xt_lo")
        g_full, u_full, silu_ready, h_piece = sem("g_full"), sem("u_full"), sem("silu"), sem("h_piece")
        hy_ready, hmag_ready, hval_ready = sem("hy"), sem("hmag"), sem("hval")
        hbegun_ready = sem("hbegun")
        xlow_ready, hlow_ready = sem("xlow"), sem("hlow")
        ht_full, ht_hi, ht_lo = sem("ht_full"), sem("ht_hi"), sem("ht_lo")
        d_full, x_done, x_out = sem("d_full"), sem("x_done"), sem("x_out")
        v_steps, s_steps, p_steps = sem("vsteps"), sem("ssteps"), sem("psteps")

        def all_steps(eng, body):
            body(0, True, True, True, False)
            with eng.Fori(1, TILES - 2) as i:
                body(i, True, True, True, True)
            body(TILES - 2, False, True, True, True)
            body(TILES - 1, False, False, True, True)
            body(TILES, False, False, False, True)

        def all_chunks(eng, body, after_first=lambda: None):
            R = len(raw)
            body(0, 0, 0)
            after_first()
            for r in range(1, R):
                body(r, r, 0)
            with eng.Fori(1, FC // R) as b:
                for r in range(R):
                    body(R * b + r, r, b)
            for a in range(FC - FC % R, FC):
                body(a, a % R, a // R)

        with nc.Block() as block:

            @block.sync
            def _(sp):
                for s in sems:
                    sp.sem_clear(s)

        with nc.Block() as block:

            @block.sync
            def _(sp):
                def load(a, r, b):
                    if isinstance(a, int) and a < 2:
                        return
                    if not (isinstance(a, int) and a < 3):
                        sp.wait_ge(g_lo, a - 2)
                        sp.wait_ge(w_lo, a - 2)
                    if r < 2:
                        load_chunk(sp, q_dram, raw_chunks(XN3T)[r], a, raw_in[r])
                    else:
                        gate_up, down = raw[r]
                        sp.dma_start(gate_up, q_dram[bass.ds(3 * a, 2)].rearrange("m p d -> p m d")).then_inc(third_in, 16)
                        sp.dma_start(down, q_dram[bass.ds(3 * a + 2, 1)].rearrange("m p d -> p (m d)")).then_inc(third_in, 16)

                sp.dma_start(ident[:], A["ident"]).then_inc(c_in, 16)
                all_chunks(sp, load)
                with sp.Fori(0, TILES) as t:
                    sp.wait_ge(x_done, t + 2)
                    sp.dma_start(out[bass.ds(t, 1)].rearrange("o p d -> (o p) d"),
                                 X[:, bass.ds(t, 1), :].rearrange("p o d -> p (o d)")).then_inc(x_out, 16)
                sp.wait_ge(x_out, 16 * TILES)

            @block.tensor
            def _(pe):
                def gate_up(i, p):
                    n = PIECES * i + p
                    if p == 0:
                        pe.wait_ge(xt_lo, i + 1)
                    if isinstance(i, int) and i == 0:
                        need = -(-PW * (p + 1) // P)
                        pe.wait_ge(g_lo, need)
                        pe.wait_ge(w_lo, need)
                    cols = slice(p * PW, (p + 1) * PW)
                    for m, ps, full, free in ((0, g_ps, g_full, silu_ready), (1, u_ps, u_full, h_piece)):
                        pe.wait_ge(free, n if p == 0 else n - 1)
                        for c in range(C):
                            mm = product3(pe, ps[p % 2][:, 0:PW], [x[:, c, :] for x in xT],
                                          [w[:, m, c, cols] for w in wgu], c == 0, c == C - 1)
                        mm.then_inc(full, 1)

                def hidden_transposed(i):
                    pe.wait_ge(hval_ready, i + 1)
                    for f, chunks in enumerate(FILLS_T):
                        n = NF * i + f
                        pe.wait_ge(ht_hi, n + 1 if f == 0 else n)
                        for s, k in enumerate(chunks):
                            tr = pe.transpose(ht_ps[f % 2][:, s * P:(s + 1) * P], hval[:, k * P:(k + 1) * P], ident[:])
                        tr.then_inc(ht_full, 1)

                def down(i):
                    pe.wait_ge(ht_lo, NF * i + NF)
                    pe.wait_ge(x_done, i + 1)
                    for k in range(FC):
                        mm = product3(pe, d_ps[:], [x[:, k, :] for x in hT], [w[:, k, :] for w in wd], k == 0, k == FC - 1)
                    mm.then_inc(d_full, 1)

                def tokens_transposed(i):
                    pe.wait_ge(xval_ready, i + 1)
                    pe.wait_ge(xt_lo, i)
                    for c in range(C):
                        tr = pe.transpose(xt_ps[:, c * P:(c + 1) * P], xy[:, c * P:(c + 1) * P], ident[:])
                    tr.then_inc(xt_full, 1)

                def step_of(i, second, nxt, cur, prev):
                    if nxt:
                        tokens_transposed(i + 1)
                        gate_up(i + 1, 0)
                    if prev:
                        hidden_transposed(i - 1)
                    if nxt:
                        gate_up(i + 1, 1)
                    if prev:
                        down(i - 1)
                    if nxt:
                        gate_up(i + 1, 2)
                        gate_up(i + 1, 3)

                pe.sem_inc(d_full, 1)
                pe.sem_inc(ht_full, 1)
                pe.wait_ge(c_in, 16)
                tokens_transposed(0)
                for p in range(PIECES):
                    gate_up(0, p)
                all_steps(pe, step_of)

            @block.scalar
            def _(act):
                step = Steps(act, s_steps)

                def chunk(a, r, b):
                    gate_up, down = raw[r]
                    count = b + 1
                    if r < 2:
                        act.wait_ge(raw_in[r], 16 * count)
                    else:
                        act.wait_ge(third_in, 32 * count)
                    act.activation(wgu[0][:, :, :, bass.ds(P * a, P)], gate_up.rearrange("p m (c o) -> p m c o", c=C),
                                   ACT.Copy)
                    act.activation(wd[0][:, bass.ds(a, 1), :].rearrange("p o d -> p (o d)"), down, ACT.Copy)\
                       .then_inc(w_hi, 1)

                def magnitudes(i, y_ready, y, sign, mag_ready):
                    act.wait_ge(y_ready, i + 1)
                    step(act.activation(sign, y, ACT.Sign))
                    act.activation(y, y, ACT.Abs).then_inc(mag_ready, 1)

                def hidden_begun(i):
                    magnitudes(i, hy_ready, hy, hsign[:], hmag_ready)
                    act.wait_ge(hmag_ready, i + 1)
                    step(act.activation(high[:], hy, ACT.Sign, bias=minus_last[:]))
                    act.activation(high[:], high[:], ACT.Relu, scale=2.0).then_inc(hbegun_ready, 1)

                def x_magnitudes(i):
                    magnitudes(i, xy_ready, xy, xsign[:], xmag_ready)

                def silu_of(i, p):
                    n = PIECES * i + p
                    act.wait_ge(g_full, n + 1)
                    act.wait_ge(h_piece, n if p == 0 else n - 1)
                    act.activation(silu[p % 2][:], g_ps[p % 2][:, 0:PW], ACT.Silu).then_inc(silu_ready, 1)

                def tokens_high(i):
                    act.wait_ge(xt_full, i + 1)
                    act.wait_ge(u_full, PIECES * i)
                    act.activation(xT[0][:].rearrange("p c t -> p (c t)"), xt_ps[:], ACT.Copy).then_inc(xt_hi, 1)

                def hidden_high(i):
                    act.wait_ge(d_full, i + 1)
                    for f, chunks in enumerate(FILLS_T):
                        act.wait_ge(ht_full, NF * i + f + 2)
                        for dst in (hT[0], hT_raw):
                            cp = act.activation(dst[:, chunks[0]:chunks[-1] + 1, :].rearrange("p k t -> p (k t)"),
                                                ht_ps[f % 2][:, 0:P * len(chunks)], ACT.Copy)
                        cp.then_inc(ht_hi, 1)

                def step_of(i, second, nxt, cur, prev):
                    step.restart()
                    if nxt:
                        tokens_high(i + 1)
                    if second:
                        x_magnitudes(i + 2)
                    if nxt:
                        silu_of(i + 1, 0)
                    if prev:
                        hidden_high(i - 1)
                    if cur:
                        hidden_begun(i)
                    if nxt:
                        silu_of(i + 1, 1)
                        silu_of(i + 1, 2)
                        silu_of(i + 1, 3)

                step.restart()
                act.wait_ge(init, 3)
                x_magnitudes(0)
                act.sem_inc(ht_hi, 1)
                all_chunks(act, chunk, after_first=lambda: tokens_high(0))
                silu_of(0, 0)
                silu_of(0, 1)
                x_magnitudes(1)
                silu_of(0, 2)
                silu_of(0, 3)
                all_steps(act, step_of)

            @block.gpsimd
            def _(pool):
                step = Steps(pool, p_steps)

                def inverse_deviation(i):
                    pool.wait_ge(mv_ready, i + 1)
                    step(pool.tensor_tensor(veps[:], mv[:, 1:2], eps[:], ALU.add))
                    pool.tensor_tensor(rstd[:], veps[:], mhalf[:], ALU.pow).then_inc(rstd_ready, 1)

                def hidden_value(i):
                    pool.wait_ge(hlow_ready, i + 1)
                    pool.wait_ge(ht_full, NF * i + 1)
                    quant_value(pool, step, low[:], hsign[:], hhalf[:], FF, hval[:]).then_inc(hval_ready, 1)

                def hidden_low(i):
                    pool.wait_ge(d_full, i + 1)
                    for f, chunks in enumerate(FILLS_T):
                        ks = slice(chunks[0], chunks[-1] + 1)
                        pool.wait_ge(ht_hi, NF * i + f + 2)
                        pool.tensor_tensor(hT[1][:, ks, :], hT_raw[:, ks, :], cast(hT[0][:, ks, :]), ALU.subtract)\
                            .then_inc(ht_lo, 1)

                def tokens_value(i):
                    pool.wait_ge(xlow_ready, i + 1)
                    quant_value(pool, step, xlow[:], xsign[:], xscale[:], D, xy).then_inc(xval_ready, 1)

                def split_low(a, r, b):
                    gate_up, down = raw[r]
                    pool.wait_ge(w_hi, a + 1)
                    pool.tensor_tensor(wgu[1][:, 1, :, bass.ds(P * a, P)], gate_up[:, 1, :].rearrange("p (c o) -> p c o", c=C),
                                       cast(wgu[0][:, 1, :, bass.ds(P * a, P)]), ALU.subtract)
                    pool.tensor_tensor(wd[1][:, bass.ds(a, 1), :].rearrange("p o d -> p (o d)"), down,
                                       cast(wd[0][:, bass.ds(a, 1), :].rearrange("p o d -> p (o d)")), ALU.subtract)\
                        .then_inc(w_lo, 1)

                pool.wait_ge(init, 3)
                def step_of(i, second, nxt, cur, prev):
                    step.restart()
                    if second:
                        inverse_deviation(i + 2)
                    if prev:
                        hidden_value(i - 1)
                        hidden_low(i - 1)
                    if second:
                        tokens_value(i + 2)

                inverse_deviation(0)
                tokens_value(0)
                inverse_deviation(1)
                all_chunks(pool, split_low)
                tokens_value(1)
                all_steps(pool, step_of)

            @block.vector
            def _(dve):
                step = Steps(dve, v_steps)

                def tile_of_x(i):
                    return X[:, bass.ds(i, 1), :].rearrange("p o d -> p (o d)")

                def statistics(i):
                    step(dve.memset(fence[:], 0.0))
                    step(dve.bn_stats(stats[:], tile_of_x(i)))
                    dve.bn_aggr(mv[:], stats[:]).then_inc(mv_ready, 1)

                def tokens_scaled(i):
                    dve.wait_ge(rstd_ready, i + 1)
                    step(dve.tensor_scalar(xn, tile_of_x(i), mv[:, 0:1], rstd[:], ALU.subtract, ALU.mult))
                    quant_scaled(dve, step, xn, D, xscale[:], xinv[:], xy).then_inc(xy_ready, 1)
                    step(halved(dve, xscale[:], xscale[:]))

                def tokens_rounded(i):
                    dve.wait_ge(xmag_ready, i + 1)
                    quant_rounded(dve, step, xy, xlow[:], xhigh[:]).then_inc(xlow_ready, 1)

                def tokens_low(i):
                    dve.wait_ge(xt_hi, i + 1)
                    dve.tensor_tensor(xT[1][:].rearrange("p c t -> p (c t)"), xt_ps[:],
                                      cast(xT[0][:].rearrange("p c t -> p (c t)")), ALU.subtract).then_inc(xt_lo, 1)

                def hidden_piece(i, p):
                    n = PIECES * i + p
                    dve.wait_ge(silu_ready, n + 1)
                    dve.wait_ge(u_full, n + 1)
                    dve.tensor_tensor(h[:, p * PW:(p + 1) * PW], u_ps[p % 2][:, 0:PW], silu[p % 2][:], ALU.mult)\
                       .then_inc(h_piece, 1)

                def hidden_scaled(i):
                    dve.wait_ge(h_piece, PIECES * i + PIECES)
                    quant_scaled(dve, step, h, FF, hscale[:], hinv[:], hy).then_inc(hy_ready, 1)
                    dve.wait_ge(hval_ready, i)
                    step(halved(dve, hscale[:], hhalf[:]))

                def hidden_rounded(i, nxt, prev):
                    def between(n):
                        if n == 1 + len(STEPS_1):
                            dve.wait_ge(hbegun_ready, i + 1)
                        if prev and n == SUM_AFTER:
                            add_product(i - 1)
                        if nxt and n in PIECE_AFTER:
                            hidden_piece(i + 1, PIECE_AFTER.index(n))

                    dve.wait_ge(hmag_ready, i + 1)
                    quant_rounded(dve, step, hy, low[:], high[:], between, begun=True).then_inc(hlow_ready, 1)

                def add_product(i):
                    dve.wait_ge(d_full, i + 2)
                    dve.tensor_tensor(tile_of_x(i), tile_of_x(i), d_ps[:], ALU.add).then_inc(x_done, 1)

                def split_low(a, r, b):
                    gate_up, _ = raw[r]
                    dve.wait_ge(w_hi, a + 1)
                    dve.tensor_tensor(wgu[1][:, 0, :, bass.ds(P * a, P)], gate_up[:, 0, :].rearrange("p (c o) -> p c o", c=C),
                                      cast(wgu[0][:, 0, :, bass.ds(P * a, P)]), ALU.subtract).then_inc(g_lo, 1)

                def step_of(i, second, nxt, cur, prev):
                    step.restart()
                    if second:
                        statistics(i + 2)
                    if nxt:
                        tokens_low(i + 1)
                    if second:
                        tokens_scaled(i + 2)
                    if cur:
                        hidden_scaled(i)
                    if second:
                        tokens_rounded(i + 2)
                    if cur:
                        hidden_rounded(i, nxt, prev)
                    elif prev:
                        add_product(i - 1)
                    if nxt:
                        hidden_piece(i + 1, PIECES - 1)

                dve.sem_inc(x_done, 1)
                dve.memset(minus_last[:], -STEP_4).then_inc(init, 1)
                dve.memset(eps[:], 1e-5).then_inc(init, 1)
                dve.memset(mhalf[:], -0.5).then_inc(init, 1)
                statistics(0)
                tokens_scaled(0)
                statistics(1)
                tokens_rounded(0)
                all_chunks(dve, split_low, after_first=lambda: tokens_low(0))
                dve.wait_ge(g_lo, FC)
                dve.wait_ge(w_lo, FC)
                hidden_piece(0, 0)
                hidden_piece(0, 1)
                tokens_scaled(1)
                tokens_rounded(1)
                hidden_piece(0, 2)
                hidden_piece(0, 3)
                all_steps(dve, step_of)


def laid_out(np_, x):
    c_ = np_.ascontiguousarray
    rows = lambda w: c_(w.reshape(-1, P, w.shape[1]).transpose(1, 0, 2))
    cols = lambda w: rows(w.T)
    wide = lambda v: c_(np_.broadcast_to(v.reshape(1, -1), (P, v.size)))
    tall = lambda v: c_(v.reshape(-1, P).T)
    per = lambda v: c_(v.reshape(E, C, P).transpose(2, 0, 1))
    ctx = x["ctx_1024"]
    eye = np_.eye(P, dtype=np_.float32)
    batch = np_.arange(P) // LQ
    same = batch[:, None] == batch[None, :]
    order = np_.arange(P)[:, None] <= np_.arange(P)[None, :]
    e32 = np_.eye(B, dtype=np_.float32)
    out = {
        "x": c_(x["x"].reshape(TILES, P, D).transpose(1, 0, 2)),
        "ctxT": c_(ctx.reshape(B, LK, C, P).transpose(0, 3, 2, 1)),
        "ctx_tail": c_(ctx[:, LK - 1].reshape(B, C, P).transpose(2, 1, 0)),
        "attn_bias": c_(np_.tile(x["fside_SxS2_0"], (BT, 1))),
        "l0_wq": rows(x["L0_xattn_Wq"]), "l0_wk": rows(x["L0_xattn_Wk"]), "l0_wv": rows(x["L0_xattn_Wv"]),
        "l0_wo": rows(x["L0_xattn_Wo"]), "l0_bq": wide(x["L0_xattn_bq"]), "l0_bo": wide(x["L0_xattn_bo"]),
        "scale_log": wide(x["L0_xattn_scale_mul_log"]),
        "a_wq": cols(x["L0_attn_Wq"]), "a_wk": cols(x["L0_attn_Wk"]), "a_wv": cols(x["L0_attn_Wv"]),
        "a_wo": c_(x["L0_attn_Wo"].T), "gate": cols(x["L0_ffn_gate_w"]),
        "experts": c_(np_.stack([m for n in range(SHARED) for m in (
                        cols(x["L0_ffn_sw1"][n * D:(n + 1) * D]), cols(x["L0_ffn_sw2"][n * D:(n + 1) * D]),
                        cols(x["L0_ffn_sw3"][:, n * D:(n + 1) * D]))]
                        + [cols(x["L0_ffn_" + k][e]) for e in range(E) for k in ("w1", "w3", "w2")])),
        "b1": per(x["L0_ffn_b1"]), "b2": per(x["L0_ffn_b2"]), "b3": per(x["L0_ffn_b3"]),
        "ffn_w": c_(np_.stack([x["L1_ffn_w_gate"].reshape(FC, P, D), x["L1_ffn_w_up"].reshape(FC, P, D),
                               x["L1_ffn_w_down"].reshape(C, P, FC, P).transpose(2, 1, 0, 3).reshape(FC, P, D)], 1)
                     .reshape(FFN_TILES, P, D)),
        "ctx": ctx, "ctx_tail_rows": c_(ctx[:, LK - 1]), "mask": x["mask_BxSxS2_ik0"].reshape(TILES, P, LK),
        "l1_wq": rows(x["L1_xattn_Wq"]), "l1_wk": rows(x["L1_xattn_Wk"]), "l1_wv": rows(x["L1_xattn_Wv"]),
        "l1_wo": cols(x["L1_xattn_Wo"]), "l1_bq": tall(x["L1_xattn_bq"]), "l1_bk": tall(x["L1_xattn_bk"]),
        "l1_bv": tall(x["L1_xattn_bv"]), "l1_bo": wide(x["L1_xattn_bo"]),
        "s_wq": rows(x["L1_attn_wq"]), "s_wk": rows(x["L1_attn_wk"]), "s_wv": rows(x["L1_attn_wv"]),
        "s_wo": x["L1_attn_wo"], "s_bqk": c_(np_.stack([x["L1_attn_bq"], x["L1_attn_bk"]], 1)),
        "s_bv": x["L1_attn_bv"].reshape(HK, 1), "s_bo": wide(x["L1_attn_bo"]),
        "ident": eye,
        "onehot": c_(np_.broadcast_to(e32, (P, B, B))),
        "causal": np_.where(same, np_.where(order.T, 0.0, -1e11), -1e30).astype(np_.float32),
        "own_batch": c_((np_.arange(B)[None, None, :] == (BT * np_.arange(TILES)[None, :, None] + batch[:, None, None]))
                        .astype(np_.float32)),
        "cmaskT": (same & order).astype(np_.float32),
        "lower": c_(np_.broadcast_to(np_.tril(np_.ones((E, E), np_.float32), -1), (P, E, E))),
    }
    return out


def program(nc, A, out):
    w_dram = nc.dram_tensor("router_weights", [E, T], F32, kind="Internal").ap()
    q_dram = nc.dram_tensor("quantised", [FFN_TILES, P, D], F32, kind="Internal").ap()
    with ExitStack() as ctx:
        X = ctx.enter_context(nc.sbuf_tensor("X", [P, TILES, D], F32))
        XN3T = ctx.enter_context(nc.sbuf_tensor("XN3T", [P, C, T], F32))
        raw_in = [ctx.enter_context(nc.semaphore(f"raw_in{r}")) for r in range(2)]

        def prefetch(sp):
            for r, raw in enumerate(raw_chunks(XN3T)):
                load_chunk(sp, q_dram, raw, r, raw_in[r])

        phase_a(nc, A, X, XN3T, w_dram)
        phase_b(nc, A, X, XN3T, w_dram, q_dram)
        phase_c(nc, A, X, XN3T, prefetch)
        phase_d(nc, A, X, XN3T, q_dram, out, raw_in)


def kernel(**inputs):
    import concourse.bacc as bacc
    from concourse.bass_utils import run_bass_kernel_spmd

    nc = bacc.Bacc("TRN2", target_bir_lowering=False, num_devices=1)
    arrays = laid_out(np, {name: np.ascontiguousarray(a) for name, a in inputs.items()})
    A = {name: nc.dram_tensor(name, a.shape, mybir.dt.from_np(a.dtype), kind="ExternalInput").ap()
         for name, a in arrays.items()}
    out = nc.dram_tensor("out", [TILES, P, D], F32, kind="ExternalOutput").ap()
    program(nc, A, out)
    result = run_bass_kernel_spmd(nc, [arrays], core_ids=[0])
    return result.results[0]["out"].reshape(B, LQ, D)
```
